# Optimizing a Trainium2 kernel written in Bass

```python
import numpy as np
import jax
import jax.numpy as jnp

def _softmax(x, axis=-1):
    return jax.nn.softmax(x, axis=axis)

def _gelu(x):
    return jax.nn.gelu(x, approximate=True)

def _silu(x):
    return jax.nn.silu(x)

def _sigmoid(x):
    return jax.nn.sigmoid(x)

def _layernorm(x, axis=-1, eps=1e-05):
    m = jnp.mean(x, axis=axis, keepdims=True)
    v = jnp.var(x, axis=axis, keepdims=True)
    return (x - m) / jnp.sqrt(v + eps)

def _scatter_add(tgt, idx, src, axis=0):
    return tgt.at[idx].add(src)

def _segment_sum(src, seg, n):
    return jax.ops.segment_sum(src, seg, n)
kernel_name = 'mk_gnn_preln_d4_gnn_r64_f6839b'

def setup_inputs(seed: int=0):
    np.random.seed(seed)
    _w = jnp.asarray

    def _rec_inputs():
        import jax
        import jax.numpy as jnp
        _gk = jax.random.key(seed)
        x = -0.0005121 + 1.001 * jax.random.normal(jax.random.fold_in(_gk, 1), (100000, 32), jnp.float32)
        src = jax.random.randint(jax.random.fold_in(_gk, 2), (50000,), 0, 100000, jnp.int32)
        dst = jnp.minimum((100000 * jax.random.uniform(jax.random.fold_in(_gk, 3), (50000,)) ** 2.0).astype(jnp.int32), 99999)
        _o = jnp.argsort(dst, stable=True)
        src = src[_o]
        dst = dst[_o]
        edge_attr_16 = 0.000312547 + 1.00004 * jax.random.normal(jax.random.fold_in(_gk, 12), (50000, 16), jnp.float32)
        edge_weight = jax.random.uniform(jax.random.fold_in(_gk, 14), (50000,), jnp.float32, 0.0, 1)
        return (x, src, dst, edge_attr_16, edge_weight)
    x, src, dst, edge_attr_16, edge_weight = _rec_inputs()

    def _L0_gnn_setup():
        import jax, jax.numpy as jnp
        import numpy as np
        N_NODES = 100000
        N_EDGES = 25000
        N_FEAT = 32
        key = jax.random.key(seed)
        k1, k2, k3, k4 = jax.random.split(key, 4)
        u = jax.random.normal(k1, (N_NODES, N_FEAT), dtype=jnp.float32)
        weights = jax.random.uniform(k2, (N_EDGES,), dtype=jnp.float32)
        row = jax.random.randint(k3, (N_EDGES,), 0, N_NODES)
        col = jax.random.randint(k4, (N_EDGES,), 0, N_NODES)
        edge_index = jnp.stack([row, col]).astype(jnp.int64)
        return {'u': u, 'weights': weights, 'edge_index': edge_index}
    _L0_gnn_all = _L0_gnn_setup()
    _L0_gnn_in = {k: v for k, v in _L0_gnn_all.items() if k in ()}
    del _L0_gnn_all

    def _L1_gnn_setup():
        import jax, jax.numpy as jnp
        import numpy as np
        N_NODES = 50000
        DEG = 16
        N_HEAD = 4
        F_IN = 32
        F_OUT = 32
        key = jax.random.key(seed)
        k_h, k_w, k_fw, k_fb = jax.random.split(key, 4)
        h = jax.random.normal(k_h, (N_NODES, F_IN), dtype=jnp.float32)
        src = jnp.repeat(jnp.arange(N_NODES, dtype=jnp.int64), DEG)
        offs = (jnp.arange(DEG, dtype=jnp.int64) + 1) * 97
        dst = (src.reshape(N_NODES, DEG) + offs[None, :]).reshape(-1) % N_NODES
        edge_index = jnp.stack([src, dst], axis=0)
        gain = 1.414
        bound_w = gain * np.sqrt(6.0 / (F_IN + F_OUT))
        w = jax.random.uniform(k_w, (N_HEAD, F_IN, F_OUT), jnp.float32, -bound_w, bound_w)
        bound_fc = np.sqrt(1.0 / (2 * F_OUT))
        fc_w = jax.random.uniform(k_fw, (1, 2 * F_OUT), jnp.float32, -bound_fc, bound_fc)
        fc_b = jax.random.uniform(k_fb, (1,), jnp.float32, -bound_fc, bound_fc)
        bias = jnp.zeros((F_OUT,), jnp.float32)
        return {'h': h, 'edge_index': edge_index, 'w': w, 'fc_w': fc_w, 'fc_b': fc_b, 'bias': bias}
    _L1_gnn_all = _L1_gnn_setup()
    _L1_gnn_in = {k: v for k, v in _L1_gnn_all.items() if k in ('w', 'fc_w', 'fc_b', 'bias')}
    del _L1_gnn_all

    def _L2_gnn_setup():
        import jax, jax.numpy as jnp
        import numpy as np
        N_NODES = 100000
        N_EDGES = 15625
        IN_CH = 32
        EDGE_CH = 16
        OUT_CH = 32
        D_CAT = 2 * IN_CH + EDGE_CH
        D_MID = 56
        key = jax.random.key(seed)
        ks = jax.random.split(key, 8)
        x = jax.random.normal(ks[0], (N_NODES, IN_CH), dtype=jnp.float32)
        edge_index = jax.random.randint(ks[1], (2, N_EDGES), 0, N_NODES, dtype=jnp.int64)
        edge_attr = jax.random.normal(ks[2], (N_EDGES, EDGE_CH), dtype=jnp.float32)
        W1 = jax.random.normal(ks[3], (D_CAT, D_MID), dtype=jnp.float32) / np.sqrt(D_CAT).astype(np.float32)
        b1 = jnp.zeros((D_MID,), dtype=jnp.float32)
        W2 = jax.random.normal(ks[4], (D_MID, OUT_CH), dtype=jnp.float32) / np.sqrt(D_MID).astype(np.float32)
        b2 = jnp.zeros((OUT_CH,), dtype=jnp.float32)
        return {'x': x, 'edge_index': edge_index, 'edge_attr': edge_attr, 'W1': W1, 'b1': b1, 'W2': W2, 'b2': b2}
    _L2_gnn_all = _L2_gnn_setup()
    _L2_gnn_in = {k: v for k, v in _L2_gnn_all.items() if k in ('W1', 'b1', 'W2', 'b2')}
    del _L2_gnn_all

    def _L3_gnn_setup():
        import jax, jax.numpy as jnp
        import numpy as np
        N_NODES = 100000
        key = jax.random.key(seed)
        k1, k2, k3 = jax.random.split(key, 3)
        node_f = jax.random.normal(k1, (N_NODES, 32), dtype=jnp.float32)
        src = jax.random.randint(k2, (25000,), 0, N_NODES, dtype=jnp.int64)
        dst = jax.random.randint(k3, (25000,), 0, N_NODES, dtype=jnp.int64)
        return {'node_f': node_f, 'src': src, 'dst': dst}
    _L3_gnn_all = _L3_gnn_setup()
    _L3_gnn_in = {k: v for k, v in _L3_gnn_all.items() if k in ()}
    del _L3_gnn_all
    return {'x': x, 'src': src, 'dst': dst, 'edge_attr_16': edge_attr_16, 'edge_weight': edge_weight, 'L1_gnn_w': _L1_gnn_in['w'], 'L1_gnn_fc_w': _L1_gnn_in['fc_w'], 'L1_gnn_fc_b': _L1_gnn_in['fc_b'], 'L1_gnn_bias': _L1_gnn_in['bias'], 'L2_gnn_W1': _L2_gnn_in['W1'], 'L2_gnn_b1': _L2_gnn_in['b1'], 'L2_gnn_W2': _L2_gnn_in['W2'], 'L2_gnn_b2': _L2_gnn_in['b2']}

def reference(x, src, dst, edge_attr_16, edge_weight, L1_gnn_w, L1_gnn_fc_w, L1_gnn_fc_b, L1_gnn_bias, L2_gnn_W1, L2_gnn_b1, L2_gnn_W2, L2_gnn_b2):
    import jax
    import jax.numpy as jnp

    def _L0_gnn_ref(u, weights, edge_index):
        import jax, jax.numpy as jnp
        import numpy as np
        N_NODES = 100000
        N_EDGES = 25000
        N_FEAT = 32
        row, col = (edge_index[0], edge_index[1])
        diff = u[col] - u[row]
        weighted_diff = weights[:, None] * diff
        laplacian = jax.ops.segment_sum(weighted_diff, row, num_segments=u.shape[0])
        return laplacian

    def _L1_gnn_ref(h, edge_index, w, fc_w, fc_b, bias):
        import jax, jax.numpy as jnp
        import numpy as np
        N_NODES = 50000
        DEG = 16
        N_HEAD = 4
        F_IN = 32
        F_OUT = 32
        n_head, f_in, f_out = w.shape
        n = h.shape[0]
        src, dst = (edge_index[0], edge_index[1])
        hp = jnp.einsum('nf,hfo->hno', h, w)
        w_src = fc_w[0, :f_out]
        w_dst = fc_w[0, f_out:]
        a_src = jnp.einsum('hnf,f->hn', hp, w_src)
        a_dst = jnp.einsum('hnf,f->hn', hp, w_dst)
        e = a_src[:, src] + a_dst[:, dst] + fc_b[0]
        e = jax.nn.leaky_relu(e, negative_slope=0.2)
        seg_max = jax.ops.segment_max(e.T, src, num_segments=n)
        e = jnp.exp(e - seg_max.T[:, src])
        seg_sum = jax.ops.segment_sum(e.T, src, num_segments=n)
        att = e / seg_sum.T[:, src]
        msg = att[:, :, None] * hp[:, dst, :]
        agg = jax.vmap(lambda m: jax.ops.segment_sum(m, src, num_segments=n))(msg)
        out = agg.mean(axis=0) + bias
        return out

    def _L2_gnn_ref(x, edge_index, edge_attr, W1, b1, W2, b2):
        import jax, jax.numpy as jnp
        import numpy as np
        N_NODES = 100000
        N_EDGES = 15625
        IN_CH = 32
        EDGE_CH = 16
        OUT_CH = 32
        D_CAT = 2 * IN_CH + EDGE_CH
        D_MID = 56
        num_nodes = x.shape[0]
        rol, col = (edge_index[0], edge_index[1])
        e = jnp.concatenate([x[rol], x[col], edge_attr], axis=-1)
        h = jax.nn.leaky_relu(e @ W1 + b1)
        v = jax.nn.leaky_relu(h @ W2 + b2)
        agg = jax.ops.segment_max(v, col, num_segments=num_nodes)
        agg = jnp.where(jnp.isneginf(agg), jnp.zeros((), dtype=agg.dtype), agg)
        out = jnp.maximum(agg, x[:, -v.shape[-1]:])
        return out

    def _L3_gnn_ref(node_f, src, dst):
        import jax, jax.numpy as jnp
        import numpy as np
        N_NODES = 100000
        n = node_f.shape[0]
        ones = jnp.ones(src.shape[0], dtype=node_f.dtype)
        out_deg = jnp.clip(jax.ops.segment_sum(ones, src, num_segments=n), 1.0)
        in_deg = jnp.clip(jax.ops.segment_sum(ones, dst, num_segments=n), 1.0)
        x = node_f * jax.lax.rsqrt(out_deg)[:, None]
        agg = jax.ops.segment_sum(x[src], dst, num_segments=n)
        return agg * jax.lax.rsqrt(in_deg)[:, None]
    edge_index = jnp.stack([src, dst])
    h = jnp.maximum(_layernorm(x, axis=-1), 0.0)
    x = x + _L0_gnn_ref(h, edge_weight, edge_index)
    h = jnp.maximum(_layernorm(x, axis=-1), 0.0)
    x = x + _L1_gnn_ref(h, edge_index, L1_gnn_w, L1_gnn_fc_w, L1_gnn_fc_b, L1_gnn_bias)
    h = jnp.maximum(_layernorm(x, axis=-1), 0.0)
    x = x + _L2_gnn_ref(h, edge_index, edge_attr_16, L2_gnn_W1, L2_gnn_b1, L2_gnn_W2, L2_gnn_b2)
    h = jnp.maximum(_layernorm(x, axis=-1), 0.0)
    x = x + _L3_gnn_ref(h, src, dst)
    return x

_drawn_inputs = setup_inputs


def setup_inputs(seed=0):
    import zlib

    import numpy as np

    out = dict(_drawn_inputs(seed))
    spreads = {'L1_gnn_bias': (0.0, 0.1), 'L2_gnn_b1': (0.0, 0.518), 'L2_gnn_b2': (0.0, 0.392)}
    factors = {'L1_gnn_fc_w': 3.155}
    for name, (base, spread) in spreads.items():
        noise = np.random.default_rng([zlib.crc32(name.encode()), seed]).standard_normal(out[name].shape)
        drawn = base * np.exp(spread * noise) if base else spread * noise
        out[name] = jnp.asarray(drawn.astype(out[name].dtype))
    for name, factor in factors.items():
        out[name] = (out[name] * factor).astype(out[name].dtype)
    return out
```

```python
from contextlib import ExitStack

import numpy as np
import concourse.bass as bass
from concourse import mybir

ALU = mybir.AluOpType
ACT = mybir.ActivationFunctionType
AX = mybir.AxisListType
F32 = mybir.dt.float32
F16 = mybir.dt.float16
I32 = mybir.dt.int32

P = 128
N = 100000
E = 50000
F = 32
H = 4
A = 16
MID = 56
C = 14
T = 392
CHUNKS = T // C
TURNS = CHUNKS // 2
EP = P * T
ROWS = 784
NP = P * ROWS
NC = ROWS // CHUNKS
LOW = 256
HIGH = 391
PADKEY = (HIGH - 1) * LOW + LOW - 1
RW = 36
WS, WD = 3, 2 + A
CAT = 2 * F + A + 1
BIG = 1.5e38
SKIP = 200000.0
assert T % (2 * C) == 0 and EP >= E and NP >= N and PADKEY >= N and (2 * C) % 4 == 0


def build_gnn(nc, x, src, dst, attr, ew, w, fc_w, fc_b, bias, W1, b1, W2, b2, out):
    mid_table = [nc.dram_tensor(f"mid_table{k}", (EP, W), F32).ap() for k, W in enumerate((WS, WD))]
    edge_table = [nc.dram_tensor(f"edge_table{k}", (EP, W), F32).ap() for k, W in enumerate((WS, WD))]
    x1_table = nc.dram_tensor("x1_table", (NP, F), F32).ap()
    x2_table = nc.dram_tensor("x2_table", (NP, RW), F32).ap()
    x3_table = nc.dram_tensor("x3_table", (NP, F), F32).ap()
    h1_table = nc.dram_tensor("h1_table", (P, T * F), F32).ap()

    with ExitStack() as ctx:
        def sb(name, shape, dt=F32):
            return ctx.enter_context(nc.sbuf_tensor(name, shape, dt))

        def sem(name):
            return ctx.enter_context(nc.semaphore(name))

        def sems(name, n=2):
            return [sem(f"{name}{i}") for i in range(n)]

        digits_row = sb("digits_row", [P, T], F16)
        before = sb("before", [P, P], F16)
        rest = sb("rest", [P, P], F16)
        ones16 = sb("ones16", [P, P], F16)
        first_row = sb("first_row", [P, P])
        ident = sb("ident", [P, P])
        onesT = sb("onesT", [P, T])
        u_heads = sb("u_heads", [P, 2, H, F])
        fcb_sb = sb("fcb_sb", [P, 1])
        bias_sb = sb("bias_sb", [P, F])
        w_stack = sb("w_stack", [P, F])
        W1_sb = sb("W1_sb", [CAT, MID])
        W2_sb = sb("W2_sb", [MID + 1, F])

        X = sb("X", [P, T, F])
        SEG = sb("SEG", [P, T + 1, F])
        PAY = [SEG[:, :, :].rearrange("p t f -> p (t f)")[:, 0:T * W].rearrange("p (t w) -> p t w", w=W)
               for W in (WS, WD)]
        scan_in = X[:, :, :].rearrange("p t f -> p (t f)")[:, 0:T * A]
        key_i = sb("key_i", [P, T], I32)
        digit = sb("digit", [P, T])
        ew_sb = sb("ew_sb", [P, T])
        keyf = sb("keyf", [P, T])
        same = [sb(f"same{k}", [P, T]) for k in range(2)]
        whole = [sb(f"whole{k}", [P, T]) for k in range(2)]
        last = [sb(f"last{k}", [P, T]) for k in range(2)]
        deg = [sb(f"deg{k}", [P, T]) for k in range(2)]
        more = sb("more", [P, T])
        tail = sb("tail", [P, T])
        src_row = [sb(f"src_row{k}", [P, T], I32) for k in range(2)]
        dst_row = [sb(f"dst_row{k}", [P, T], I32) for k in range(2)]
        out_row = [sb(f"out_row{k}", [P, T], I32) for k in range(2)]
        a_src = sb("a_src", [P, H, T])
        a_dst = sb("a_dst", [P, H, T])
        seg_flat = SEG[:, :, :].rearrange("p t f -> p (t f)")
        scan_a, scan_b = (seg_flat[:, q * H * T:(q + 1) * H * T].rearrange("p (h t) -> p h t", h=H)
                          for q in range(2))

        onehot = [sb(f"onehot{i}", [P, T], F16) for i in range(4)]
        digit_c = sb("digit_c", [P, C])
        base = sb("base", [P, T])
        hist_sb = sb("hist_sb", [P, T])
        junk = sb("junk", [P, T])
        rank_c = sb("rank_c", [P, C])
        int_c = sb("int_c", [P, 2, C], I32)
        flt_c = sb("flt_c", [P, 2, C])
        row_c = [sb(f"row_c{b}", [P, 2, C], I32) for b in range(2)]
        got = [sb(f"got{b}", [P, 2, C * RW]) for b in range(2)]
        put = [sb(f"put{b}", [P, C * RW]) for b in range(2)]
        attr_c = [sb(f"attr_c{b}", [P, C, WD]) for b in range(2)]
        sums = sb("sums", [P, NC])
        var = sb("var", [P, NC])
        std = sb("std", [P, NC])
        cen = sb("cen", [P, NC, F])
        sqr = sb("sqr", [P, NC, F])
        ha = sb("ha", [P, C, F])
        hb = sb("hb", [P, C, F])
        a_dst_flat = a_dst[:, :, :].rearrange("p h t -> p (h t)")
        a_src_flat = a_src[:, :, :].rearrange("p h t -> p (h t)")
        cat = a_dst_flat[:, 0:C * CAT].rearrange("p (c k) -> p c k", k=CAT)
        catT = a_src_flat[:, 0:4 * P]
        hid = a_src_flat[0:MID, 4 * P:8 * P]
        hidT = a_src_flat[0:MID + 1, 8 * P:12 * P]
        node_in_all = sb("node_in", [P, 2, NC * RW])
        node_in = [node_in_all[:, b, :].rearrange("p (r w) -> p r w", w=RW) for b in range(2)]
        prod = node_in_all[:, :, :].rearrange("p b n -> p (b n)")[:, 0:C * H * F]\
            .rearrange("p (c h f) -> p c h f", h=H, f=F)
        node_out = [sb(f"node_out{b}", [P, NC, F]) for b in range(2)]
        w_all = X[:, 0:P, :]
        w_prod = X[:, P:2 * P, :]
        fcw_sb = sb("fcw_sb", [P, 2 * F])
        primer = sb("primer", [16, F])
        edge_prev = sb("edge_prev", [P, 1])
        edge_next = sb("edge_next", [P, 1])
        ends = sb("ends", [P, 2, F])
        endsT = sb("endsT", [F, 2, P])
        carryT = sb("carryT", [F, P + 1])
        carry = sb("carry", [P, F])

        hist_ps = ctx.enter_context(nc.psum_tensor("hist_ps", [P, 512], F32))
        count_ps = [ctx.enter_context(nc.psum_tensor(f"count_ps{b}", [P, 512], F32)) for b in range(2)]
        turn_ps = [ctx.enter_context(nc.psum_tensor(f"turn_ps{b}", [P, 512], F32)) for b in range(2)]
        y_ps = ctx.enter_context(nc.psum_tensor("y_ps", [P, 512], F32))
        hid_ps = ctx.enter_context(nc.psum_tensor("hid_ps", [P, 512], F32))
        carry_ps = ctx.enter_context(nc.psum_tensor("carry_ps", [P, 512], F32))

        turns = {e: sem(f"turns_{e}") for e in ("dve", "act", "pool", "sp", "pe")}
        dve_chain = sem("dve_chain")
        consts_iota, consts_load, consts_dve = sem("consts_iota"), sem("consts_load"), sem("consts_dve")
        edges_in = sem("edges_in")
        attr_copied = sem("attr_copied")
        hist_hot, hist_free, hist_done, base_ready = sem("hist_hot"), sem("hist_free"), sem("hist_done"), sem("base_ready")
        rank_hot, rank_free, rank_ready, rank_read, rank_done = (
            sem("rank_hot"), sem("rank_free"), sem("rank_ready"), sem("rank_read"), sem("rank_done"))
        rows_ready, pay_ready = sems("rows_ready"), sems("pay_ready")
        sort_scatter = [sems(f"sort_scatter{n}_") for n in range(4)]
        pass_written, pass_loaded, pay_free, pay_made = sem("pass_written"), sem("pass_loaded"), sem("pay_free"), sem("pay_made")
        ends_ready, ends_turned, carry_ready, carry_turned = (
            sem("ends_ready"), sem("ends_turned"), sem("carry_ready"), sem("carry_turned"))
        var_ready, std_ready = sem("var_ready"), sem("std_ready")
        got_free = sems("got_free")
        gathers = {n: sems(f"gather_{n}_") for n in ("l0", "l1", "l2", "l3")}
        scatters = {n: sems(f"scatter_{n}_") for n in ("l0", "l1", "l2", "l3")}
        put_ready = sems("put_ready")
        layer_done = sem("layer_done")
        layer_start = sem("layer_start")
        init_in, init_out, init_padded = sems("init_in"), sems("init_out"), sems("init_padded")
        tables_ready = sem("tables_ready")
        h1_ready, h1_stored, h1_loaded, h1_used = sems("h1_ready"), sems("h1_stored"), sems("h1_loaded"), sems("h1_used")
        h1_all = sem("h1_all")
        e_ready, p_ready = sem("e_ready"), sem("p_ready")
        q_ready, q_free, y_ready, y_used = sem("q_ready"), sem("q_free"), sem("y_ready"), sem("y_used")
        turned, copied = sem("turned"), sem("copied")
        attr_loaded, attr_used = sems("attr_loaded"), sems("attr_used")
        cat_ready, cat_used, hid_ready, hid_copied, hid_act, v_ready = (
            sem("cat_ready"), sem("cat_used"), sem("hid_ready"), sem("hid_copied"), sem("hid_act"), sem("v_ready"))
        node_loaded, node_used, node_ready, node_stored = (
            sems("node_loaded"), sems("node_used"), sems("node_ready"), sems("node_stored"))
        nodes_done = sem("nodes_done")
        staging_set = sem("staging_set")

        PRIMED = [s for pair in (*sort_scatter, *scatters.values()) for s in pair]
        PRIME = 16
        primer_row = bias.rearrange("(a n) -> a n", a=1)

        def take(eng, s, n=1):
            eng.wait_ge(s, n)
            eng.sem_inc(s, -n)

        def landed(eng, name, s, value):
            eng.wait_ge(s, value)
            eng.sem_inc(turns[name], 1)

        block = ctx.enter_context(nc.Block())
        GROUPS = [(0, 4), (4, 8), (8, 12), (12, 14)]

        @block.gpsimd
        def _(pool):
            nc.gpsimd.iota(digits_row[:, :], [[1, T]], base=0, channel_multiplier=0,
                           allow_small_or_imprecise_dtypes=True)
            nc.gpsimd.memset(ident[:, :], 0.0)
            nc.gpsimd.memset(before[:, :], 1.0)
            nc.gpsimd.memset(rest[:, :], 1.0)
            nc.gpsimd.memset(ones16[:, :], 1.0)
            nc.gpsimd.memset(first_row[:, :], 1.0)
            pool.drain().then_inc(consts_iota, 1)
            pool.wait_ge(consts_iota, 1)
            nc.gpsimd.affine_select(out=ident[:, :], in_=ident[:, :], compare_op=ALU.not_equal, fill=1.0,
                                    base=0, pattern=[[-1, P]], channel_multiplier=1).then_inc(consts_iota, 1)
            nc.gpsimd.affine_select(out=before[:, :], in_=before[:, :], compare_op=ALU.is_ge, fill=0.0,
                                    base=-1, pattern=[[1, P]], channel_multiplier=-1).then_inc(consts_iota, 1)
            nc.gpsimd.affine_select(out=rest[:, :], in_=rest[:, :], compare_op=ALU.is_ge, fill=0.0,
                                    base=0, pattern=[[-1, P]], channel_multiplier=1).then_inc(consts_iota, 1)
            nc.gpsimd.affine_select(out=first_row[:, :], in_=first_row[:, :], compare_op=ALU.is_ge, fill=0.0,
                                    base=0, pattern=[[0, P]], channel_multiplier=-1).then_inc(consts_iota, 1)
            pool.wait_ge(staging_set, 1)

            for n, s in enumerate(PRIMED):
                pool.dma_start(primer[n:n + 1, :], primer_row).then_inc(s, 16)

            def gather(b, way, table, width, s):
                for j in range(C):
                    pool.indirect_dma_start(
                        got[b][:, way, j * width:(j + 1) * width], None, table,
                        bass.IndirectOffsetOnAxis(ap=row_c[b][:, way, j:j + 1], axis=0),
                        bounds_check=N - 1, oob_is_err=False).then_inc(s, 16)

            def scatter(b, table, data, width, s, bound):
                for j in range(C):
                    pool.indirect_dma_start(
                        table, bass.IndirectOffsetOnAxis(ap=row_c[b][:, 1, j:j + 1], axis=0),
                        data[:, j * width:(j + 1) * width], None,
                        bounds_check=bound, oob_is_err=False).then_inc(s, 16)

            for k, W in enumerate((WS, WD)):
                for n in range(2):
                    with pool.Fori(0, TURNS) as i:
                        for b in range(2):
                            take(pool, rows_ready[b])
                            take(pool, pay_ready[b])
                            scatter(b, (mid_table, edge_table)[n][k],
                                    put[b][:, :], W,
                                    sort_scatter[2 * k + n][b], EP - 1)
                    for b in range(2):
                        pool.wait_ge(sort_scatter[2 * k + n][b], PRIME + 16 * C * TURNS)
                    pool.sem_inc(pass_written, 1)

            for layer, (table, width, ways, target, wide) in enumerate((
                    (x, F, 2, x1_table, F), (x1_table, F, 1, x2_table, RW),
                    (x2_table, RW, 2, x3_table, F), (x3_table, F, 1, out, F))):
                name = f"l{layer}"
                with pool.Fori(0, TURNS) as i:
                    for b in range(2):
                        take(pool, rows_ready[b])
                        for way in range(ways):
                            gather(b, way, table, width, gathers[name][b])
                if layer == 0:
                    pool.wait_ge(tables_ready, 1)
                if layer == 2:
                    pool.wait_ge(nodes_done, 1)
                with pool.Fori(0, TURNS) as i:
                    for b in range(2):
                        take(pool, put_ready[b])
                        scatter(b, target, put[b][:, :], wide, scatters[name][b], N - 1)
                for b in range(2):
                    pool.wait_ge(scatters[name][b], PRIME + 16 * C * TURNS)
                pool.sem_inc(layer_done, 1)

        @block.sync
        def _(sp):
            sp.dma_start(key_i[:, :], src.rearrange("(p t) -> p t", t=T)).then_inc(edges_in, 16)
            sp.dma_start(ew_sb[:, :], ew.rearrange("(p t) -> p t", t=T)).then_inc(edges_in, 16)
            sp.dma_start(src_row[0][:, :], dst.rearrange("(p t) -> p t", t=T)).then_inc(edges_in, 16)
            sp.dma_start(w_all.rearrange("p t f -> p (t f)"),
                         w.rearrange("h f o -> (h f o)").rearrange("(a n) -> a n", a=1)
                         .to_broadcast([P, H * F * F])).then_inc(consts_load, 16)
            sp.dma_start(fcw_sb[:, :], fc_w.to_broadcast([P, 2 * F])).then_inc(consts_load, 16)
            sp.dma_start(fcb_sb[:, :], fc_b.rearrange("(a n) -> a n", a=1).to_broadcast([P, 1])).then_inc(consts_load, 16)
            sp.dma_start(bias_sb[:, :], bias.rearrange("(a n) -> a n", a=1).to_broadcast([P, F])).then_inc(consts_load, 16)
            sp.dma_start(w_stack[:, :], w.rearrange("h f o -> (h f) o")).then_inc(consts_load, 16)
            sp.dma_start(W1_sb[0:CAT - 1, :], W1).then_inc(consts_load, 16)
            sp.dma_start(W1_sb[CAT - 1:CAT, :], b1.rearrange("(a n) -> a n", a=1)).then_inc(consts_load, 16)
            sp.dma_start(W2_sb[0:MID, :], W2).then_inc(consts_load, 16)
            sp.dma_start(W2_sb[MID:MID + 1, :], b2.rearrange("(a n) -> a n", a=1)).then_inc(consts_load, 16)

            xv = x.rearrange("(p r) f -> p r f", p=P)
            x1v = x1_table.rearrange("(p r) f -> p r f", p=P)
            x2v = x2_table.rearrange("(p r) f -> p r f", p=P)
            sp.wait_ge(staging_set, 1)
            with sp.Fori(0, TURNS) as i:
                for b in range(2):
                    c = i * 2 + b
                    take(sp, node_used[b])
                    sp.dma_start(node_out[b][:, :, :], xv[:, bass.ts(c, NC), :]).then_inc(init_in[b], 16)
                    take(sp, init_padded[b])
                    sp.dma_start(x1v[:, bass.ts(c, NC), :], node_out[b][:, :, :]).then_inc(init_out[b], 16)
                    sp.dma_start(x2v[:, bass.ts(c, NC), :], node_in[b][:, :, :]).then_inc(init_out[b], 16)
            for b in range(2):
                take(sp, node_used[b])
            sp.sem_inc(tables_ready, 1)

            for k, W in enumerate((WS, WD)):
                if k == 1:
                    sp.wait_ge(pay_free, 1)
                    sp.dma_start(key_i[:, :], dst.rearrange("(p t) -> p t", t=T)).then_inc(edges_in, 16)
                    sp.dma_start(src_row[1][:, :], src.rearrange("(p t) -> p t", t=T)).then_inc(edges_in, 16)
                    sp.dma_start(scan_in, attr.rearrange("(p t) a -> p (t a)", t=T)).then_inc(edges_in, 16)
                for n in range(2):
                    sp.wait_ge(pass_written, 2 * k + n + 1)
                    rows = (mid_table, edge_table)[n][k]
                    sp.dma_start(PAY[k].rearrange("p t w -> p (t w)"),
                                 rows.rearrange("(p t) w -> p (t w)", t=T)).then_inc(pass_loaded, 16)
                    if n == 1:
                        tv = rows.rearrange("(p t) w -> p t w", t=T)
                        sp.dma_start(edge_prev[1:P, :], tv[0:P - 1, T - 1, k:k + 1],
                                     allow_slow_non_contiguous=True).then_inc(pass_loaded, 16)
                        sp.dma_start(edge_next[0:P - 1, :], tv[1:P, 0, k:k + 1],
                                     allow_slow_non_contiguous=True).then_inc(pass_loaded, 16)

            h1v = h1_table.rearrange("p (c n) -> p c n", c=CHUNKS)
            with sp.Fori(0, TURNS) as i:
                for b in range(2):
                    take(sp, h1_ready[b])
                    sp.dma_start(h1v[:, i * 2 + b, :], put[b][:, 0:C * F]).then_inc(h1_stored[b], 16)
            for b in range(2):
                take(sp, h1_used[b], 1)
            with sp.Fori(0, TURNS) as i:
                for b in range(2):
                    take(sp, h1_used[b])
                    sp.dma_start(got[b][:, 0, 0:C * F], h1v[:, i * 2 + b, :]).then_inc(h1_loaded[b], 16)

            av = edge_table[1].rearrange("(p t) w -> p t w", t=T)
            sp.wait_ge(layer_done, 2)
            with sp.Fori(0, TURNS) as i:
                for b in range(2):
                    c = i * 2 + b
                    take(sp, attr_used[b])
                    sp.dma_start(attr_c[b][:, :, :], av[:, bass.ts(c, C), :]).then_inc(attr_loaded[b], 16)
                    take(sp, node_used[b])
                    sp.dma_start(node_in[b][:, :, :], x2v[:, bass.ts(c, NC), :]).then_inc(node_loaded[b], 16)
            sp.wait_ge(layer_done, 4)

        @block.scalar
        def _(act):
            act.wait_ge(staging_set, 1)
            for b in range(2):
                act.sem_inc(node_used[b], 1)
            with act.Fori(0, TURNS) as i:
                for b in range(2):
                    take(act, init_in[b], 16)
                    nc.scalar.activation(node_in[b][:, :, 0:F], node_out[b][:, :, :], ACT.Copy).then_inc(init_padded[b], 1)
                    take(act, init_out[b], 32)
                    act.sem_inc(node_used[b], 1)

            for k, W in enumerate((WS, WD)):
                if k == 1:
                    act.wait_ge(edges_in, 16 * 6)
                    nc.scalar.activation(PAY[1][:, :, 2:WD], scan_in.rearrange("p (t a) -> p t a", a=A),
                                         ACT.Copy).then_inc(attr_copied, 1)
                for n in range(2):
                    take(act, pay_made)
                    with act.Fori(0, TURNS) as i:
                        for b in range(2):
                            landed(act, "act", sort_scatter[2 * k + n][b], i * (16 * C) + PRIME)
                            pc = put[b][:, 0:C * W].rearrange("p (c w) -> p c w", w=W)
                            nc.scalar.activation(pc, PAY[k][:, bass.ts(i * 2 + b, C), :], ACT.Copy).then_inc(pay_ready[b], 1)

            def root(n, m=1):
                for _ in range(m):
                    take(act, var_ready)
                    nc.scalar.activation(std[:, 0:n], var[:, 0:n], ACT.Sqrt).then_inc(std_ready, 1)

            with act.Fori(0, TURNS) as i:
                root(C, 4)
            with act.Fori(0, TURNS) as i:
                root(C, 2)
            with act.Fori(0, TURNS) as i:
                root(C, 2)
            take(act, e_ready)
            nc.scalar.activation(a_dst[:, :, :], a_dst[:, :, :], ACT.Exp).then_inc(p_ready, 1)
            with act.Fori(0, TURNS) as i:
                for b in range(2):
                    for g, (j0, j1) in enumerate(GROUPS):
                        take(act, turned)
                        nc.scalar.activation(catT[:, 0:(j1 - j0) * P], turn_ps[g % 2][:, 0:(j1 - j0) * P],
                                             ACT.Copy).then_inc(copied, 1)
            x3v = x3_table.rearrange("(p r) f -> p r f", p=P)
            ov = out.rearrange("(p r) f -> p r f", p=P)
            with act.Fori(0, TURNS) as i:
                for b in range(2):
                    root(C)
                    root(C)
                    root(C)
                    for g, (j0, j1) in enumerate(GROUPS):
                        n = (j1 - j0) * P
                        take(act, turned)
                        nc.scalar.activation(catT[0:CAT, 0:n], turn_ps[g % 2][0:CAT, 0:n], ACT.Copy).then_inc(copied, 1)
                        take(act, hid_ready)
                        nc.scalar.activation(hid[:, 0:n], hid_ps[0:MID, 0:n], ACT.Copy).then_inc(hid_copied, 1)
                    root(NC)
                    c = i * 2 + b
                    take(act, node_ready[b])
                    act.dma_start(x3v[:, bass.ts(c, NC), :], node_out[b][:, :, :]).then_inc(node_stored[b], 16)
                    act.dma_start(ov[:, bass.ts(c, NC), :], node_out[b][:, :, :]).then_inc(node_stored[b], 16)
            for b in range(2):
                take(act, node_stored[b], 32)
            act.sem_inc(nodes_done, 1)
            with act.Fori(0, TURNS) as i:
                root(C, 2)
            with act.Fori(0, TURNS) as i:
                root(C, 2)
            with act.Fori(0, TURNS) as i:
                root(C, 2)

        @block.tensor
        def _(pe):
            pe.wait_ge(consts_iota, 5)
            pe.wait_ge(consts_dve, 1)
            pe.wait_ge(consts_load, 16 * 9)

            def turn_ends():
                take(pe, ends_ready)
                nc.tensor.transpose(carry_ps[0:F, 0:P], ends[:, 0, :], ident[:, :])
                nc.tensor.transpose(carry_ps[0:F, P:2 * P], ends[:, 1, :], ident[:, :]).then_inc(ends_turned, 1)
                take(pe, carry_ready)
                nc.tensor.transpose(carry_ps[:, 256:256 + F], carryT[:, 0:P], ident[0:F, 0:F]).then_inc(carry_turned, 1)

            for k in range(2):
                for n, R in enumerate((LOW, HIGH)):
                    take(pe, hist_hot)
                    nc.tensor.matmul(hist_ps[:, 0:R], ones16[:, :], onehot[3][:, 0:R], start=True, stop=True)\
                        .then_inc(hist_free, 4)
                    with pe.Fori(0, TURNS) as i:
                        for j in range(2 * C):
                            pe.wait_ge(hist_hot, j + 1)
                            nc.tensor.matmul(hist_ps[:, 0:R], ones16[:, :], onehot[j % 4][:, 0:R],
                                             start=False, stop=True, skip_group_check=True).then_inc(hist_free, 1)
                        pe.sem_inc(hist_hot, -2 * C)
                    take(pe, base_ready)
                    for q in range(2):
                        nc.tensor.matmul(count_ps[q][:, 0:R], first_row[:, :], base[:, 0:R], start=True, stop=True,
                                         skip_group_check=True)
                    with pe.Fori(0, TURNS) as i:
                        for j in range(2 * C):
                            pe.wait_ge(rank_hot, j + 1)
                            nc.tensor.matmul(count_ps[j % 2][:, 0:R], before[:, :], onehot[j % 4][:, 0:R],
                                             start=False, stop=True, skip_group_check=True).then_inc(rank_ready, 1)
                            pe.wait_ge(rank_read, j + 1)
                            nc.tensor.matmul(count_ps[1 - j % 2][:, 0:R], rest[:, :], onehot[(j - 1) % 4][:, 0:R],
                                             start=False, stop=True, skip_group_check=True).then_inc(rank_free, 1)
                            nc.tensor.matmul(count_ps[1 - j % 2][:, 0:R], ones16[:, :], onehot[j % 4][:, 0:R],
                                             start=False, stop=True, skip_group_check=True).then_inc(rank_done, 1)
                        pe.sem_inc(rank_hot, -2 * C)
                        pe.sem_inc(rank_read, -2 * C)
                turn_ends()

            turn_ends()
            for _ in range(5):
                turn_ends()
            with pe.Fori(0, TURNS) as i:
                for b in range(2):
                    take(pe, q_ready)
                    for g, (j0, j1) in enumerate(GROUPS):
                        for j in range(j0, j1):
                            t = nc.tensor.transpose(turn_ps[g % 2][:, (j - j0) * P:(j - j0 + 1) * P],
                                                    prod[:, j, :, :].rearrange("p h f -> p (h f)"), ident[:, :])
                        t.then_inc(turned, 1)
                        if g == 0:
                            take(pe, y_used)
                        take(pe, copied)
                        for j in range(j0, j1):
                            t = nc.tensor.matmul(y_ps[:, j * F:(j + 1) * F], catT[:, (j - j0) * P:(j - j0 + 1) * P],
                                                 w_stack[:, :], start=True, stop=True, skip_group_check=True)
                        t.then_inc(q_free, 1)
                        if g == 3:
                            pe.wait_ge(q_free, 4)
                            pe.sem_inc(q_free, -4)
                            pe.sem_inc(y_ready, 1)
                        else:
                            pe.wait_ge(q_free, g + 1)
                            
            turn_ends()
            with pe.Fori(0, TURNS) as i:
                for b in range(2):
                    take(pe, cat_ready)
                    for g, (j0, j1) in enumerate(GROUPS):
                        n = (j1 - j0) * P
                        for j in range(j0, j1):
                            t = nc.tensor.transpose(turn_ps[g % 2][0:CAT, (j - j0) * P:(j - j0 + 1) * P],
                                                    cat[:, j, :], ident[:, :])
                        t.then_inc(turned, 1)
                        take(pe, copied)
                        nc.tensor.matmul(hid_ps[0:MID, 0:n], W1_sb[:, :], catT[0:CAT, 0:n], start=True, stop=True,
                                         skip_group_check=True).then_inc(hid_ready, 1)
                        take(pe, hid_act)
                        if g == 0:
                            take(pe, y_used)
                        for j in range(j0, j1):
                            t = nc.tensor.matmul(y_ps[:, j * F:(j + 1) * F], hidT[:, (j - j0) * P:(j - j0 + 1) * P],
                                                 W2_sb[:, :], start=True, stop=True, skip_group_check=True)
                        t.then_inc(v_ready, 1)
                    pe.wait_ge(v_ready, 4)
                    pe.sem_inc(v_ready, -4)
                    pe.sem_inc(y_ready, 1)
            turn_ends()
            turn_ends()

        @block.vector
        def _(dve):
            v = nc.vector
            chain = [0]

            def link(ins):
                chain[0] += 1
                ins.then_inc(dve_chain, 1)
                dve.wait_ge(dve_chain, chain[0])

            def chain_end():
                if chain[0]:
                    dve.sem_inc(dve_chain, -chain[0])
                chain[0] = 0

            def per_row(a, n, f=F):
                return a.unsqueeze(2).to_broadcast([P, n, f])

            def per_feature(a, n, f=F):
                return a.unsqueeze(1).to_broadcast([P, n, f])

            def layernorm_relu(src_ap, dst_ap, n):
                link(v.tensor_reduce(sums[:, 0:n], src_ap, AX.X, ALU.add))
                link(v.tensor_scalar(sums[:, 0:n], sums[:, 0:n], 1.0 / F, None, ALU.mult))
                link(v.tensor_tensor(cen[:, 0:n, :], src_ap, per_row(sums[:, 0:n], n), ALU.subtract))
                link(v.tensor_tensor(sqr[:, 0:n, :], cen[:, 0:n, :], cen[:, 0:n, :], ALU.mult))
                link(v.tensor_reduce(var[:, 0:n], sqr[:, 0:n, :], AX.X, ALU.add))
                link(v.tensor_scalar(var[:, 0:n], var[:, 0:n], 1.0 / F, 1e-5, ALU.mult, ALU.add))
                root(n)
                link(v.tensor_tensor(cen[:, 0:n, :], cen[:, 0:n, :], per_row(std[:, 0:n], n), ALU.mult))
                link(v.tensor_scalar(dst_ap, cen[:, 0:n, :], 0.0, None, ALU.max))

            def root(n):
                dve.sem_inc(var_ready, 1)
                take(dve, std_ready)
                link(v.reciprocal(std[:, 0:n], std[:, 0:n]))

            link(v.memset(onesT[:, :], 1.0))
            for b in range(2):
                link(v.memset(got[b][:, :, :], 0.0))
                link(v.memset(put[b][:, :], 0.0))
                link(v.memset(node_in[b][:, :, :], 0.0))
            link(v.memset(edge_prev[:, :], -1.0))
            link(v.memset(edge_next[:, :], -1.0))
            link(v.memset(ends[:, :, :], 0.0))
            link(v.memset(carryT[:, :], 0.0))
            dve.sem_inc(staging_set, 1)
            dve.wait_ge(consts_load, 16 * 9)
            for side in range(2):
                link(v.tensor_tensor(w_prod, w_all, per_feature(fcw_sb[:, side * F:(side + 1) * F], P), ALU.mult))
                link(v.tensor_reduce(u_heads[:, side, :, :].rearrange("p h f -> p (h f)"), w_prod, AX.X, ALU.add))
            dve.sem_inc(consts_dve, 1)
            dve.wait_ge(consts_iota, 5)
            dve.wait_ge(edges_in, 48)
            chain_end()

            def carries(op, values, factors, f, back=False):
                neutral = 0.0 if op == ALU.add else -BIG
                link(v.tensor_copy(ends[:, 0, 0:f], values))
                link(v.tensor_copy(ends[:, 1, 0:f], factors.to_broadcast([P, f])))
                dve.sem_inc(ends_ready, 1)
                take(dve, ends_turned)
                link(v.tensor_copy(endsT[:, :, :], carry_ps[0:F, 0:2 * P].rearrange("f (a p) -> f a p", a=2)))
                if op == ALU.max:
                    link(v.tensor_scalar(endsT[:, 1, :], endsT[:, 1, :], -1.0, BIG, ALU.add, ALU.mult))
                op0 = ALU.mult if op == ALU.add else ALU.add
                link(v.memset(carryT[:, :], neutral))
                if back:
                    link(v.tensor_tensor_scan(carryT[:, P - 2::-1], endsT[:, 1, P - 1:0:-1], endsT[:, 0, P - 1:0:-1],
                                              neutral, op0, op))
                else:
                    link(v.tensor_tensor_scan(carryT[:, 1:P + 1], endsT[:, 1, :], endsT[:, 0, :], neutral, op0, op))
                dve.sem_inc(carry_ready, 1)
                take(dve, carry_turned)
                link(v.tensor_copy(carry[:, :], carry_ps[:, 256:256 + F]))

            for k, W in enumerate((WS, WD)):
                if k == 0:
                    link(v.tensor_copy(PAY[0][:, :, 0], key_i[:, :]))
                    link(v.tensor_copy(PAY[0][:, :, 1], src_row[0][:, :]))
                    link(v.tensor_copy(PAY[0][:, :, 2], ew_sb[:, :]))
                else:
                    dve.sem_inc(pay_free, 1)
                    dve.wait_ge(edges_in, 16 * 6)
                    dve.wait_ge(attr_copied, 1)
                    link(v.tensor_copy(PAY[1][:, :, 0], src_row[1][:, :]))
                    link(v.tensor_copy(PAY[1][:, :, 1], key_i[:, :]))
                for n, R in enumerate((LOW, HIGH)):
                    if n == 1:
                        dve.wait_ge(pass_loaded, 16 * (1 + 4 * k))
                        link(v.tensor_copy(key_i[:, :], PAY[k][:, :, k]))
                    dve.sem_inc(pay_made, 1)
                    if n == 0:
                        link(v.tensor_scalar(key_i[:, :], key_i[:, :], LOW - 1, None, ALU.bitwise_and))
                    else:
                        link(v.tensor_scalar(key_i[:, :], key_i[:, :], 8, None, ALU.logical_shift_right))
                    link(v.tensor_copy(digit[:, :], key_i[:, :]))
                    link(v.memset(onehot[3][:, :], 0.0))
                    dve.sem_inc(hist_hot, 1)
                    chain_end()
                    with dve.Fori(0, TURNS) as i:
                        for b in range(2):
                            link(v.tensor_scalar(digit_c[:, :], digit[:, bass.ts(i * 2 + b, C)], 1.0, None, ALU.mult))
                            for j in range(C):
                                g = b * C + j
                                dve.wait_ge(hist_free, g + 1)
                                v.tensor_scalar(onehot[g % 4][:, 0:R], digits_row[:, 0:R], digit_c[:, j:j + 1], None,
                                                ALU.is_equal).then_inc(hist_hot, 1)
                            v.drain()
                        dve.sem_inc(hist_free, -2 * C)
                        chain_end()
                    take(dve, hist_free, 4)
                    link(v.tensor_copy(hist_sb[:, 0:R], hist_ps[:, 0:R]))
                    link(v.tensor_tensor_scan(base[:, 0:R], onesT[:, 0:R], hist_sb[:, 0:R], 0.0, ALU.mult, ALU.add))
                    link(v.tensor_tensor(base[:, 0:R], base[:, 0:R], hist_sb[:, 0:R], ALU.subtract))
                    link(v.memset(onehot[3][:, :], 0.0))
                    dve.sem_inc(base_ready, 1)
                    dve.sem_inc(rank_read, 1)
                    dve.sem_inc(rank_free, 3)
                    chain_end()
                    with dve.Fori(0, TURNS) as i:
                        for b in range(2):
                            link(v.tensor_scalar(digit_c[:, :], digit[:, bass.ts(i * 2 + b, C)], 1.0, None, ALU.mult))

                            def make_hot(j):
                                g = b * C + j
                                dve.wait_ge(rank_free, g + 1)
                                v.tensor_scalar(onehot[g % 4][:, 0:R], digits_row[:, 0:R], digit_c[:, j:j + 1], None,
                                                ALU.is_equal).then_inc(rank_hot, 1)

                            make_hot(0)
                            for j in range(C):
                                g = b * C + j
                                if j + 1 < C:
                                    make_hot(j + 1)
                                dve.wait_ge(rank_ready, g + 1)
                                v.tensor_tensor_reduce((junk, hist_sb)[g % 2][:, 0:R], count_ps[g % 2][:, 0:R], onehot[g % 4][:, 0:R],
                                                       1.0, 0.0, ALU.mult, ALU.add, rank_c[:, j:j + 1]).then_inc(rank_read, 1)
                            landed(dve, "dve", sort_scatter[2 * k + n][b], i * (16 * C) + PRIME)
                            v.drain()
                            if n == 0:
                                link(v.tensor_copy(int_c[:, 0, :], rank_c[:, :]))
                                link(v.tensor_scalar(int_c[:, 1, :], int_c[:, 0, :], 7, None, ALU.logical_shift_right))
                                link(v.tensor_scalar(int_c[:, 0, :], int_c[:, 0, :], P - 1, None, ALU.bitwise_and))
                                link(v.tensor_copy(flt_c[:, :, :], int_c[:, :, :]))
                                link(v.scalar_tensor_tensor(out=rank_c[:, :], in0=flt_c[:, 0, :], scalar=float(T),
                                                            in1=flt_c[:, 1, :], op0=ALU.mult, op1=ALU.add))
                            v.tensor_copy(row_c[b][:, 1, :], rank_c[:, :]).then_inc(rows_ready[b], 1)
                        dve.sem_inc(rank_free, -2 * C)
                        dve.sem_inc(rank_ready, -2 * C)
                        chain_end()
                    take(dve, rank_free, 3)
                    take(dve, rank_done, T)
                    take(dve, rank_read)

                dve.wait_ge(pass_loaded, 16 * (4 + 4 * k))
                S, D = PAY[k][:, :, 0], PAY[k][:, :, 1]
                link(v.tensor_copy(keyf[:, :], PAY[k][:, :, k]))
                if k == 0:
                    link(v.tensor_copy(ew_sb[:, :], PAY[0][:, :, 2]))
                link(v.tensor_scalar(junk[:, :], S, float(N - 1), None, ALU.min))
                link(v.tensor_copy(src_row[k][:, :], junk[:, :]))
                link(v.tensor_scalar(junk[:, :], D, float(N - 1), None, ALU.min))
                link(v.tensor_copy(dst_row[k][:, :], junk[:, :]))
                link(v.tensor_tensor(same[k][:, 1:T], keyf[:, 1:T], keyf[:, 0:T - 1], ALU.is_equal))
                link(v.tensor_tensor(same[k][:, 0:1], keyf[:, 0:1], edge_prev[:, :], ALU.is_equal))
                link(v.tensor_tensor(last[k][:, 0:T - 1], keyf[:, 0:T - 1], keyf[:, 1:T], ALU.not_equal))
                link(v.tensor_tensor(last[k][:, T - 1:T], keyf[:, T - 1:T], edge_next[:, :], ALU.not_equal))
                link(v.tensor_tensor_scan(whole[k][:, :], same[k][:, :], onesT[:, :], 1.0, ALU.mult, ALU.mult))
                link(v.tensor_scalar(junk[:, :], last[k][:, :], -SKIP, SKIP, ALU.mult, ALU.add))
                link(v.tensor_tensor(junk[:, :], junk[:, :], keyf[:, :], ALU.add))
                link(v.tensor_copy(out_row[k][:, :], junk[:, :]))
                if k == 0:
                    link(v.tensor_scalar(more[:, :], last[0][:, :], -1.0, 1.0, ALU.mult, ALU.add))
                    link(v.tensor_tensor_scan(tail[:, ::-1], more[:, ::-1], onesT[:, :], 1.0, ALU.mult, ALU.mult))
                link(v.tensor_tensor_scan(deg[k][:, :], same[k][:, :], onesT[:, :], 0.0, ALU.mult, ALU.add))
                carries(ALU.add, deg[k][:, T - 1:T], whole[k][:, T - 1:T], 1)
                link(v.scalar_tensor_tensor(out=deg[k][:, :], in0=whole[k][:, :], scalar=carry[:, 0:1],
                                            in1=deg[k][:, :], op0=ALU.mult, op1=ALU.add))
                chain_end()

            def scan_chunk(c, data, factors, neutral_op, op):
                for f in range(F):
                    ins = v.tensor_tensor_scan(SEG[:, bass.ds(c * C + 1, C), f], factors, data[:, :, f],
                                               SEG[:, bass.ds(c * C, 1), f], neutral_op, op)
                link(ins)

            def give_rows(b, c, sides):
                for way, rows in sides:
                    link(v.tensor_copy(row_c[b][:, way, :], rows[:, bass.ts(c, C)]))
                dve.sem_inc(rows_ready[b], 1)

            def passed(name, b, i, ways):
                landed(dve, "dve", gathers[name][b], (i + 1) * (16 * C * ways))

            def rows_of(b, way, width=F):
                return got[b][:, way, 0:C * width].rearrange("p (c w) -> p c w", w=width)

            def heads_dot(side, h_ap, dst_ap):
                link(v.tensor_tensor(prod[:, :, :, :],
                                     h_ap.unsqueeze(2).to_broadcast([P, C, H, F]),
                                     u_heads[:, side, :, :].unsqueeze(1).to_broadcast([P, C, H, F]), ALU.mult))
                link(v.tensor_reduce(dst_ap, prod[:, :, :, :].rearrange("p c h f -> p h c f"), AX.X, ALU.add))

            def gather_loop(name, sides, body, between):
                ways = len(sides)
                for b in range(2):
                    for way, rows in sides:
                        link(v.tensor_copy(row_c[b][:, way, :], rows[:, b * C:(b + 1) * C]))
                    dve.sem_inc(rows_ready[b], 1)
                chain_end()
                with dve.Fori(0, TURNS - 1) as i:
                    for b in range(2):
                        passed(name, b, i, ways)
                        body(b, i)
                        give_rows(b, i * 2 + b + 2, sides)
                    chain_end()
                for b in range(2):
                    passed(name, b, TURNS - 1, ways)
                    body(b, TURNS - 1)
                chain_end()

            def scatter_loop(name, k, body):
                with dve.Fori(0, TURNS) as i:
                    for b in range(2):
                        landed(dve, "dve", scatters[name][b], i * (16 * C) + PRIME)
                        link(v.tensor_copy(row_c[b][:, 1, :], out_row[k][:, bass.ts(i * 2 + b, C)]))
                        body(b, i * 2 + b)
                        dve.sem_inc(put_ready[b], 1)
                    chain_end()

            def neutral_column(value):
                link(v.memset(SEG[:, 0, :], value))

            def with_carry(c, k, dst_ap):
                link(v.tensor_tensor(dst_ap, per_row(whole[k][:, bass.ts(c, C)], C), per_feature(carry[:, :], C), ALU.mult))
                link(v.tensor_tensor(dst_ap, dst_ap, SEG[:, bass.ds(c * C + 1, C), :], ALU.add))

            def l0_gathered(b, i):
                c = i * 2 + b
                layernorm_relu(rows_of(b, 0), ha[:, :, :], C)
                layernorm_relu(rows_of(b, 1), hb[:, :, :], C)
                link(v.tensor_tensor(X[:, bass.ts(c, C), :], rows_of(b, 1), per_row(onesT[:, 0:C], C), ALU.mult))
                link(v.tensor_tensor(ha[:, :, :], ha[:, :, :], hb[:, :, :], ALU.subtract))
                link(v.tensor_tensor(ha[:, :, :], ha[:, :, :], per_row(ew_sb[:, bass.ts(c, C)], C), ALU.mult))
                scan_chunk(c, ha, same[0][:, bass.ts(c, C)], ALU.mult, ALU.add)

            neutral_column(0.0)
            gather_loop("l0", [(0, dst_row[0]), (1, src_row[0])], l0_gathered, None)
            carries(ALU.add, SEG[:, T, :], whole[0][:, T - 1:T], F)
            chain_end()

            def l0_put(b, c):
                rows = put[b][:, 0:C * F].rearrange("p (c w) -> p c w", w=F)
                with_carry(c, 0, ha[:, :, :])
                link(v.tensor_tensor(rows, ha[:, :, :], X[:, bass.ts(c, C), :], ALU.add))
                link(v.tensor_tensor(X[:, bass.ts(c, C), :], rows, per_row(onesT[:, 0:C], C), ALU.mult))
                layernorm_relu(rows, hb[:, :, :], C)
                heads_dot(0, hb[:, :, :], a_src[:, :, bass.ts(c, C)])

            dve.wait_ge(tables_ready, 1)
            scatter_loop("l0", 0, l0_put)

            def per_head(a):
                return a.unsqueeze(1).to_broadcast([P, H, T])

            def spread_back(a, tmp, dst_ap):
                link(v.tensor_tensor(tmp[:, :, :], a[:, :, :], per_head(last[0][:, :]), ALU.mult))
                for h in range(H):
                    ins = v.tensor_tensor_scan(dst_ap[:, h, ::-1], more[:, ::-1], tmp[:, h, ::-1], 0.0, ALU.mult, ALU.add)
                link(ins)
                carries(ALU.add, dst_ap[:, :, 0], tail[:, 0:1], H, back=True)
                link(v.tensor_tensor(tmp[:, :, :], per_head(tail[:, :]),
                                     carry[:, 0:H].unsqueeze(2).to_broadcast([P, H, T]), ALU.mult))
                link(v.tensor_tensor(dst_ap[:, :, :], dst_ap[:, :, :], tmp[:, :, :], ALU.add))

            spread_back(a_src, scan_a, scan_b)
            dve.wait_ge(layer_done, 1)
            chain_end()

            def l1_gathered(b, i):
                c = i * 2 + b
                rows = put[b][:, 0:C * F].rearrange("p (c w) -> p c w", w=F)
                take(dve, h1_stored[b], 16)
                layernorm_relu(rows_of(b, 0), rows, C)
                dve.sem_inc(h1_ready[b], 1)
                heads_dot(1, rows, a_dst[:, :, bass.ts(c, C)])

            for b in range(2):
                dve.sem_inc(h1_stored[b], 16)
            gather_loop("l1", [(0, dst_row[0])], l1_gathered, None)
            for b in range(2):
                take(dve, h1_stored[b], 16)
                dve.sem_inc(h1_used[b], 1)
                dve.sem_inc(h1_used[b], 1)
            link(v.tensor_tensor(scan_a[:, :, :], a_dst[:, :, :], scan_b[:, :, :], ALU.add))
            link(v.tensor_scalar(scan_a[:, :, :], scan_a[:, :, :], fcb_sb[:, 0:1], None, ALU.add))
            link(v.scalar_tensor_tensor(out=a_dst[:, :, :], in0=scan_a[:, :, :], scalar=0.2, in1=scan_a[:, :, :],
                                        op0=ALU.mult, op1=ALU.max))
            link(v.tensor_scalar(junk[:, :], same[0][:, :], -1.0, BIG, ALU.add, ALU.mult))
            for h in range(H):
                ins = v.tensor_tensor_scan(scan_a[:, h, :], junk[:, :], a_dst[:, h, :], -BIG, ALU.add, ALU.max)
            link(ins)
            carries(ALU.max, scan_a[:, :, T - 1], whole[0][:, T - 1:T], H)
            link(v.tensor_scalar(junk[:, :], whole[0][:, :], -1.0, BIG, ALU.add, ALU.mult))
            for h in range(H):
                ins = v.scalar_tensor_tensor(out=scan_a[:, h, :], in0=junk[:, :], scalar=carry[:, h:h + 1],
                                             in1=scan_a[:, h, :], op0=ALU.add, op1=ALU.max)
            link(ins)
            spread_back(scan_a, scan_b, a_src)
            link(v.tensor_tensor(a_dst[:, :, :], a_dst[:, :, :], a_src[:, :, :], ALU.subtract))
            dve.sem_inc(e_ready, 1)
            take(dve, p_ready)
            for h in range(H):
                ins = v.tensor_tensor_scan(scan_a[:, h, :], same[0][:, :], a_dst[:, h, :], 0.0, ALU.mult, ALU.add)
            link(ins)
            carries(ALU.add, scan_a[:, :, T - 1], whole[0][:, T - 1:T], H)
            for h in range(H):
                ins = v.scalar_tensor_tensor(out=scan_a[:, h, :], in0=whole[0][:, :], scalar=carry[:, h:h + 1],
                                             in1=scan_a[:, h, :], op0=ALU.mult, op1=ALU.add)
            link(ins)
            spread_back(scan_a, scan_b, a_src)
            link(v.reciprocal(a_src[:, :, :], a_src[:, :, :]))
            link(v.tensor_tensor(a_dst[:, :, :], a_dst[:, :, :], a_src[:, :, :], ALU.mult))
            link(v.tensor_scalar(a_dst[:, :, :], a_dst[:, :, :], 1.0 / H, None, ALU.mult))
            neutral_column(0.0)
            dve.sem_inc(y_used, 1)
            chain_end()
            with dve.Fori(0, TURNS) as i:
                for b in range(2):
                    c = i * 2 + b
                    take(dve, h1_loaded[b], 16)
                    for h in range(H):
                        ins = v.tensor_tensor(prod[:, :, h, :], rows_of(b, 0),
                                              per_row(a_dst[:, h, bass.ts(c, C)], C), ALU.mult)
                    link(ins)
                    dve.sem_inc(h1_used[b], 1)
                    dve.sem_inc(q_ready, 1)
                    take(dve, y_ready)
                    scan_chunk(c, y_ps[:, 0:C * F].rearrange("p (c w) -> p c w", w=F),
                               same[0][:, bass.ts(c, C)], ALU.mult, ALU.add)
                    dve.sem_inc(y_used, 1)
                chain_end()
            carries(ALU.add, SEG[:, T, :], whole[0][:, T - 1:T], F)
            chain_end()

            def l1_put(b, c):
                rows = put[b][:, :].rearrange("p (c w) -> p c w", w=RW)
                with_carry(c, 0, ha[:, :, :])
                link(v.tensor_tensor(rows[:, :, 0:F], ha[:, :, :], X[:, bass.ts(c, C), :], ALU.add))
                link(v.tensor_scalar(rows[:, :, F], deg[0][:, bass.ts(c, C)], 1.0, None, ALU.mult))

            scatter_loop("l1", 0, l1_put)
            neutral_column(-BIG)
            dve.wait_ge(layer_done, 2)
            link(v.memset(hidT, 1.0))
            link(v.memset(cat, 1.0))
            for b in range(2):
                dve.sem_inc(attr_used[b], 1)
                dve.sem_inc(node_stored[b], 32)
                dve.sem_inc(node_used[b], 1)
            link(v.tensor_scalar(digit[:, :], same[1][:, :], -1.0, BIG, ALU.add, ALU.mult))
            link(v.tensor_scalar(base[:, :], whole[1][:, :], -1.0, BIG, ALU.add, ALU.mult))
            chain_end()

            def l2_gathered(b, i):
                c = i * 2 + b
                s_rows, d_rows = rows_of(b, 0, RW), rows_of(b, 1, RW)
                link(v.tensor_tensor(ha[:, :, :], s_rows[:, :, 0:F], per_feature(bias_sb[:, :], C), ALU.add))
                layernorm_relu(ha[:, :, :], cat[:, :, 0:F], C)
                link(v.tensor_tensor(hb[:, :, :], d_rows[:, :, 0:F], per_feature(bias_sb[:, :], C), ALU.add))
                layernorm_relu(hb[:, :, :], cat[:, :, F:2 * F], C)
                link(v.tensor_tensor(X[:, bass.ts(c, C), :], hb[:, :, :], per_row(onesT[:, 0:C], C), ALU.mult))
                link(v.tensor_scalar(var[:, 0:C], s_rows[:, :, F], 1.0, None, ALU.max))
                root(C)
                link(v.tensor_tensor(more[:, bass.ts(c, C)], std[:, 0:C], onesT[:, 0:C], ALU.mult))
                take(dve, attr_loaded[b], 16)
                link(v.tensor_copy(cat[:, :, 2 * F:2 * F + A], attr_c[b][:, :, 2:WD]))
                dve.sem_inc(attr_used[b], 1)
                dve.sem_inc(cat_ready, 1)
                for g, (j0, j1) in enumerate(GROUPS):
                    n = (j1 - j0) * P
                    take(dve, hid_copied)
                    link(v.scalar_tensor_tensor(out=hidT[0:MID, 0:n], in0=hid[:, 0:n], scalar=0.01,
                                                in1=hid[:, 0:n], op0=ALU.mult, op1=ALU.max))
                    dve.sem_inc(hid_act, 1)
                take(dve, y_ready)
                link(v.tensor_copy(ha[:, :, :], y_ps[:, 0:C * F].rearrange("p (c w) -> p c w", w=F)))
                dve.sem_inc(y_used, 1)
                link(v.scalar_tensor_tensor(out=hb[:, :, :], in0=ha[:, :, :], scalar=0.01,
                                            in1=ha[:, :, :], op0=ALU.mult, op1=ALU.max))
                scan_chunk(c, hb, digit[:, bass.ts(c, C)], ALU.add, ALU.max)
                take(dve, node_loaded[b], 16)
                take(dve, node_stored[b], 32)
                link(v.tensor_tensor(node_out[b][:, :, :], node_in[b][:, :, 0:F], per_feature(bias_sb[:, :], NC), ALU.add))
                dve.sem_inc(node_used[b], 1)
                layernorm_relu(node_out[b][:, :, :], sqr[:, :, :], NC)
                link(v.tensor_tensor(node_out[b][:, :, :], node_out[b][:, :, :], sqr[:, :, :], ALU.add))
                dve.sem_inc(node_ready[b], 1)

            gather_loop("l2", [(0, src_row[1]), (1, dst_row[1])], l2_gathered, None)
            carries(ALU.max, SEG[:, T, :], whole[1][:, T - 1:T], F)
            chain_end()

            def l2_put(b, c):
                rows = put[b][:, 0:C * F].rearrange("p (c w) -> p c w", w=F)
                x2 = X[:, bass.ts(c, C), :]
                link(v.tensor_tensor(ha[:, :, :], x2, per_row(onesT[:, 0:C], C), ALU.mult))
                layernorm_relu(ha[:, :, :], hb[:, :, :], C)
                link(v.tensor_tensor(rows, per_row(base[:, bass.ts(c, C)], C), per_feature(carry[:, :], C), ALU.add))
                link(v.tensor_tensor(rows, rows, SEG[:, bass.ds(c * C + 1, C), :], ALU.max))
                link(v.tensor_tensor(rows, rows, hb[:, :, :], ALU.max))
                link(v.tensor_tensor(rows, rows, ha[:, :, :], ALU.add))
                link(v.tensor_tensor(x2, rows, per_row(onesT[:, 0:C], C), ALU.mult))

            scatter_loop("l2", 1, l2_put)

            neutral_column(0.0)
            link(v.tensor_scalar(deg[1][:, :], deg[1][:, :], 1.0, None, ALU.max))
            dve.wait_ge(layer_done, 3)
            chain_end()

            def l3_gathered(b, i):
                c = i * 2 + b
                layernorm_relu(rows_of(b, 0), ha[:, :, :], C)
                link(v.tensor_tensor(ha[:, :, :], ha[:, :, :], per_row(more[:, bass.ts(c, C)], C), ALU.mult))
                scan_chunk(c, ha, same[1][:, bass.ts(c, C)], ALU.mult, ALU.add)

            gather_loop("l3", [(0, src_row[1])], l3_gathered, None)
            carries(ALU.add, SEG[:, T, :], whole[1][:, T - 1:T], F)
            chain_end()

            def l3_put(b, c):
                rows = put[b][:, 0:C * F].rearrange("p (c w) -> p c w", w=F)
                with_carry(c, 1, ha[:, :, :])
                link(v.tensor_scalar(var[:, 0:C], deg[1][:, bass.ts(c, C)], 1.0, None, ALU.mult))
                root(C)
                link(v.tensor_tensor(ha[:, :, :], ha[:, :, :], per_row(std[:, 0:C], C), ALU.mult))
                link(v.tensor_tensor(rows, ha[:, :, :], X[:, bass.ts(c, C), :], ALU.add))

            scatter_loop("l3", 1, l3_put)
            dve.wait_ge(layer_done, 4)


_INS = ["x", "src", "dst", "edge_attr_16", "edge_weight", "L1_gnn_w", "L1_gnn_fc_w", "L1_gnn_fc_b", "L1_gnn_bias",
        "L2_gnn_W1", "L2_gnn_b1", "L2_gnn_W2", "L2_gnn_b2"]


def kernel(**inputs):
    import concourse.bacc as _bacc
    from concourse.bass_utils import run_bass_kernel_spmd as _run

    def padded(a, rows, fill):
        a = np.asarray(a)
        return np.concatenate([a, np.full((rows - a.shape[0],) + a.shape[1:], fill, a.dtype)])

    given = {n: np.ascontiguousarray(inputs[n]) for n in _INS}
    given["x"] = padded(given["x"], NP, 0)
    given["src"] = padded(given["src"], EP, PADKEY)
    given["dst"] = padded(given["dst"], EP, PADKEY)
    given["edge_attr_16"] = padded(given["edge_attr_16"], EP, 0)
    given["edge_weight"] = padded(given["edge_weight"], EP, 0)
    nc = _bacc.Bacc("TRN2", target_bir_lowering=False, num_devices=1)
    arrays, args = {}, []
    for n in _INS:
        a = given[n]
        arrays[f"in_{n}_dram"] = a
        args.append(nc.dram_tensor(f"in_{n}_dram", a.shape, mybir.dt.from_np(a.dtype), kind="ExternalInput").ap())
    out = nc.dram_tensor("out_0_dram", (NP, F), F32, kind="ExternalOutput").ap()
    build_gnn(nc, *args, out)
    r = _run(nc, [arrays], core_ids=[0])
    return r.results[0]["out_0_dram"][0:N]
```

```python
from contextlib import ExitStack

import numpy as np
import concourse.bass as bass
from concourse import mybir

ALU = mybir.AluOpType
ACT = mybir.ActivationFunctionType
AX = mybir.AxisListType
F32 = mybir.dt.float32
F16 = mybir.dt.float16
I32 = mybir.dt.int32

P = 128
N = 100000
E = 50000
F = 32
H = 4
A = 16
MID = 56
C = 14
T = 392
CHUNKS = T // C
TURNS = CHUNKS // 2
EP = P * T
ROWS = 784
NP = P * ROWS
NC = ROWS // CHUNKS
LOW = 256
HIGH = 391
PADKEY = (HIGH - 1) * LOW + LOW - 1
RW = 36
WS, WD = 3, 2 + A
CAT = 2 * F + A + 1
BIG = 1.5e38
SKIP = 200000.0
assert T % (2 * C) == 0 and EP >= E and NP >= N and PADKEY >= N and (2 * C) % 4 == 0


def build_gnn(nc, x, src, dst, attr, ew, w, fc_w, fc_b, bias, W1, b1, W2, b2, out):
    mid_table = [nc.dram_tensor(f"mid_table{k}", (EP, W), F32).ap() for k, W in enumerate((WS, WD))]
    edge_table = [nc.dram_tensor(f"edge_table{k}", (EP, W), F32).ap() for k, W in enumerate((WS, WD))]
    x1_table = nc.dram_tensor("x1_table", (NP, F), F32).ap()
    x2_table = nc.dram_tensor("x2_table", (NP, RW), F32).ap()
    x3_table = nc.dram_tensor("x3_table", (NP, F), F32).ap()
    h1_table = nc.dram_tensor("h1_table", (P, T * F), F32).ap()

    with ExitStack() as ctx:
        def sb(name, shape, dt=F32):
            return ctx.enter_context(nc.sbuf_tensor(name, shape, dt))

        def sem(name):
            return ctx.enter_context(nc.semaphore(name))

        def sems(name, n=2):
            return [sem(f"{name}{i}") for i in range(n)]

        digits_row = sb("digits_row", [P, T], F16)
        before = sb("before", [P, P], F16)
        rest = sb("rest", [P, P], F16)
        ones16 = sb("ones16", [P, P], F16)
        first_row = sb("first_row", [P, P])
        ident = sb("ident", [P, P])
        onesT = sb("onesT", [P, T])
        u_heads = sb("u_heads", [P, 2, H, F])
        fcb_sb = sb("fcb_sb", [P, 1])
        bias_sb = sb("bias_sb", [P, F])
        w_stack = sb("w_stack", [P, F])
        W1_sb = sb("W1_sb", [CAT, MID])
        W2_sb = sb("W2_sb", [MID + 1, F])

        X = sb("X", [P, T, F])
        SEG = sb("SEG", [P, T + 1, F])
        PAY = [SEG[:, :, :].rearrange("p t f -> p (t f)")[:, 0:T * W].rearrange("p (t w) -> p t w", w=W)
               for W in (WS, WD)]
        scan_in = X[:, :, :].rearrange("p t f -> p (t f)")[:, 0:T * A]
        key_i = sb("key_i", [P, T], I32)
        digit = sb("digit", [P, T])
        high = sb("high", [P, T])
        ew_sb = sb("ew_sb", [P, T])
        keyf = sb("keyf", [P, T])
        same = [sb(f"same{k}", [P, T]) for k in range(2)]
        whole = [sb(f"whole{k}", [P, T]) for k in range(2)]
        last = [sb(f"last{k}", [P, T]) for k in range(2)]
        deg = [sb(f"deg{k}", [P, T]) for k in range(2)]
        more = sb("more", [P, T])
        tail = sb("tail", [P, T])
        src_row = [sb(f"src_row{k}", [P, T], I32) for k in range(2)]
        dst_row = [sb(f"dst_row{k}", [P, T], I32) for k in range(2)]
        out_row = [sb(f"out_row{k}", [P, T], I32) for k in range(2)]
        a_src = sb("a_src", [P, H, T])
        a_dst = sb("a_dst", [P, H, T])
        seg_flat = SEG[:, :, :].rearrange("p t f -> p (t f)")
        scan_a, scan_b = (seg_flat[:, q * H * T:(q + 1) * H * T].rearrange("p (h t) -> p h t", h=H)
                          for q in range(2))

        onehot = [sb(f"onehot{i}", [P, T], F16) for i in range(4)]
        high_hot = [sb(f"high_hot{i}", [P, HIGH + 1], F16) for i in range(2)]
        digit_c = sb("digit_c", [P, C])
        high_c = sb("high_c", [P, C])
        base = sb("base", [P, T])
        hist_sb = sb("hist_sb", [P, T])
        junk = sb("junk", [P, T])
        rank_c = sb("rank_c", [P, C])
        int_c = sb("int_c", [P, 2, C], I32)
        flt_c = sb("flt_c", [P, 2, C])
        row_c = [sb(f"row_c{b}", [P, 2, C], I32) for b in range(2)]
        got = [sb(f"got{b}", [P, 2, C * RW]) for b in range(2)]
        put = [sb(f"put{b}", [P, C * RW]) for b in range(2)]
        attr_c = [sb(f"attr_c{b}", [P, C, WD]) for b in range(2)]
        sums = sb("sums", [P, NC])
        var = sb("var", [P, NC])
        std = sb("std", [P, NC])
        cen = sb("cen", [P, NC, F])
        cen_flat = cen[:, :, :].rearrange("p c f -> p (c f)")
        sqr = sb("sqr", [P, NC, F])
        ha = sb("ha", [P, C, F])
        hb = sb("hb", [P, C, F])
        a_dst_flat = a_dst[:, :, :].rearrange("p h t -> p (h t)")
        a_src_flat = a_src[:, :, :].rearrange("p h t -> p (h t)")
        cat = a_dst_flat[:, 0:C * CAT].rearrange("p (c k) -> p c k", k=CAT)
        catT = a_src_flat[:, 0:4 * P]
        hid = a_src_flat[0:MID, 4 * P:8 * P]
        hidT = a_src_flat[0:MID + 1, 8 * P:12 * P]
        qT = [a_src_flat[:, q * 4 * P:(q + 1) * 4 * P] for q in range(2)]
        node_in_all = sb("node_in", [P, 2, NC * RW])
        node_in = [node_in_all[:, b, :].rearrange("p (r w) -> p r w", w=RW) for b in range(2)]
        prod = node_in_all[:, :, :].rearrange("p b n -> p (b n)")[:, 0:C * H * F]\
            .rearrange("p (c h f) -> p c h f", h=H, f=F)
        node_out = [sb(f"node_out{b}", [P, NC, F]) for b in range(2)]
        w_all = X[:, 0:P, :]
        w_prod = X[:, P:2 * P, :]
        fcw_sb = sb("fcw_sb", [P, 2 * F])
        primer = sb("primer", [16, F])
        dst_prev = sb("dst_prev", [P, 1], I32)
        disorder = sb("disorder", [P, 1])
        unsorted = sb("unsorted", [1, 1], I32)
        fix = sb("fix", [P, RW])
        fix_c = sb("fix_c", [P, RW])
        fix_row = sb("fix_row", [P, 1], I32)
        edge_prev = sb("edge_prev", [P, 1])
        edge_next = sb("edge_next", [P, 1])
        ends = sb("ends", [P, 2, F])
        endsT = sb("endsT", [F, 2, P])
        carryT = sb("carryT", [F, P + 1])
        carry = sb("carry", [P, F])

        hist_ps = ctx.enter_context(nc.psum_tensor("hist_ps", [P, 512], F32))
        count_ps = [ctx.enter_context(nc.psum_tensor(f"count_ps{b}", [P, 512], F32)) for b in range(2)]
        turn_ps = [ctx.enter_context(nc.psum_tensor(f"turn_ps{b}", [P, 512], F32)) for b in range(2)]
        y_ps = ctx.enter_context(nc.psum_tensor("y_ps", [P, 512], F32))
        hid_ps = ctx.enter_context(nc.psum_tensor("hid_ps", [P, 512], F32))
        y_banks = [y_ps, hid_ps]
        carry_ps = ctx.enter_context(nc.psum_tensor("carry_ps", [P, 512], F32))

        turns = {e: sem(f"turns_{e}") for e in ("dve", "act", "pool", "sp", "pe")}
        dve_chain = sem("dve_chain")
        consts_iota, consts_load, consts_dve = sem("consts_iota"), sem("consts_load"), sem("consts_dve")
        edges_in = sem("edges_in")
        attr_copied = sem("attr_copied")
        hist_hot, hist_free, hist_done, base_ready = sem("hist_hot"), sem("hist_free"), sem("hist_done"), sem("base_ready")
        rank_hot, rank_free, rank_ready, rank_read, rank_done = (
            sem("rank_hot"), sem("rank_free"), sem("rank_ready"), sem("rank_read"), sem("rank_done"))
        rows_ready, pay_ready = sems("rows_ready"), sems("pay_ready")
        sort_scatter = [sems(f"sort_scatter{n}_") for n in range(4)]
        high_hot_ready, high_free = sem("high_hot_ready"), sem("high_free")
        disorder_ready, disorder_sum, unsorted_ready = sem("disorder_ready"), sem("disorder_sum"), sem("unsorted_ready")
        natural_ready, natural_stored, edges_loaded = sem("natural_ready"), sem("natural_stored"), sem("edges_loaded")
        q_used, q_last, fix_ready, fix_written = sem("q_used"), sem("q_last"), sem("fix_ready"), sem("fix_written")
        pass_written, pass_loaded, pay_free, pay_made = sem("pass_written"), sem("pass_loaded"), sem("pay_free"), sem("pay_made")
        ends_ready, ends_turned, carry_ready, carry_turned = (
            sem("ends_ready"), sem("ends_turned"), sem("carry_ready"), sem("carry_turned"))
        var_ready, std_ready = sem("var_ready"), sem("std_ready")
        got_free = sems("got_free")
        gathers = {n: sems(f"gather_{n}_") for n in ("l0", "l1", "l2", "l3")}
        scatters = {n: sems(f"scatter_{n}_") for n in ("l0", "l1", "l2", "l3")}
        put_ready = sems("put_ready")
        layer_done = sem("layer_done")
        layer_start = sem("layer_start")
        init_in, init_out, init_padded = sems("init_in"), sems("init_out"), sems("init_padded")
        tables_ready = sem("tables_ready")
        h1_ready, h1_stored, h1_loaded, h1_used = sems("h1_ready"), sems("h1_stored"), sems("h1_loaded"), sems("h1_used")
        h1_all = sem("h1_all")
        e_ready, p_ready = sem("e_ready"), sem("p_ready")
        q_ready, q_free, y_ready, y_used = sem("q_ready"), sem("q_free"), sem("y_ready"), sem("y_used")
        turned, copied = sem("turned"), sem("copied")
        attr_loaded, attr_used = sems("attr_loaded"), sems("attr_used")
        cat_ready, cat_used, hid_ready, hid_copied, hid_act, v_ready = (
            sem("cat_ready"), sem("cat_used"), sem("hid_ready"), sem("hid_copied"), sem("hid_act"), sem("v_ready"))
        node_loaded, node_used, node_ready, node_stored = (
            sems("node_loaded"), sems("node_used"), sems("node_ready"), sems("node_stored"))
        nodes_done = sem("nodes_done")
        staging_set = sem("staging_set")

        PRIMED = [s for pair in (*sort_scatter, *scatters.values()) for s in pair]
        PRIME = 16
        primer_row = bias.rearrange("(a n) -> a n", a=1)

        def take(eng, s, n=1):
            eng.wait_ge(s, n)
            eng.sem_inc(s, -n)

        def landed(eng, name, s, value):
            eng.wait_ge(s, value)
            eng.sem_inc(turns[name], 1)

        def dst_unsorted(eng):
            eng.wait_ge(unsorted_ready, 1)
            return eng.value_load(unsorted[0:1, 0:1], min_val=0, max_val=1) != 0

        block = ctx.enter_context(nc.Block())
        GROUPS = [(0, 4), (4, 8), (8, 12), (12, 14)]

        @block.gpsimd
        def _(pool):
            nc.gpsimd.iota(digits_row[:, :], [[1, T]], base=0, channel_multiplier=0,
                           allow_small_or_imprecise_dtypes=True)
            nc.gpsimd.memset(ident[:, :], 0.0)
            nc.gpsimd.memset(before[:, :], 1.0)
            nc.gpsimd.memset(rest[:, :], 1.0)
            nc.gpsimd.memset(ones16[:, :], 1.0)
            nc.gpsimd.memset(first_row[:, :], 1.0)
            pool.drain().then_inc(consts_iota, 1)
            pool.wait_ge(consts_iota, 1)
            nc.gpsimd.affine_select(out=ident[:, :], in_=ident[:, :], compare_op=ALU.not_equal, fill=1.0,
                                    base=0, pattern=[[-1, P]], channel_multiplier=1).then_inc(consts_iota, 1)
            nc.gpsimd.affine_select(out=before[:, :], in_=before[:, :], compare_op=ALU.is_ge, fill=0.0,
                                    base=-1, pattern=[[1, P]], channel_multiplier=-1).then_inc(consts_iota, 1)
            nc.gpsimd.affine_select(out=rest[:, :], in_=rest[:, :], compare_op=ALU.is_ge, fill=0.0,
                                    base=0, pattern=[[-1, P]], channel_multiplier=1).then_inc(consts_iota, 1)
            nc.gpsimd.affine_select(out=first_row[:, :], in_=first_row[:, :], compare_op=ALU.is_ge, fill=0.0,
                                    base=0, pattern=[[0, P]], channel_multiplier=-1).then_inc(consts_iota, 1)
            pool.wait_ge(staging_set, 2)

            for n, s in enumerate(PRIMED):
                pool.dma_start(primer[n:n + 1, :], primer_row).then_inc(s, 16)

            def gather(b, way, table, width, s):
                for j in range(C):
                    pool.indirect_dma_start(
                        got[b][:, way, j * width:(j + 1) * width], None, table,
                        bass.IndirectOffsetOnAxis(ap=row_c[b][:, way, j:j + 1], axis=0),
                        bounds_check=N - 1, oob_is_err=False).then_inc(s, 16)

            def scatter(b, table, data, width, s, bound):
                for j in range(C):
                    pool.indirect_dma_start(
                        table, bass.IndirectOffsetOnAxis(ap=row_c[b][:, 1, j:j + 1], axis=0),
                        data[:, j * width:(j + 1) * width], None,
                        bounds_check=bound, oob_is_err=False).then_inc(s, 16)

            def sort(k, W):
                for n in range(2):
                    with pool.Fori(0, TURNS) as i:
                        for b in range(2):
                            take(pool, rows_ready[b])
                            take(pool, pay_ready[b])
                            scatter(b, (mid_table, edge_table)[n][k],
                                    put[b][:, :], W,
                                    sort_scatter[2 * k + n][b], EP - 1)
                    for b in range(2):
                        pool.wait_ge(sort_scatter[2 * k + n][b], PRIME + 16 * C * TURNS)
                    pool.sem_inc(pass_written, 1)

            sort(0, WS)
            with pool.If(dst_unsorted(pool)):
                sort(1, WD)

            for layer, (table, width, ways, target, wide) in enumerate((
                    (x, F, 2, x1_table, F), (x1_table, F, 1, x2_table, RW),
                    (x2_table, RW, 2, x3_table, F), (x3_table, F, 1, out, F))):
                name = f"l{layer}"
                with pool.Fori(0, TURNS) as i:
                    for b in range(2):
                        take(pool, rows_ready[b])
                        for way in range(ways):
                            gather(b, way, table, width, gathers[name][b])
                if layer == 0:
                    pool.wait_ge(tables_ready, 1)
                if layer == 2:
                    pool.wait_ge(nodes_done, 1)
                with pool.Fori(0, TURNS) as i:
                    for b in range(2):
                        take(pool, put_ready[b])
                        scatter(b, target, put[b][:, :], wide, scatters[name][b], N - 1)
                if layer == 1:
                    pool.wait_ge(fix_ready, 1)
                    pool.indirect_dma_start(target, bass.IndirectOffsetOnAxis(ap=fix_row[:, 0:1], axis=0), fix[:, :],
                                            None, bounds_check=N - 1, oob_is_err=False).then_inc(fix_written, 16)
                    pool.wait_ge(fix_written, 16)
                for b in range(2):
                    pool.wait_ge(scatters[name][b], PRIME + 16 * C * TURNS)
                pool.sem_inc(layer_done, 1)

        @block.sync
        def _(sp):
            sp.dma_start(key_i[:, :], src.rearrange("(p t) -> p t", t=T)).then_inc(edges_in, 16)
            sp.dma_start(ew_sb[:, :], ew.rearrange("(p t) -> p t", t=T)).then_inc(edges_in, 16)
            sp.dma_start(src_row[0][:, :], dst.rearrange("(p t) -> p t", t=T)).then_inc(edges_in, 16)
            sp.wait_ge(staging_set, 1)
            sp.dma_start(dst_prev[1:P, :], dst.rearrange("(p t) -> p t", t=T)[0:P - 1, T - 1:T],
                         allow_slow_non_contiguous=True).then_inc(edges_in, 16)
            sp.dma_start(w_all.rearrange("p t f -> p (t f)"),
                         w.rearrange("h f o -> (h f o)").rearrange("(a n) -> a n", a=1)
                         .to_broadcast([P, H * F * F])).then_inc(consts_load, 16)
            sp.dma_start(fcw_sb[:, :], fc_w.to_broadcast([P, 2 * F])).then_inc(consts_load, 16)
            sp.dma_start(fcb_sb[:, :], fc_b.rearrange("(a n) -> a n", a=1).to_broadcast([P, 1])).then_inc(consts_load, 16)
            sp.dma_start(bias_sb[:, :], bias.rearrange("(a n) -> a n", a=1).to_broadcast([P, F])).then_inc(consts_load, 16)
            sp.dma_start(w_stack[:, :], w.rearrange("h f o -> (h f) o")).then_inc(consts_load, 16)
            sp.dma_start(W1_sb[0:CAT - 1, :], W1).then_inc(consts_load, 16)
            sp.dma_start(W1_sb[CAT - 1:CAT, :], b1.rearrange("(a n) -> a n", a=1)).then_inc(consts_load, 16)
            sp.dma_start(W2_sb[0:MID, :], W2).then_inc(consts_load, 16)
            sp.dma_start(W2_sb[MID:MID + 1, :], b2.rearrange("(a n) -> a n", a=1)).then_inc(consts_load, 16)

            xv = x.rearrange("(p r) f -> p r f", p=P)
            x1v = x1_table.rearrange("(p r) f -> p r f", p=P)
            x2v = x2_table.rearrange("(p r) f -> p r f", p=P)
            sp.wait_ge(staging_set, 2)
            for b in range(2):
                sp.sem_inc(init_out[b], 32)
            with sp.Fori(0, TURNS) as i:
                for b in range(2):
                    c = i * 2 + b
                    take(sp, init_out[b], 32)
                    sp.dma_start(node_out[b][:, :, :], xv[:, bass.ts(c, NC), :]).then_inc(init_in[b], 16)
                    take(sp, init_padded[b])
                    sp.dma_start(x1v[:, bass.ts(c, NC), :], node_out[b][:, :, :]).then_inc(init_out[b], 16)
                    sp.dma_start(x2v[:, bass.ts(c, NC), :], node_in[b][:, :, :]).then_inc(init_out[b], 16)
            for b in range(2):
                take(sp, init_out[b], 32)
            sp.sem_inc(tables_ready, 1)

            def reload(k):
                for n in range(2):
                    sp.wait_ge(pass_written, 2 * k + n + 1)
                    sp.dma_start(PAY[k].rearrange("p t w -> p (t w)"),
                                 (mid_table, edge_table)[n][k].rearrange("(p t) w -> p (t w)", t=T))\
                        .then_inc(pass_loaded, 16)

            def load_neighbours(k):
                tv = edge_table[k].rearrange("(p t) w -> p t w", t=T)
                sp.dma_start(edge_prev[1:P, :], tv[0:P - 1, T - 1, k:k + 1],
                             allow_slow_non_contiguous=True).then_inc(edges_loaded, 16)
                sp.dma_start(edge_next[0:P - 1, :], tv[1:P, 0, k:k + 1],
                             allow_slow_non_contiguous=True).then_inc(edges_loaded, 16)

            reload(0)
            load_neighbours(0)
            sp.wait_ge(pay_free, 1)
            sp.dma_start(key_i[:, :], dst.rearrange("(p t) -> p t", t=T)).then_inc(edges_in, 16)
            sp.dma_start(src_row[1][:, :], src.rearrange("(p t) -> p t", t=T)).then_inc(edges_in, 16)
            sp.dma_start(scan_in, attr.rearrange("(p t) a -> p (t a)", t=T)).then_inc(edges_in, 16)
            with sp.If(dst_unsorted(sp)):
                reload(1)
            with sp.Else():
                sp.wait_ge(natural_ready, 1)
                sp.dma_start(edge_table[1].rearrange("(p t) w -> p (t w)", t=T),
                             PAY[1].rearrange("p t w -> p (t w)")).then_inc(natural_stored, 16)
                sp.wait_ge(natural_stored, 16)
            load_neighbours(1)

            h1v = h1_table.rearrange("p (c n) -> p c n", c=CHUNKS)
            with sp.Fori(0, TURNS) as i:
                for b in range(2):
                    take(sp, h1_ready[b])
                    sp.dma_start(h1v[:, i * 2 + b, :], put[b][:, 0:C * F]).then_inc(h1_stored[b], 16)
            for b in range(2):
                take(sp, h1_used[b], 1)
            with sp.Fori(0, TURNS) as i:
                for b in range(2):
                    take(sp, h1_used[b])
                    sp.dma_start(got[b][:, 0, 0:C * F], h1v[:, i * 2 + b, :]).then_inc(h1_loaded[b], 16)

            av = edge_table[1].rearrange("(p t) w -> p t w", t=T)
            sp.wait_ge(layer_done, 2)
            with sp.Fori(0, TURNS) as i:
                for b in range(2):
                    c = i * 2 + b
                    take(sp, attr_used[b])
                    sp.dma_start(attr_c[b][:, :, :], av[:, bass.ts(c, C), :]).then_inc(attr_loaded[b], 16)
                    take(sp, node_used[b])
                    sp.dma_start(node_in[b][:, :, :], x2v[:, bass.ts(c, NC), :]).then_inc(node_loaded[b], 16)
            sp.wait_ge(layer_done, 4)

        @block.scalar
        def _(act):
            act.wait_ge(staging_set, 2)
            def sort(k, W):
                for n in range(2):
                    take(act, pay_made)
                    with act.Fori(0, TURNS) as i:
                        for b in range(2):
                            landed(act, "act", sort_scatter[2 * k + n][b], i * (16 * C) + PRIME)
                            pc = put[b][:, 0:C * W].rearrange("p (c w) -> p c w", w=W)
                            nc.scalar.activation(pc, PAY[k][:, bass.ts(i * 2 + b, C), :], ACT.Copy).then_inc(pay_ready[b], 1)
                            if k == 0 and n == 0:
                                take(act, init_in[b], 16)
                                nc.scalar.activation(node_in[b][:, :, 0:F], node_out[b][:, :, :], ACT.Copy)\
                                    .then_inc(init_padded[b], 1)

            sort(0, WS)
            act.wait_ge(edges_in, 16 * 7)
            nc.scalar.activation(PAY[1][:, :, 2:WD], scan_in.rearrange("p (t a) -> p t a", a=A),
                                 ACT.Copy).then_inc(attr_copied, 1)
            with act.If(dst_unsorted(act)):
                sort(1, WD)

            def root(n, m=1):
                for _ in range(m):
                    take(act, var_ready)
                    nc.scalar.activation(std[:, 0:n], var[:, 0:n], ACT.Sqrt).then_inc(std_ready, 1)

            with act.Fori(0, TURNS) as i:
                root(C, 4)
            with act.Fori(0, TURNS) as i:
                root(C, 2)
            with act.Fori(0, TURNS) as i:
                root(C, 2)
            take(act, e_ready)
            nc.scalar.activation(a_dst[:, :, :], a_dst[:, :, :], ACT.Exp).then_inc(p_ready, 1)
            act.sem_inc(q_free, 1)
            act.sem_inc(q_last, 1)
            with act.Fori(0, TURNS) as i:
                for b in range(2):
                    for g, (j0, j1) in enumerate(GROUPS):
                        take(act, turned)
                        if g == 3:
                            act.sem_inc(q_used, 1)
                        take(act, q_last if g == 1 else q_free)
                        nc.scalar.activation(qT[g % 2][:, 0:(j1 - j0) * P], turn_ps[g % 2][:, 0:(j1 - j0) * P],
                                             ACT.Copy).then_inc(copied, 1)
            x3v = x3_table.rearrange("(p r) f -> p r f", p=P)
            ov = out.rearrange("(p r) f -> p r f", p=P)
            with act.Fori(0, TURNS) as i:
                for b in range(2):
                    root(C)
                    root(C)
                    root(C)
                    for g, (j0, j1) in enumerate(GROUPS):
                        n = (j1 - j0) * P
                        take(act, turned)
                        nc.scalar.activation(catT[0:CAT, 0:n], turn_ps[g % 2][0:CAT, 0:n], ACT.Copy).then_inc(copied, 1)
                        take(act, hid_ready)
                        nc.scalar.activation(hid[:, 0:n], hid_ps[0:MID, 0:n], ACT.Copy).then_inc(hid_copied, 1)
                    root(NC)
                    c = i * 2 + b
                    take(act, node_ready[b])
                    act.dma_start(x3v[:, bass.ts(c, NC), :], node_out[b][:, :, :]).then_inc(node_stored[b], 16)
                    act.dma_start(ov[:, bass.ts(c, NC), :], node_out[b][:, :, :]).then_inc(node_stored[b], 16)
            for b in range(2):
                take(act, node_stored[b], 32)
            act.sem_inc(nodes_done, 1)
            with act.Fori(0, TURNS) as i:
                root(C, 2)
            with act.Fori(0, TURNS) as i:
                root(C, 2)
            with act.Fori(0, TURNS) as i:
                root(C, 2)

        @block.tensor
        def _(pe):
            pe.wait_ge(consts_iota, 5)
            pe.wait_ge(consts_dve, 1)
            pe.wait_ge(consts_load, 16 * 9)

            def turn_ends():
                take(pe, ends_ready)
                nc.tensor.transpose(carry_ps[0:F, 0:P], ends[:, 0, :], ident[:, :])
                nc.tensor.transpose(carry_ps[0:F, P:2 * P], ends[:, 1, :], ident[:, :]).then_inc(ends_turned, 1)
                take(pe, carry_ready)
                nc.tensor.transpose(carry_ps[:, 256:256 + F], carryT[:, 0:P], ident[0:F, 0:F]).then_inc(carry_turned, 1)

            take(pe, disorder_ready)
            nc.tensor.matmul(carry_ps[0:1, 0:1], disorder[:, :], onesT[:, 0:1], start=True, stop=True)\
                .then_inc(disorder_sum, 1)

            def sort():
                for n, R in enumerate((LOW, HIGH)):
                    if n == 0:
                        take(pe, hist_hot)
                        nc.tensor.matmul(hist_ps[:, 0:R], ones16[:, :], onehot[3][:, 0:R], start=True, stop=True)\
                            .then_inc(hist_free, 4)
                        with pe.Fori(0, TURNS) as i:
                            for j in range(2 * C):
                                pe.wait_ge(hist_hot, j + 1)
                                nc.tensor.matmul(hist_ps[:, 0:R], ones16[:, :], onehot[j % 4][:, 0:R],
                                                 start=False, stop=True, skip_group_check=True).then_inc(hist_free, 1)
                            pe.sem_inc(hist_hot, -2 * C)
                    take(pe, base_ready)
                    if n == 0:
                        nc.tensor.matmul(hist_ps[:, 0:HIGH], ones16[:, :], high_hot[1][:, 0:HIGH], start=True,
                                         stop=True).then_inc(high_free, 2)
                    for q in range(2):
                        nc.tensor.matmul(count_ps[q][:, 0:R], first_row[:, :], base[:, 0:R], start=True, stop=True,
                                         skip_group_check=True)
                    with pe.Fori(0, TURNS) as i:
                        for j in range(2 * C):
                            pe.wait_ge(rank_hot, j + 1)
                            nc.tensor.matmul(count_ps[j % 2][:, 0:R], before[:, :], onehot[j % 4][:, 0:R],
                                             start=False, stop=True, skip_group_check=True).then_inc(rank_ready, 1)
                            pe.wait_ge(rank_read, j + 1)
                            nc.tensor.matmul(count_ps[1 - j % 2][:, 0:R], rest[:, :], onehot[(j - 1) % 4][:, 0:R],
                                             start=False, stop=True, skip_group_check=True).then_inc(rank_free, 1)
                            nc.tensor.matmul(count_ps[1 - j % 2][:, 0:R], ones16[:, :], onehot[j % 4][:, 0:R],
                                             start=False, stop=True, skip_group_check=True).then_inc(rank_done, 1)
                            if n == 0:
                                pe.wait_ge(high_hot_ready, j + 1)
                                nc.tensor.matmul(hist_ps[:, 0:HIGH], ones16[:, :], high_hot[j % 2][:, 0:HIGH],
                                                 start=False, stop=True, skip_group_check=True).then_inc(high_free, 1)
                        if n == 0:
                            pe.sem_inc(high_hot_ready, -2 * C)
                        pe.sem_inc(rank_hot, -2 * C)
                        pe.sem_inc(rank_read, -2 * C)

            sort()
            turn_ends()
            with pe.If(dst_unsorted(pe)):
                sort()
            turn_ends()
            turn_ends()
            for _ in range(5):
                turn_ends()
            with pe.Fori(0, TURNS) as i:
                for b in range(2):
                    take(pe, q_ready)

                    def turn(g):
                        j0, j1 = GROUPS[g]
                        for j in range(j0, j1):
                            t = nc.tensor.transpose(turn_ps[g % 2][:, (j - j0) * P:(j - j0 + 1) * P],
                                                    prod[:, j, :, :].rearrange("p h f -> p (h f)"), ident[:, :])
                        t.then_inc(turned, 1)

                    turn(0)
                    take(pe, y_used)
                    for g, (j0, j1) in enumerate(GROUPS):
                        if g < 3:
                            turn(g + 1)
                        pe.wait_ge(copied, g + 1)
                        for j in range(j0, j1):
                            t = nc.tensor.matmul(y_banks[b][:, j * F:(j + 1) * F], qT[g % 2][:, (j - j0) * P:(j - j0 + 1) * P],
                                                 w_stack[:, :], start=True, stop=True, skip_group_check=True)
                        t.then_inc(q_free if g < 3 else y_ready, 1)
                    pe.sem_inc(copied, -4)
            turn_ends()
            with pe.Fori(0, TURNS) as i:
                for b in range(2):
                    take(pe, cat_ready)
                    for g, (j0, j1) in enumerate(GROUPS):
                        n = (j1 - j0) * P
                        for j in range(j0, j1):
                            t = nc.tensor.transpose(turn_ps[g % 2][0:CAT, (j - j0) * P:(j - j0 + 1) * P],
                                                    cat[:, j, :], ident[:, :])
                        t.then_inc(turned, 1)
                        take(pe, copied)
                        nc.tensor.matmul(hid_ps[0:MID, 0:n], W1_sb[:, :], catT[0:CAT, 0:n], start=True, stop=True,
                                         skip_group_check=True).then_inc(hid_ready, 1)
                        take(pe, hid_act)
                        if g == 0:
                            take(pe, y_used)
                        for j in range(j0, j1):
                            t = nc.tensor.matmul(y_ps[:, j * F:(j + 1) * F], hidT[:, (j - j0) * P:(j - j0 + 1) * P],
                                                 W2_sb[:, :], start=True, stop=True, skip_group_check=True)
                        t.then_inc(v_ready, 1)
                    pe.wait_ge(v_ready, 4)
                    pe.sem_inc(v_ready, -4)
                    pe.sem_inc(y_ready, 1)
            turn_ends()
            turn_ends()

        @block.vector
        def _(dve):
            v = nc.vector
            chain = [0]

            def link(ins):
                chain[0] += 1
                ins.then_inc(dve_chain, 1)
                dve.wait_ge(dve_chain, chain[0])

            def chain_end():
                if chain[0]:
                    dve.sem_inc(dve_chain, -chain[0])
                chain[0] = 0

            def per_row(a, n, f=F):
                return a.unsqueeze(2).to_broadcast([P, n, f])

            def per_feature(a, n, f=F):
                return a.unsqueeze(1).to_broadcast([P, n, f])

            def layernorm_relu(src_ap, dst_ap, n):
                link(v.tensor_reduce(sums[:, 0:n], src_ap, AX.X, ALU.add))
                link(v.tensor_scalar(sums[:, 0:n], sums[:, 0:n], 1.0 / F, None, ALU.mult))
                link(v.tensor_tensor(cen[:, 0:n, :], src_ap, per_row(sums[:, 0:n], n), ALU.subtract))
                link(v.tensor_tensor(sqr[:, 0:n, :], cen[:, 0:n, :], cen[:, 0:n, :], ALU.mult))
                link(v.tensor_reduce(var[:, 0:n], sqr[:, 0:n, :], AX.X, ALU.add))
                link(v.tensor_scalar(var[:, 0:n], var[:, 0:n], 1.0 / F, 1e-5, ALU.mult, ALU.add))
                root(n)
                link(v.tensor_tensor(cen[:, 0:n, :], cen[:, 0:n, :], per_row(std[:, 0:n], n), ALU.mult))
                link(v.tensor_scalar(dst_ap, cen[:, 0:n, :], 0.0, None, ALU.max))

            def root(n):
                dve.sem_inc(var_ready, 1)
                take(dve, std_ready)
                link(v.reciprocal(std[:, 0:n], std[:, 0:n]))

            link(v.memset(dst_prev[:, :], -1))
            dve.sem_inc(staging_set, 1)
            link(v.memset(onesT[:, :], 1.0))
            for b in range(2):
                link(v.memset(got[b][:, :, :], 0.0))
                link(v.memset(put[b][:, :], 0.0))
                link(v.memset(node_in[b][:, :, :], 0.0))
            link(v.memset(edge_prev[:, :], -1.0))
            link(v.memset(fix[:, :], 0.0))
            link(v.memset(edge_next[:, :], -1.0))
            link(v.memset(ends[:, :, :], 0.0))
            link(v.memset(carryT[:, :], 0.0))
            dve.sem_inc(staging_set, 1)
            dve.wait_ge(consts_load, 16 * 9)
            for side in range(2):
                link(v.tensor_tensor(w_prod, w_all, per_feature(fcw_sb[:, side * F:(side + 1) * F], P), ALU.mult))
                link(v.tensor_reduce(u_heads[:, side, :, :].rearrange("p h f -> p (h f)"), w_prod, AX.X, ALU.add))
            dve.sem_inc(consts_dve, 1)
            dve.wait_ge(consts_iota, 5)
            dve.wait_ge(edges_in, 64)
            link(v.tensor_copy(keyf[:, :], src_row[0][:, :]))
            link(v.tensor_copy(disorder[:, :], dst_prev[:, :]))
            link(v.tensor_tensor(junk[:, 0:1], keyf[:, 0:1], disorder[:, :], ALU.is_lt))
            link(v.tensor_tensor(junk[:, 1:T], keyf[:, 1:T], keyf[:, 0:T - 1], ALU.is_lt))
            link(v.tensor_reduce(disorder[:, :], junk[:, :], AX.X, ALU.add))
            dve.sem_inc(disorder_ready, 1)
            take(dve, disorder_sum)
            link(v.tensor_scalar(junk[0:1, 0:1], carry_ps[0:1, 0:1], 1.0, None, ALU.min))
            link(v.tensor_copy(unsorted[:, :], junk[0:1, 0:1]))
            dve.sem_inc(unsorted_ready, 1)
            chain_end()

            def carries(op, values, factors, f, back=False):
                neutral = 0.0 if op == ALU.add else -BIG
                link(v.tensor_copy(ends[:, 0, 0:f], values))
                link(v.tensor_copy(ends[:, 1, 0:f], factors.to_broadcast([P, f])))
                dve.sem_inc(ends_ready, 1)
                take(dve, ends_turned)
                link(v.tensor_copy(endsT[:, :, :], carry_ps[0:F, 0:2 * P].rearrange("f (a p) -> f a p", a=2)))
                if op == ALU.max:
                    link(v.tensor_scalar(endsT[:, 1, :], endsT[:, 1, :], -1.0, BIG, ALU.add, ALU.mult))
                op0 = ALU.mult if op == ALU.add else ALU.add
                link(v.memset(carryT[:, :], neutral))
                if back:
                    link(v.tensor_tensor_scan(carryT[:, P - 2::-1], endsT[:, 1, P - 1:0:-1], endsT[:, 0, P - 1:0:-1],
                                              neutral, op0, op))
                else:
                    link(v.tensor_tensor_scan(carryT[:, 1:P + 1], endsT[:, 1, :], endsT[:, 0, :], neutral, op0, op))
                dve.sem_inc(carry_ready, 1)
                take(dve, carry_turned)
                link(v.tensor_copy(carry[:, :], carry_ps[:, 256:256 + F]))

            def first_places(R, q_hist):
                link(v.tensor_copy(hist_sb[:, 0:R], q_hist[:, 0:R]))
                link(v.tensor_tensor_scan(base[:, 0:R], onesT[:, 0:R], hist_sb[:, 0:R], 0.0, ALU.mult, ALU.add))
                link(v.tensor_tensor(base[:, 0:R], base[:, 0:R], hist_sb[:, 0:R], ALU.subtract))

            def sort(k):
                for n, R in enumerate((LOW, HIGH)):
                    if n == 0:
                        dve.sem_inc(pay_made, 1)
                        link(v.tensor_scalar(dst_row[k][:, :], key_i[:, :], 8, None, ALU.logical_shift_right))
                        link(v.tensor_copy(high[:, :], dst_row[k][:, :]))
                        link(v.tensor_scalar(key_i[:, :], key_i[:, :], LOW - 1, None, ALU.bitwise_and))
                        link(v.tensor_copy(digit[:, :], key_i[:, :]))
                        link(v.memset(onehot[3][:, :], 0.0))
                        dve.sem_inc(hist_hot, 1)
                        chain_end()
                        with dve.Fori(0, TURNS) as i:
                            for b in range(2):
                                link(v.tensor_scalar(digit_c[:, :], digit[:, bass.ts(i * 2 + b, C)], 1.0, None, ALU.mult))
                                for j in range(C):
                                    g = b * C + j
                                    dve.wait_ge(hist_free, g + 1)
                                    v.tensor_scalar(onehot[g % 4][:, 0:R], digits_row[:, 0:R], digit_c[:, j:j + 1], None,
                                                    ALU.is_equal).then_inc(hist_hot, 1)
                                v.drain()
                            dve.sem_inc(hist_free, -2 * C)
                            chain_end()
                        take(dve, hist_free, 4)
                        first_places(R, hist_ps)
                        link(v.memset(high_hot[1][:, :], 0.0))
                    else:
                        take(dve, high_free, 2)
                        first_places(R, hist_ps)
                        dve.wait_ge(pass_loaded, 16 * (1 + 2 * k))
                        dve.sem_inc(pay_made, 1)
                        link(v.tensor_copy(key_i[:, :], PAY[k][:, :, k]))
                        link(v.tensor_scalar(key_i[:, :], key_i[:, :], 8, None, ALU.logical_shift_right))
                        link(v.tensor_copy(digit[:, :], key_i[:, :]))
                    link(v.memset(onehot[3][:, :], 0.0))
                    dve.sem_inc(base_ready, 1)
                    dve.sem_inc(rank_read, 1)
                    dve.sem_inc(rank_free, 3)
                    chain_end()
                    with dve.Fori(0, TURNS) as i:
                        for b in range(2):
                            link(v.tensor_scalar(digit_c[:, :], digit[:, bass.ts(i * 2 + b, C)], 1.0, None, ALU.mult))
                            if n == 0:
                                link(v.tensor_scalar(high_c[:, :], high[:, bass.ts(i * 2 + b, C)], 1.0, None, ALU.mult))

                            def make_hot(j):
                                g = b * C + j
                                dve.wait_ge(rank_free, g + 1)
                                v.tensor_scalar(onehot[g % 4][:, 0:R], digits_row[:, 0:R], digit_c[:, j:j + 1], None,
                                                ALU.is_equal).then_inc(rank_hot, 1)

                            make_hot(0)
                            for j in range(C):
                                g = b * C + j
                                if j + 1 < C:
                                    make_hot(j + 1)
                                if n == 0:
                                    dve.wait_ge(high_free, g + 1)
                                    v.tensor_scalar(high_hot[g % 2][:, 0:HIGH], digits_row[:, 0:HIGH], high_c[:, j:j + 1],
                                                    None, ALU.is_equal).then_inc(high_hot_ready, 1)
                                dve.wait_ge(rank_ready, g + 1)
                                v.tensor_tensor_reduce((junk, hist_sb)[g % 2][:, 0:R], count_ps[g % 2][:, 0:R],
                                                       onehot[g % 4][:, 0:R],
                                                       1.0, 0.0, ALU.mult, ALU.add, rank_c[:, j:j + 1]).then_inc(rank_read, 1)
                            landed(dve, "dve", sort_scatter[2 * k + n][b], i * (16 * C) + PRIME)
                            v.drain()
                            if n == 0:
                                link(v.tensor_copy(int_c[:, 0, :], rank_c[:, :]))
                                link(v.tensor_scalar(int_c[:, 1, :], int_c[:, 0, :], 7, None, ALU.logical_shift_right))
                                link(v.tensor_scalar(int_c[:, 0, :], int_c[:, 0, :], P - 1, None, ALU.bitwise_and))
                                link(v.tensor_copy(flt_c[:, :, :], int_c[:, :, :]))
                                link(v.scalar_tensor_tensor(out=rank_c[:, :], in0=flt_c[:, 0, :], scalar=float(T),
                                                            in1=flt_c[:, 1, :], op0=ALU.mult, op1=ALU.add))
                            link(v.tensor_copy(row_c[b][:, 1, :], rank_c[:, :]))
                            dve.sem_inc(rows_ready[b], 1)
                        if n == 0:
                            dve.sem_inc(high_free, -2 * C)
                        dve.sem_inc(rank_free, -2 * C)
                        dve.sem_inc(rank_ready, -2 * C)
                        chain_end()
                    take(dve, rank_free, 3)
                    take(dve, rank_done, T)
                    take(dve, rank_read)
                dve.wait_ge(pass_loaded, 16 * (2 + 2 * k))

            def segments(k):
                dve.wait_ge(edges_loaded, 32 * (k + 1))
                S, D = PAY[k][:, :, 0], PAY[k][:, :, 1]
                link(v.tensor_copy(keyf[:, :], PAY[k][:, :, k]))
                if k == 0:
                    link(v.tensor_copy(ew_sb[:, :], PAY[0][:, :, 2]))
                link(v.tensor_scalar(junk[:, :], S, float(N - 1), None, ALU.min))
                link(v.tensor_copy(src_row[k][:, :], junk[:, :]))
                link(v.tensor_scalar(junk[:, :], D, float(N - 1), None, ALU.min))
                link(v.tensor_copy(dst_row[k][:, :], junk[:, :]))
                link(v.tensor_tensor(same[k][:, 1:T], keyf[:, 1:T], keyf[:, 0:T - 1], ALU.is_equal))
                link(v.tensor_tensor(same[k][:, 0:1], keyf[:, 0:1], edge_prev[:, :], ALU.is_equal))
                link(v.tensor_tensor(last[k][:, 0:T - 1], keyf[:, 0:T - 1], keyf[:, 1:T], ALU.not_equal))
                link(v.tensor_tensor(last[k][:, T - 1:T], keyf[:, T - 1:T], edge_next[:, :], ALU.not_equal))
                link(v.tensor_tensor_scan(whole[k][:, :], same[k][:, :], onesT[:, :], 1.0, ALU.mult, ALU.mult))
                link(v.tensor_scalar(junk[:, :], last[k][:, :], -SKIP, SKIP, ALU.mult, ALU.add))
                link(v.tensor_tensor(junk[:, :], junk[:, :], keyf[:, :], ALU.add))
                link(v.tensor_copy(out_row[k][:, :], junk[:, :]))
                if k == 0:
                    link(v.tensor_scalar(more[:, :], last[0][:, :], -1.0, 1.0, ALU.mult, ALU.add))
                    link(v.tensor_tensor_scan(tail[:, ::-1], more[:, ::-1], onesT[:, :], 1.0, ALU.mult, ALU.mult))
                link(v.tensor_tensor_scan(deg[k][:, :], same[k][:, :], onesT[:, :], 0.0, ALU.mult, ALU.add))
                carries(ALU.add, deg[k][:, T - 1:T], whole[k][:, T - 1:T], 1)
                link(v.scalar_tensor_tensor(out=deg[k][:, :], in0=whole[k][:, :], scalar=carry[:, 0:1],
                                            in1=deg[k][:, :], op0=ALU.mult, op1=ALU.add))
                chain_end()

            link(v.tensor_copy(PAY[0][:, :, 0], key_i[:, :]))
            link(v.tensor_copy(PAY[0][:, :, 1], src_row[0][:, :]))
            link(v.tensor_copy(PAY[0][:, :, 2], ew_sb[:, :]))
            sort(0)
            segments(0)
            dve.sem_inc(pay_free, 1)
            dve.wait_ge(edges_in, 16 * 7)
            link(v.tensor_copy(PAY[1][:, :, 0], src_row[1][:, :]))
            link(v.tensor_copy(PAY[1][:, :, 1], key_i[:, :]))
            dve.wait_ge(attr_copied, 1)
            dve.sem_inc(natural_ready, 1)
            chain_end()
            with dve.If(dst_unsorted(dve)):
                sort(1)
            segments(1)

            def scan_chunk(c, data, factors, neutral_op, op):
                for f in range(F):
                    ins = v.tensor_tensor_scan(SEG[:, bass.ds(c * C + 1, C), f], factors, data[:, :, f],
                                               SEG[:, bass.ds(c * C, 1), f], neutral_op, op)
                link(ins)

            def give_rows(b, c, sides):
                for way, rows in sides:
                    link(v.tensor_copy(row_c[b][:, way, :], rows[:, bass.ts(c, C)]))
                dve.sem_inc(rows_ready[b], 1)

            def passed(name, b, i, ways):
                landed(dve, "dve", gathers[name][b], (i + 1) * (16 * C * ways))

            def rows_of(b, way, width=F):
                return got[b][:, way, 0:C * width].rearrange("p (c w) -> p c w", w=width)

            def heads_dot(side, h_ap, dst_ap):
                link(v.tensor_tensor(prod[:, :, :, :],
                                     h_ap.unsqueeze(2).to_broadcast([P, C, H, F]),
                                     u_heads[:, side, :, :].unsqueeze(1).to_broadcast([P, C, H, F]), ALU.mult))
                link(v.tensor_reduce(dst_ap, prod[:, :, :, :].rearrange("p c h f -> p h c f"), AX.X, ALU.add))

            def gather_loop(name, sides, body, between):
                ways = len(sides)
                for b in range(2):
                    for way, rows in sides:
                        link(v.tensor_copy(row_c[b][:, way, :], rows[:, b * C:(b + 1) * C]))
                    dve.sem_inc(rows_ready[b], 1)
                chain_end()
                with dve.Fori(0, TURNS - 1) as i:
                    for b in range(2):
                        passed(name, b, i, ways)
                        body(b, i)
                        give_rows(b, i * 2 + b + 2, sides)
                    chain_end()
                for b in range(2):
                    passed(name, b, TURNS - 1, ways)
                    body(b, TURNS - 1)
                chain_end()

            def scatter_loop(name, k, body):
                with dve.Fori(0, TURNS) as i:
                    for b in range(2):
                        landed(dve, "dve", scatters[name][b], i * (16 * C) + PRIME)
                        link(v.tensor_copy(row_c[b][:, 1, :], out_row[k][:, bass.ts(i * 2 + b, C)]))
                        body(b, i * 2 + b)
                        dve.sem_inc(put_ready[b], 1)
                    chain_end()

            def neutral_column(value):
                link(v.memset(SEG[:, 0, :], value))

            def with_carry(c, k, dst_ap):
                link(v.tensor_tensor(dst_ap, per_row(whole[k][:, bass.ts(c, C)], C), per_feature(carry[:, :], C), ALU.mult))
                link(v.tensor_tensor(dst_ap, dst_ap, SEG[:, bass.ds(c * C + 1, C), :], ALU.add))

            def l0_gathered(b, i):
                c = i * 2 + b
                layernorm_relu(rows_of(b, 0), ha[:, :, :], C)
                layernorm_relu(rows_of(b, 1), hb[:, :, :], C)
                link(v.tensor_tensor(X[:, bass.ts(c, C), :], rows_of(b, 1), per_row(onesT[:, 0:C], C), ALU.mult))
                link(v.tensor_tensor(ha[:, :, :], ha[:, :, :], hb[:, :, :], ALU.subtract))
                link(v.tensor_tensor(ha[:, :, :], ha[:, :, :], per_row(ew_sb[:, bass.ts(c, C)], C), ALU.mult))
                scan_chunk(c, ha, same[0][:, bass.ts(c, C)], ALU.mult, ALU.add)

            neutral_column(0.0)
            gather_loop("l0", [(0, dst_row[0]), (1, src_row[0])], l0_gathered, None)
            carries(ALU.add, SEG[:, T, :], whole[0][:, T - 1:T], F)
            chain_end()

            def l0_put(b, c):
                rows = put[b][:, 0:C * F].rearrange("p (c w) -> p c w", w=F)
                with_carry(c, 0, ha[:, :, :])
                link(v.tensor_tensor(rows, ha[:, :, :], X[:, bass.ts(c, C), :], ALU.add))
                link(v.tensor_tensor(X[:, bass.ts(c, C), :], rows, per_row(onesT[:, 0:C], C), ALU.mult))
                layernorm_relu(rows, hb[:, :, :], C)
                heads_dot(0, hb[:, :, :], a_src[:, :, bass.ts(c, C)])

            dve.wait_ge(tables_ready, 1)
            scatter_loop("l0", 0, l0_put)

            def per_head(a):
                return a.unsqueeze(1).to_broadcast([P, H, T])

            def spread_back(a, tmp, dst_ap):
                link(v.tensor_tensor(tmp[:, :, :], a[:, :, :], per_head(last[0][:, :]), ALU.mult))
                for h in range(H):
                    ins = v.tensor_tensor_scan(dst_ap[:, h, ::-1], more[:, ::-1], tmp[:, h, ::-1], 0.0, ALU.mult, ALU.add)
                link(ins)
                carries(ALU.add, dst_ap[:, :, 0], tail[:, 0:1], H, back=True)
                link(v.tensor_tensor(tmp[:, :, :], per_head(tail[:, :]),
                                     carry[:, 0:H].unsqueeze(2).to_broadcast([P, H, T]), ALU.mult))
                link(v.tensor_tensor(dst_ap[:, :, :], dst_ap[:, :, :], tmp[:, :, :], ALU.add))

            spread_back(a_src, scan_a, scan_b)
            dve.wait_ge(layer_done, 1)
            chain_end()

            def l1_gathered(b, i):
                c = i * 2 + b
                rows = put[b][:, 0:C * F].rearrange("p (c w) -> p c w", w=F)
                take(dve, h1_stored[b], 16)
                layernorm_relu(rows_of(b, 0), rows, C)
                dve.sem_inc(h1_ready[b], 1)
                heads_dot(1, rows, a_dst[:, :, bass.ts(c, C)])

            for b in range(2):
                dve.sem_inc(h1_stored[b], 16)
            gather_loop("l1", [(0, dst_row[0])], l1_gathered, None)
            for b in range(2):
                take(dve, h1_stored[b], 16)
                dve.sem_inc(h1_used[b], 1)
                dve.sem_inc(h1_used[b], 1)
            link(v.tensor_tensor(scan_a[:, :, :], a_dst[:, :, :], scan_b[:, :, :], ALU.add))
            link(v.tensor_scalar(scan_a[:, :, :], scan_a[:, :, :], fcb_sb[:, 0:1], None, ALU.add))
            link(v.scalar_tensor_tensor(out=a_dst[:, :, :], in0=scan_a[:, :, :], scalar=0.2, in1=scan_a[:, :, :],
                                        op0=ALU.mult, op1=ALU.max))
            link(v.tensor_scalar(junk[:, :], same[0][:, :], -1.0, BIG, ALU.add, ALU.mult))
            for h in range(H):
                ins = v.tensor_tensor_scan(scan_a[:, h, :], junk[:, :], a_dst[:, h, :], -BIG, ALU.add, ALU.max)
            link(ins)
            carries(ALU.max, scan_a[:, :, T - 1], whole[0][:, T - 1:T], H)
            link(v.tensor_scalar(junk[:, :], whole[0][:, :], -1.0, BIG, ALU.add, ALU.mult))
            for h in range(H):
                ins = v.scalar_tensor_tensor(out=scan_a[:, h, :], in0=junk[:, :], scalar=carry[:, h:h + 1],
                                             in1=scan_a[:, h, :], op0=ALU.add, op1=ALU.max)
            link(ins)
            spread_back(scan_a, scan_b, a_src)
            link(v.tensor_tensor(a_dst[:, :, :], a_dst[:, :, :], a_src[:, :, :], ALU.subtract))
            dve.sem_inc(e_ready, 1)
            take(dve, p_ready)
            for h in range(H):
                ins = v.tensor_tensor_scan(scan_a[:, h, :], same[0][:, :], a_dst[:, h, :], 0.0, ALU.mult, ALU.add)
            link(ins)
            carries(ALU.add, scan_a[:, :, T - 1], whole[0][:, T - 1:T], H)
            for h in range(H):
                ins = v.scalar_tensor_tensor(out=scan_a[:, h, :], in0=whole[0][:, :], scalar=carry[:, h:h + 1],
                                             in1=scan_a[:, h, :], op0=ALU.mult, op1=ALU.add)
            link(ins)
            spread_back(scan_a, scan_b, a_src)
            link(v.reciprocal(a_src[:, :, :], a_src[:, :, :]))
            link(v.tensor_tensor(a_dst[:, :, :], a_dst[:, :, :], a_src[:, :, :], ALU.mult))
            link(v.tensor_scalar(a_dst[:, :, :], a_dst[:, :, :], 1.0 / H, None, ALU.mult))
            neutral_column(0.0)
            link(v.tensor_tensor(digit[:, :], last[0][:, :], whole[0][:, :], ALU.mult))
            link(v.tensor_copy(junk[:, :], out_row[0][:, :]))
            link(v.tensor_tensor(hist_sb[:, 0:T], junk[:, :], digit[:, :], ALU.mult))
            link(v.tensor_reduce(sums[:, 0:1], hist_sb[:, 0:T], AX.X, ALU.add))
            link(v.tensor_reduce(sums[:, 1:2], digit[:, :], AX.X, ALU.add))
            link(v.tensor_scalar(sums[:, 1:2], sums[:, 1:2], -SKIP, SKIP, ALU.mult, ALU.add))
            link(v.tensor_tensor(sums[:, 0:1], sums[:, 0:1], sums[:, 1:2], ALU.add))
            link(v.tensor_copy(fix_row[:, :], sums[:, 0:1]))
            link(v.scalar_tensor_tensor(out=junk[:, :], in0=whole[0][:, :], scalar=SKIP, in1=junk[:, :],
                                        op0=ALU.mult, op1=ALU.add))
            link(v.tensor_copy(key_i[:, :], junk[:, :]))

            def weigh(b, c):
                take(dve, h1_loaded[b], 16)
                for h in range(H):
                    ins = v.tensor_tensor(prod[:, :, h, :], rows_of(b, 0),
                                          per_row(a_dst[:, h, bass.ts(c, C)], C), ALU.mult)
                link(ins)
                dve.sem_inc(h1_used[b], 1)
                dve.sem_inc(q_ready, 1)

            def l1_put(b, c, i):
                take(dve, y_ready)
                dve.sem_inc(q_last, 1)
                scan_chunk(c, y_banks[b][:, 0:C * F].rearrange("p (c w) -> p c w", w=F),
                           same[0][:, bass.ts(c, C)], ALU.mult, ALU.add)
                dve.sem_inc(y_used, 1)
                landed(dve, "dve", scatters["l1"][b], i * (16 * C) + PRIME)
                link(v.tensor_copy(row_c[b][:, 1, :], key_i[:, bass.ts(c, C)]))
                rows = put[b][:, :].rearrange("p (c w) -> p c w", w=RW)
                link(v.tensor_tensor(rows[:, :, 0:F], SEG[:, bass.ds(c * C + 1, C), :], X[:, bass.ts(c, C), :], ALU.add))
                link(v.tensor_scalar(rows[:, :, F], deg[0][:, bass.ts(c, C)], 1.0, None, ALU.mult))
                dve.sem_inc(put_ready[b], 1)
                marked = cen_flat[:, 0:C * RW].rearrange("p (c w) -> p c w", w=RW)
                link(v.tensor_tensor(marked, rows, per_row(digit[:, bass.ts(c, C)], C, RW), ALU.mult))
                link(v.tensor_reduce(fix_c[:, :], marked.rearrange("p c w -> p w c"), AX.X, ALU.add))
                link(v.tensor_tensor(fix[:, :], fix[:, :], fix_c[:, :], ALU.add))

            dve.sem_inc(y_used, 2)
            weigh(0, 0)
            chain_end()
            with dve.Fori(0, TURNS - 1) as i:
                for b in range(2):
                    take(dve, q_used)
                    weigh(1 - b, i * 2 + b + 1)
                    l1_put(b, i * 2 + b, i)
                chain_end()
            for b in range(2):
                take(dve, q_used)
                if b == 0:
                    weigh(1, CHUNKS - 1)
                l1_put(b, CHUNKS - 2 + b, TURNS - 1)
            take(dve, y_used)
            carries(ALU.add, SEG[:, T, :], whole[0][:, T - 1:T], F)
            link(v.tensor_tensor(fix[:, 0:F], fix[:, 0:F], carry[:, :], ALU.add))
            dve.sem_inc(fix_ready, 1)
            chain_end()
            neutral_column(-BIG)
            dve.wait_ge(layer_done, 2)
            link(v.memset(hidT, 1.0))
            link(v.memset(cat, 1.0))
            for b in range(2):
                dve.sem_inc(attr_used[b], 1)
                dve.sem_inc(node_stored[b], 32)
                dve.sem_inc(node_used[b], 1)
            link(v.tensor_scalar(digit[:, :], same[1][:, :], -1.0, BIG, ALU.add, ALU.mult))
            link(v.tensor_scalar(base[:, :], whole[1][:, :], -1.0, BIG, ALU.add, ALU.mult))
            chain_end()

            def l2_gathered(b, i):
                c = i * 2 + b
                s_rows, d_rows = rows_of(b, 0, RW), rows_of(b, 1, RW)
                link(v.tensor_tensor(ha[:, :, :], s_rows[:, :, 0:F], per_feature(bias_sb[:, :], C), ALU.add))
                layernorm_relu(ha[:, :, :], cat[:, :, 0:F], C)
                link(v.tensor_tensor(hb[:, :, :], d_rows[:, :, 0:F], per_feature(bias_sb[:, :], C), ALU.add))
                layernorm_relu(hb[:, :, :], cat[:, :, F:2 * F], C)
                link(v.tensor_tensor(X[:, bass.ts(c, C), :], hb[:, :, :], per_row(onesT[:, 0:C], C), ALU.mult))
                link(v.tensor_scalar(var[:, 0:C], s_rows[:, :, F], 1.0, None, ALU.max))
                root(C)
                link(v.tensor_tensor(more[:, bass.ts(c, C)], std[:, 0:C], onesT[:, 0:C], ALU.mult))
                take(dve, attr_loaded[b], 16)
                link(v.tensor_copy(cat[:, :, 2 * F:2 * F + A], attr_c[b][:, :, 2:WD]))
                dve.sem_inc(attr_used[b], 1)
                dve.sem_inc(cat_ready, 1)
                for g, (j0, j1) in enumerate(GROUPS):
                    n = (j1 - j0) * P
                    take(dve, hid_copied)
                    link(v.scalar_tensor_tensor(out=hidT[0:MID, 0:n], in0=hid[:, 0:n], scalar=0.01,
                                                in1=hid[:, 0:n], op0=ALU.mult, op1=ALU.max))
                    dve.sem_inc(hid_act, 1)
                take(dve, y_ready)
                link(v.tensor_copy(ha[:, :, :], y_ps[:, 0:C * F].rearrange("p (c w) -> p c w", w=F)))
                dve.sem_inc(y_used, 1)
                link(v.scalar_tensor_tensor(out=hb[:, :, :], in0=ha[:, :, :], scalar=0.01,
                                            in1=ha[:, :, :], op0=ALU.mult, op1=ALU.max))
                scan_chunk(c, hb, digit[:, bass.ts(c, C)], ALU.add, ALU.max)
                take(dve, node_loaded[b], 16)
                take(dve, node_stored[b], 32)
                link(v.tensor_tensor(node_out[b][:, :, :], node_in[b][:, :, 0:F], per_feature(bias_sb[:, :], NC), ALU.add))
                dve.sem_inc(node_used[b], 1)
                layernorm_relu(node_out[b][:, :, :], sqr[:, :, :], NC)
                link(v.tensor_tensor(node_out[b][:, :, :], node_out[b][:, :, :], sqr[:, :, :], ALU.add))
                dve.sem_inc(node_ready[b], 1)

            gather_loop("l2", [(0, src_row[1]), (1, dst_row[1])], l2_gathered, None)
            carries(ALU.max, SEG[:, T, :], whole[1][:, T - 1:T], F)
            chain_end()

            def l2_put(b, c):
                rows = put[b][:, 0:C * F].rearrange("p (c w) -> p c w", w=F)
                x2 = X[:, bass.ts(c, C), :]
                link(v.tensor_tensor(ha[:, :, :], x2, per_row(onesT[:, 0:C], C), ALU.mult))
                layernorm_relu(ha[:, :, :], hb[:, :, :], C)
                link(v.tensor_tensor(rows, per_row(base[:, bass.ts(c, C)], C), per_feature(carry[:, :], C), ALU.add))
                link(v.tensor_tensor(rows, rows, SEG[:, bass.ds(c * C + 1, C), :], ALU.max))
                link(v.tensor_tensor(rows, rows, hb[:, :, :], ALU.max))
                link(v.tensor_tensor(rows, rows, ha[:, :, :], ALU.add))
                link(v.tensor_tensor(x2, rows, per_row(onesT[:, 0:C], C), ALU.mult))

            scatter_loop("l2", 1, l2_put)

            neutral_column(0.0)
            link(v.tensor_scalar(deg[1][:, :], deg[1][:, :], 1.0, None, ALU.max))
            dve.wait_ge(layer_done, 3)
            chain_end()

            def l3_gathered(b, i):
                c = i * 2 + b
                layernorm_relu(rows_of(b, 0), ha[:, :, :], C)
                link(v.tensor_tensor(ha[:, :, :], ha[:, :, :], per_row(more[:, bass.ts(c, C)], C), ALU.mult))
                scan_chunk(c, ha, same[1][:, bass.ts(c, C)], ALU.mult, ALU.add)

            gather_loop("l3", [(0, src_row[1])], l3_gathered, None)
            carries(ALU.add, SEG[:, T, :], whole[1][:, T - 1:T], F)
            chain_end()

            def l3_put(b, c):
                rows = put[b][:, 0:C * F].rearrange("p (c w) -> p c w", w=F)
                with_carry(c, 1, ha[:, :, :])
                link(v.tensor_scalar(var[:, 0:C], deg[1][:, bass.ts(c, C)], 1.0, None, ALU.mult))
                root(C)
                link(v.tensor_tensor(ha[:, :, :], ha[:, :, :], per_row(std[:, 0:C], C), ALU.mult))
                link(v.tensor_tensor(rows, ha[:, :, :], X[:, bass.ts(c, C), :], ALU.add))

            scatter_loop("l3", 1, l3_put)
            dve.wait_ge(layer_done, 4)


_INS = ["x", "src", "dst", "edge_attr_16", "edge_weight", "L1_gnn_w", "L1_gnn_fc_w", "L1_gnn_fc_b", "L1_gnn_bias",
        "L2_gnn_W1", "L2_gnn_b1", "L2_gnn_W2", "L2_gnn_b2"]


def kernel(**inputs):
    import concourse.bacc as _bacc
    from concourse.bass_utils import run_bass_kernel_spmd as _run

    def padded(a, rows, fill):
        a = np.asarray(a)
        return np.concatenate([a, np.full((rows - a.shape[0],) + a.shape[1:], fill, a.dtype)])

    given = {n: np.ascontiguousarray(inputs[n]) for n in _INS}
    given["x"] = padded(given["x"], NP, 0)
    given["src"] = padded(given["src"], EP, PADKEY)
    given["dst"] = padded(given["dst"], EP, PADKEY)
    given["edge_attr_16"] = padded(given["edge_attr_16"], EP, 0)
    given["edge_weight"] = padded(given["edge_weight"], EP, 0)
    nc = _bacc.Bacc("TRN2", target_bir_lowering=False, num_devices=1)
    arrays, args = {}, []
    for n in _INS:
        a = given[n]
        arrays[f"in_{n}_dram"] = a
        args.append(nc.dram_tensor(f"in_{n}_dram", a.shape, mybir.dt.from_np(a.dtype), kind="ExternalInput").ap())
    out = nc.dram_tensor("out_0_dram", (NP, F), F32, kind="ExternalOutput").ap()
    build_gnn(nc, *args, out)
    r = _run(nc, [arrays], core_ids=[0])
    return r.results[0]["out_0_dram"][0:N]
```

```python
from contextlib import ExitStack

import numpy as np
import concourse.bass as bass
from concourse import mybir

ALU = mybir.AluOpType
ACT = mybir.ActivationFunctionType
AX = mybir.AxisListType
F32 = mybir.dt.float32
F16 = mybir.dt.float16
I32 = mybir.dt.int32

P = 128
N = 100000
E = 50000
F = 32
H = 4
A = 16
MID = 56
C = 14
T = 392
CHUNKS = T // C
TURNS = CHUNKS // 2
EP = P * T
ROWS = 784
NP = P * ROWS
NC = ROWS // CHUNKS
LOW = 256
HIGH = 391
PADKEY = (HIGH - 1) * LOW + LOW - 1
RW = 36
WS, WD = 3, 2 + A
M2 = 64
CAT = 2 * F + A + 1
BIG = 1.5e38
SKIP = 200000.0
assert T % (2 * C) == 0 and EP >= E and NP >= N and PADKEY >= N and (2 * C) % 4 == 0


def build_gnn(nc, x, src, dst, attr, ew, w, fc_w, fc_b, bias, W1, b1, W2, b2, out):
    mid_table = [nc.dram_tensor(f"mid_table{k}", (EP, W), F32).ap() for k, W in enumerate((WS, WD))]
    attr_table = nc.dram_tensor("attr_table", (EP, A), F32).ap()
    edge_table = [nc.dram_tensor(f"edge_table{k}", (EP, W), F32).ap() for k, W in enumerate((WS, WD))]
    x1_table = nc.dram_tensor("x1_table", (NP, F), F32).ap()
    x2_table = nc.dram_tensor("x2_table", (NP, RW), F32).ap()
    x3_table = nc.dram_tensor("x3_table", (NP, F), F32).ap()
    h1_table = nc.dram_tensor("h1_table", (P, T * F), F32).ap()

    with ExitStack() as ctx:
        def sb(name, shape, dt=F32):
            return ctx.enter_context(nc.sbuf_tensor(name, shape, dt))

        def sem(name):
            return ctx.enter_context(nc.semaphore(name))

        def sems(name, n=2):
            return [sem(f"{name}{i}") for i in range(n)]

        digits_row = sb("digits_row", [P, T], F16)
        before = sb("before", [P, P], F16)
        rest = sb("rest", [P, P], F16)
        ones16 = sb("ones16", [P, P], F16)
        first_row = sb("first_row", [P, P])
        ident = sb("ident", [P, P])
        onesT = sb("onesT", [P, T])
        u_heads = sb("u_heads", [P, 2, H, F])
        fcb_sb = sb("fcb_sb", [P, 1])
        bias_sb = sb("bias_sb", [P, F])
        w_stack = sb("w_stack", [P, F])
        W1_sb = sb("W1_sb", [CAT, 2 * M2])
        W2_sb = sb("W2_sb", [2 * M2, F])

        X = sb("X", [P, T, F])
        SEG = sb("SEG", [P, T + 1, F])
        PAY = [SEG[:, :, :].rearrange("p t f -> p (t f)")[:, 0:T * W].rearrange("p (t w) -> p t w", w=W)
               for W in (WS, WD)]
        x_flat = X[:, :, :].rearrange("p t f -> p (t f)")
        hot16 = [x_flat[:, (2 + q) * T * 8:(3 + q) * T * 8].bitcast(F16).rearrange(order, a=16)
                 for q, order in enumerate(("p (t a) -> p a t", "p (a t) -> p a t"))]
        fixed_hot = x_flat[:, 2 * T * 8:3 * T * 8].bitcast(F16)
        attr_in_order = x_flat[:, 0:T * A]
        key_i = sb("key_i", [P, T], I32)
        digit = sb("digit", [P, T])
        high = sb("high", [P, T])
        mark, inner_row = high, key_i
        ew_sb = sb("ew_sb", [P, T])
        keyf = sb("keyf", [P, T])
        same = [sb(f"same{k}", [P, T]) for k in range(2)]
        whole = [sb(f"whole{k}", [P, T]) for k in range(2)]
        last = [sb(f"last{k}", [P, T]) for k in range(2)]
        deg = [sb(f"deg{k}", [P, T]) for k in range(2)]
        more = sb("more", [P, T])
        tail = sb("tail", [P, T])
        src_row = [sb(f"src_row{k}", [P, T], I32) for k in range(2)]
        dst_row = [sb(f"dst_row{k}", [P, T], I32) for k in range(2)]
        out_row = [sb(f"out_row{k}", [P, T], I32) for k in range(2)]
        a_src = sb("a_src", [P, H, T])
        a_dst = sb("a_dst", [P, H, T])
        seg_flat = SEG[:, :, :].rearrange("p t f -> p (t f)")
        back, own_score = (seg_flat[:, q * H * T:(q + 1) * H * T].rearrange("p (h t) -> p h t", h=H)
                           for q in range(2))
        fore = seg_flat[:, 2 * H * T:2 * H * T + H * (T + 1)].rearrange("p (h t) -> p h t", h=H)

        onehot = [sb(f"onehot{i}", [P, T], F16) for i in range(4)]
        half_i = sb("half_i", [P, 2], I32)
        half_f = sb("half_f", [P, 2])
        block_mask = sb("block_mask", [P, 8])
        place_mask = sb("place_mask", [P, 16])
        pair_sums = sb("pair_sums", [P, 16])
        spread16 = sb("spread16", [P, 16, 16])
        high_hot = [sb(f"high_hot{i}", [P, HIGH + 1], F16) for i in range(2)]
        digit_c = sb("digit_c", [P, C])
        high_c = sb("high_c", [P, C])
        base = sb("base", [P, T])
        pairs = base[:, 0:P].rearrange("p (b k) -> p b k", b=16)
        hist_sb = sb("hist_sb", [P, T])
        junk = sb("junk", [P, T])
        rank_c = sb("rank_c", [P, C])
        int_c = sb("int_c", [P, 2, C], I32)
        flt_c = sb("flt_c", [P, 2, C])
        row_c = [sb(f"row_c{b}", [P, 3, C], I32) for b in range(2)]
        got = [sb(f"got{b}", [P, 2 * C * RW]) for b in range(2)]
        put = [sb(f"put{b}", [P, C * RW]) for b in range(2)]
        hidT = [sb(f"hidT{b}", [P, 4 * P]) for b in range(2)]
        attr_c = [sb(f"attr_c{b}", [P, C, A]) for b in range(2)]
        sums = sb("sums", [P, NC])
        var = sb("var", [P, 3 * C])
        std = sb("std", [P, 3 * C])
        cen = sb("cen", [P, NC, F])
        cen_flat = cen[:, :, :].rearrange("p c f -> p (c f)")
        sqr = sb("sqr", [P, NC, F])
        both = sb("both", [P, 2 * C, F])
        ha, hb = both[:, 0:C, :], both[:, C:2 * C, :]
        a_dst_flat = a_dst[:, :, :].rearrange("p h t -> p (h t)")
        a_src_flat = a_src[:, :, :].rearrange("p h t -> p (h t)")
        cat = a_dst_flat[:, 0:C * CAT].rearrange("p (c k) -> p c k", k=CAT)
        catT = [a_src_flat[0:CAT, q * 4 * P:(q + 1) * 4 * P] for q in range(2)]
        qT = [a_src_flat[:, q * 4 * P:(q + 1) * 4 * P] for q in range(2)]
        node_in_all = sb("node_in", [P, 2, NC * RW])
        node_in = [node_in_all[:, b, :].rearrange("p (r w) -> p r w", w=RW) for b in range(2)]
        prod = node_in_all[:, :, :].rearrange("p b n -> p (b n)")[:, 0:C * H * F]\
            .rearrange("p (c h f) -> p c h f", h=H, f=F)
        node_out = [sb(f"node_out{b}", [P, NC, F]) for b in range(2)]
        fcw_sb = sb("fcw_sb", [F, 2])
        fcw_wide = hist_sb[0:F, 0:2 * P].rearrange("o (s p) -> o s p", s=2)
        w_turned = junk[0:F, 0:P]
        primer = sb("primer", [16, F])
        dst_prev = sb("dst_prev", [P, 1], I32)
        dst_next = sb("dst_next", [P, 1], I32)
        disorder = sb("disorder", [P, 1])
        unsorted = sb("unsorted", [1, 1], I32)
        fix = sb("fix", [P, RW])
        fix_c = sb("fix_c", [P, RW])
        fix_row = sb("fix_row", [P, 1], I32)
        fix_h = sb("fix_h", [P, 1, F])
        fix_score = sb("fix_score", [P, H, 1])
        fix_std = sb("fix_std", [P, 1])
        carry_l0 = sb("carry_l0", [P, F])
        fix_x2 = sb("fix_x2", [P, F])
        fix_max = sb("fix_max", [P, F])
        gain_l2 = sb("gain_l2", [P, F])
        edge_prev = [sb(f"edge_prev{k}", [P, 1]) for k in range(2)]
        edge_next = [sb(f"edge_next{k}", [P, 1]) for k in range(2)]
        ends = sb("ends", [P, 2, F])
        endsT = sb("endsT", [F, 2, P])
        carryT = sb("carryT", [F, P + 1])
        carryT_back = sb("carryT_back", [F, P])
        carry = sb("carry", [P, F])
        carry_back = sb("carry_back", [P, F])

        hist_ps = ctx.enter_context(nc.psum_tensor("hist_ps", [P, 512], F32))
        count_ps = [ctx.enter_context(nc.psum_tensor(f"count_ps{b}", [P, 512], F32)) for b in range(2)]
        turn_ps = [ctx.enter_context(nc.psum_tensor(f"turn_ps{b}", [P, 512], F32)) for b in range(2)]
        y_ps = ctx.enter_context(nc.psum_tensor("y_ps", [P, 512], F32))
        hid_ps = ctx.enter_context(nc.psum_tensor("hid_ps", [P, 512], F32))
        y_banks = [y_ps, hid_ps]
        turn_banks = [turn_ps[0], turn_ps[1], count_ps[0], count_ps[1]]
        hid_banks = [hid_ps, hist_ps]
        carry_ps = ctx.enter_context(nc.psum_tensor("carry_ps", [P, 512], F32))

        turns = {e: sem(f"turns_{e}") for e in ("dve", "act", "pool", "sp", "pe")}
        dve_chain = sem("dve_chain")
        consts_iota, consts_load, consts_dve = sem("consts_iota"), sem("consts_load"), sem("consts_dve")
        edges_in = sem("edges_in")
        attr_copied, attr_in, attr_stored = sem("attr_copied"), sem("attr_in"), sem("attr_stored")
        w_in_turn, w_ready, u_ready = sem("w_in_turn"), sem("w_ready"), sem("u_ready")
        hot16_ready, pairs_ready, spread_ready, hist_ready, base_ready = (
            sem("hot16_ready"), sem("pairs_ready"), sem("spread_ready"), sem("hist_ready"), sem("base_ready"))
        rank_hot, rank_free, rank_ready, rank_read, rank_done = (
            sem("rank_hot"), sem("rank_free"), sem("rank_ready"), sem("rank_read"), sem("rank_done"))
        rows_ready, pay_ready = sems("rows_ready"), sems("pay_ready")
        sort_scatter = [sems(f"sort_scatter{n}_") for n in range(4)]
        high_hot_ready, high_free = sem("high_hot_ready"), sem("high_free")
        disorder_ready, disorder_sum, unsorted_ready = sem("disorder_ready"), sem("disorder_sum"), sem("unsorted_ready")
        sorted_used, edges_loaded = sem("sorted_used"), sem("edges_loaded")
        q_used, q_last, fix_ready, fix_written = sem("q_used"), sem("q_last"), sem("fix_ready"), sem("fix_written")
        deg_ready, deg_rooted = sem("deg_ready"), sem("deg_rooted")
        pass_written, pass_loaded, pay_made = sem("pass_written"), sem("pass_loaded"), sem("pay_made")
        ends_ready, ends_turned, carry_ready, carry_turned = (
            sem("ends_ready"), sem("ends_turned"), sem("carry_ready"), sem("carry_turned"))
        var_ready, std_ready = sem("var_ready"), sem("std_ready")
        gathers = {n: sems(f"gather_{n}_") for n in ("l0", "l1", "l2", "l3")}
        scatters = {n: sems(f"scatter_{n}_") for n in ("l0", "l1", "l2", "l3")}
        put_ready = sems("put_ready")
        layer_done = sem("layer_done")
        init_in, init_out, init_padded = sems("init_in"), sems("init_out"), sems("init_padded")
        tables_ready = sem("tables_ready")
        h1_ready, h1_stored, h1_loaded, h1_used = sems("h1_ready"), sems("h1_stored"), sems("h1_loaded"), sems("h1_used")
        e_ready, p_ready = sem("e_ready"), sem("p_ready")
        q_ready, q_free, y_ready, y_used = sem("q_ready"), sem("q_free"), sem("y_ready"), sem("y_used")
        turned, copied = sem("turned"), sem("copied")
        attr_loaded, attr_used = sems("attr_loaded"), sems("attr_used")
        cat_ready, cat_used, hid_ready, hid_copied = sem("cat_ready"), sem("cat_used"), sem("hid_ready"), sem("hid_copied")
        x2_ready, x2_copied = sem("x2_ready"), sem("x2_copied")
        node_loaded, node_used, node_ready, node_stored = (
            sems("node_loaded"), sems("node_used"), sems("node_ready"), sems("node_stored"))
        nodes_done = sem("nodes_done")
        staging_set, buffers_clear = sem("staging_set"), sem("buffers_clear")

        PRIMED = [s for pair in (*sort_scatter, *scatters.values()) for s in pair]
        PRIME = 16
        primer_row = bias.rearrange("(a n) -> a n", a=1)

        def take(eng, s, n=1):
            eng.wait_ge(s, n)
            eng.sem_inc(s, -n)

        def landed(eng, name, s, value):
            eng.wait_ge(s, value)
            eng.sem_inc(turns[name], 1)

        def dst_unsorted(eng):
            eng.wait_ge(unsorted_ready, 1)
            return eng.value_load(unsorted[0:1, 0:1], min_val=0, max_val=1) != 0

        block = ctx.enter_context(nc.Block())
        GROUPS = [(0, 4), (4, 8), (8, 12), (12, 14)]

        @block.gpsimd
        def _(pool):
            nc.gpsimd.iota(digits_row[:, :], [[1, T]], base=0, channel_multiplier=0,
                           allow_small_or_imprecise_dtypes=True)
            nc.gpsimd.iota(half_i[:, :], [[0, 2]], base=0, channel_multiplier=1)
            nc.gpsimd.memset(ident[:, :], 0.0)
            nc.gpsimd.memset(before[:, :], 1.0)
            nc.gpsimd.memset(rest[:, :], 1.0)
            nc.gpsimd.memset(ones16[:, :], 1.0)
            nc.gpsimd.memset(first_row[:, :], 1.0)
            pool.drain().then_inc(consts_iota, 1)
            pool.wait_ge(consts_iota, 1)
            nc.gpsimd.affine_select(out=ident[:, :], in_=ident[:, :], compare_op=ALU.not_equal, fill=1.0,
                                    base=0, pattern=[[-1, P]], channel_multiplier=1).then_inc(consts_iota, 1)
            nc.gpsimd.affine_select(out=before[:, :], in_=before[:, :], compare_op=ALU.is_ge, fill=0.0,
                                    base=-1, pattern=[[1, P]], channel_multiplier=-1).then_inc(consts_iota, 1)
            nc.gpsimd.affine_select(out=rest[:, :], in_=rest[:, :], compare_op=ALU.is_ge, fill=0.0,
                                    base=0, pattern=[[-1, P]], channel_multiplier=1).then_inc(consts_iota, 1)
            nc.gpsimd.affine_select(out=first_row[:, :], in_=first_row[:, :], compare_op=ALU.is_ge, fill=0.0,
                                    base=0, pattern=[[0, P]], channel_multiplier=-1).then_inc(consts_iota, 1)
            for b in range(2):
                nc.gpsimd.memset(got[b][:, :], 0.0)
                nc.gpsimd.memset(put[b][:, :], 0.0)
                nc.gpsimd.memset(node_in[b][:, :, :], 0.0)
                nc.gpsimd.memset(hidT[b][:, :], 1.0)
            pool.drain().then_inc(buffers_clear, 1)
            pool.wait_ge(staging_set, 2)
            pool.wait_ge(buffers_clear, 1)

            for n, s in enumerate(PRIMED):
                pool.dma_start(primer[n:n + 1, :], primer_row).then_inc(s, 16)

            def gather(b, way, table, width, s):
                for j in range(C):
                    pool.indirect_dma_start(
                        got[b][:, (way * C + j) * width:(way * C + j + 1) * width], None, table,
                        bass.IndirectOffsetOnAxis(ap=row_c[b][:, way, j:j + 1], axis=0),
                        bounds_check=N - 1, oob_is_err=False).then_inc(s, 16)

            def scatter(b, table, data, width, s, bound):
                for j in range(C):
                    pool.indirect_dma_start(
                        table, bass.IndirectOffsetOnAxis(ap=row_c[b][:, 2, j:j + 1], axis=0),
                        data[:, j * width:(j + 1) * width], None,
                        bounds_check=bound, oob_is_err=False).then_inc(s, 16)

            def sort(k, W):
                for n in range(2):
                    with pool.Fori(0, TURNS) as i:
                        for b in range(2):
                            take(pool, rows_ready[b])
                            take(pool, pay_ready[b])
                            scatter(b, (mid_table, edge_table)[n][k],
                                    put[b][:, :], W,
                                    sort_scatter[2 * k + n][b], EP - 1)
                    for b in range(2):
                        pool.wait_ge(sort_scatter[2 * k + n][b], PRIME + 16 * C * TURNS)
                    pool.sem_inc(pass_written, 1)

            sort(0, WS)
            with pool.If(dst_unsorted(pool)):
                sort(1, WD)

            for layer, (table, width, ways, target, wide) in enumerate((
                    (x, F, 2, x1_table, F), (x1_table, F, 1, x2_table, RW),
                    (x2_table, RW, 2, x3_table, F), (x3_table, F, 1, out, F))):
                name = f"l{layer}"

                def gather_chunk(b):
                    take(pool, rows_ready[b])
                    for way in range(ways):
                        gather(b, way, table, width, gathers[name][b])

                def scatter_chunk(b):
                    take(pool, put_ready[b])
                    scatter(b, target, put[b][:, :], wide, scatters[name][b], N - 1)

                if layer in (0, 3):
                    gather_chunk(0)
                    gather_chunk(1)
                    pool.wait_ge(tables_ready, 1)
                    with pool.Fori(0, TURNS - 1) as i:
                        for b in range(2):
                            gather_chunk(b)
                            scatter_chunk(b)
                    scatter_chunk(0)
                    scatter_chunk(1)
                else:
                    with pool.Fori(0, TURNS) as i:
                        for b in range(2):
                            gather_chunk(b)
                    if layer == 2:
                        pool.wait_ge(nodes_done, 1)
                    with pool.Fori(0, TURNS) as i:
                        for b in range(2):
                            scatter_chunk(b)
                take(pool, fix_ready)
                pool.indirect_dma_start(target, bass.IndirectOffsetOnAxis(ap=fix_row[:, 0:1], axis=0),
                                        fix[:, 0:wide], None, bounds_check=N - 1, oob_is_err=False)\
                    .then_inc(fix_written, 16)
                pool.wait_ge(fix_written, 16 * (layer + 1))
                for b in range(2):
                    pool.wait_ge(scatters[name][b], PRIME + 16 * C * TURNS)
                pool.sem_inc(layer_done, 1)

        @block.sync
        def _(sp):
            sp.dma_start(key_i[:, :], src.rearrange("(p t) -> p t", t=T)).then_inc(edges_in, 16)
            sp.dma_start(ew_sb[:, :], ew.rearrange("(p t) -> p t", t=T)).then_inc(edges_in, 16)
            sp.dma_start(dst_row[1][:, :], dst.rearrange("(p t) -> p t", t=T)).then_inc(edges_in, 16)
            sp.dma_start(src_row[1][:, :], src.rearrange("(p t) -> p t", t=T)).then_inc(edges_in, 16)
            sp.wait_ge(staging_set, 1)
            sp.dma_start(dst_prev[1:P, :], dst.rearrange("(p t) -> p t", t=T)[0:P - 1, T - 1:T],
                         allow_slow_non_contiguous=True).then_inc(edges_in, 16)
            sp.dma_start(dst_next[0:P - 1, :], dst.rearrange("(p t) -> p t", t=T)[1:P, 0:1],
                         allow_slow_non_contiguous=True).then_inc(edges_in, 16)
            sp.dma_start(fcw_sb[:, :], fc_w.rearrange("a (s o) -> o (a s)", s=2),
                         allow_slow_non_contiguous=True).then_inc(consts_load, 16)
            sp.dma_start(fcb_sb[:, :], fc_b.rearrange("(a n) -> a n", a=1).to_broadcast([P, 1])).then_inc(consts_load, 16)
            sp.dma_start(bias_sb[:, :], bias.rearrange("(a n) -> a n", a=1).to_broadcast([P, F])).then_inc(consts_load, 16)
            sp.dma_start(w_stack[:, :], w.rearrange("h f o -> (h f) o")).then_inc(consts_load, 16)
            sp.wait_ge(staging_set, 2)
            for q in (0, M2):
                sp.dma_start(W1_sb[0:CAT - 1, q:q + MID], W1).then_inc(consts_load, 16)
                sp.dma_start(W1_sb[CAT - 1:CAT, q:q + MID], b1.rearrange("(a n) -> a n", a=1)).then_inc(consts_load, 16)
                sp.dma_start(W2_sb[q:q + MID, :], W2).then_inc(consts_load, 16)
            sp.dma_start(W2_sb[MID:MID + 1, :], b2.rearrange("(a n) -> a n", a=1)).then_inc(consts_load, 16)

            xv = x.rearrange("(p r) f -> p r f", p=P)
            x1v = x1_table.rearrange("(p r) f -> p r f", p=P)
            x2v = x2_table.rearrange("(p r) f -> p r f", p=P)
            sp.wait_ge(buffers_clear, 1)
            for b in range(2):
                sp.sem_inc(init_out[b], 32)
            with sp.Fori(0, TURNS) as i:
                for b in range(2):
                    c = i * 2 + b
                    take(sp, init_out[b], 32)
                    sp.dma_start(node_out[b][:, :, :], xv[:, bass.ts(c, NC), :]).then_inc(init_in[b], 16)
                    take(sp, init_padded[b])
                    sp.dma_start(x1v[:, bass.ts(c, NC), :], node_out[b][:, :, :]).then_inc(init_out[b], 16)
                    sp.dma_start(x2v[:, bass.ts(c, NC), :], node_in[b][:, :, :]).then_inc(init_out[b], 16)
            for b in range(2):
                take(sp, init_out[b], 32)
            sp.sem_inc(tables_ready, 1)

            def reload(k):
                for n in range(2):
                    sp.wait_ge(pass_written, 2 * k + n + 1)
                    sp.dma_start(PAY[k].rearrange("p t w -> p (t w)"),
                                 (mid_table, edge_table)[n][k].rearrange("(p t) w -> p (t w)", t=T))\
                        .then_inc(pass_loaded, 16)

            def load_neighbours(k):
                tv = edge_table[k].rearrange("(p t) w -> p t w", t=T)
                sp.dma_start(edge_prev[k][1:P, :], tv[0:P - 1, T - 1, k:k + 1],
                             allow_slow_non_contiguous=True).then_inc(edges_loaded, 16)
                sp.dma_start(edge_next[k][0:P - 1, :], tv[1:P, 0, k:k + 1],
                             allow_slow_non_contiguous=True).then_inc(edges_loaded, 16)

            reload(0)
            load_neighbours(0)
            with sp.If(dst_unsorted(sp)):
                sp.dma_start(attr_in_order, attr.rearrange("(p t) a -> p (t a)", t=T)).then_inc(attr_in, 16)
                reload(1)
                load_neighbours(1)
                sp.wait_ge(pass_loaded, 64)
                sp.dma_start(attr_table.rearrange("(p t) a -> p t a", t=T), PAY[1][:, :, 2:WD]).then_inc(attr_stored, 16)
            with sp.Else():
                sp.dma_start(attr_table.rearrange("(p t) a -> p (t a)", t=T),
                             attr.rearrange("(p t) a -> p (t a)", t=T)).then_inc(attr_stored, 16)

            h1v = h1_table.rearrange("p (c n) -> p c n", c=CHUNKS)
            with sp.Fori(0, TURNS) as i:
                for b in range(2):
                    take(sp, h1_ready[b])
                    sp.dma_start(h1v[:, i * 2 + b, :], put[b][:, 0:C * F]).then_inc(h1_stored[b], 16)
            for b in range(2):
                take(sp, h1_used[b], 1)
            with sp.Fori(0, TURNS) as i:
                for b in range(2):
                    take(sp, h1_used[b])
                    sp.dma_start(got[b][:, 0:C * F], h1v[:, i * 2 + b, :]).then_inc(h1_loaded[b], 16)

            av = attr_table.rearrange("(p t) a -> p t a", t=T)
            sp.wait_ge(attr_stored, 16)
            sp.wait_ge(layer_done, 2)
            with sp.Fori(0, TURNS) as i:
                for b in range(2):
                    c = i * 2 + b
                    take(sp, attr_used[b])
                    sp.dma_start(attr_c[b][:, :, :], av[:, bass.ts(c, C), :]).then_inc(attr_loaded[b], 16)
                    take(sp, node_used[b])
                    sp.dma_start(node_in[b][:, :, :], x2v[:, bass.ts(c, NC), :]).then_inc(node_loaded[b], 16)
            sp.wait_ge(layer_done, 4)

        @block.scalar
        def _(act):
            act.wait_ge(staging_set, 2)
            act.wait_ge(buffers_clear, 1)
            def sort(k, W):
                for n in range(2):
                    take(act, pay_made)
                    with act.Fori(0, TURNS) as i:
                        for b in range(2):
                            landed(act, "act", sort_scatter[2 * k + n][b], i * (16 * C) + PRIME)
                            pc = put[b][:, 0:C * W].rearrange("p (c w) -> p c w", w=W)
                            nc.scalar.activation(pc, PAY[k][:, bass.ts(i * 2 + b, C), :], ACT.Copy).then_inc(pay_ready[b], 1)
                            if k == 0 and n == 0:
                                take(act, init_in[b], 16)
                                nc.scalar.activation(node_in[b][:, :, 0:F], node_out[b][:, :, :], ACT.Copy)\
                                    .then_inc(init_padded[b], 1)

            sort(0, WS)
            with act.If(dst_unsorted(act)):
                act.wait_ge(attr_in, 16)
                act.wait_ge(sorted_used, 1)
                nc.scalar.activation(PAY[1][:, :, 2:WD], attr_in_order.rearrange("p (t a) -> p t a", a=A),
                                     ACT.Copy).then_inc(attr_copied, 1)
                sort(1, WD)

            def root(n, m=1):
                for _ in range(m):
                    take(act, var_ready)
                    nc.scalar.activation(std[:, 0:n], var[:, 0:n], ACT.Sqrt).then_inc(std_ready, 1)

            with act.Fori(0, TURNS) as i:
                for b in range(2):
                    root(2 * C)
                    root(C)
            root(1)
            with act.Fori(0, TURNS) as i:
                root(C, 2)
            take(act, e_ready)
            nc.scalar.activation(a_dst[:, :, :], a_dst[:, :, :], ACT.Exp).then_inc(p_ready, 1)
            act.sem_inc(q_free, 1)
            act.sem_inc(q_last, 1)
            with act.Fori(0, TURNS) as i:
                for b in range(2):
                    for g, (j0, j1) in enumerate(GROUPS):
                        take(act, turned)
                        if g == 3:
                            act.sem_inc(q_used, 1)
                        take(act, q_last if g == 1 else q_free)
                        nc.scalar.activation(qT[g % 2][:, 0:(j1 - j0) * P], turn_ps[g % 2][:, 0:(j1 - j0) * P],
                                             ACT.Copy).then_inc(copied, 1)
            x3v = x3_table.rearrange("(p r) f -> p r f", p=P)
            ov = out.rearrange("(p r) f -> p r f", p=P)
            act.sem_inc(cat_used, 1)

            def store_nodes(b, c):
                take(act, node_ready[b])
                act.dma_start(x3v[:, bass.ts(c, NC), :], node_out[b][:, :, :]).then_inc(node_stored[b], 16)
                act.dma_start(ov[:, bass.ts(c, NC), :], node_out[b][:, :, :]).then_inc(node_stored[b], 16)

            def copy_cat(g):
                n = (GROUPS[g][1] - GROUPS[g][0]) * P
                act.wait_ge(turned, g + 1)
                nc.scalar.activation(catT[g % 2][:, 0:n], turn_banks[g][0:CAT, 0:n], ACT.Copy).then_inc(copied, 1)

            def copy_hid(g):
                n = (GROUPS[g][1] - GROUPS[g][0]) * P
                act.wait_ge(hid_ready, g + 1)
                nc.scalar.activation(hidT[g % 2][0:MID, 0:n], hid_banks[g % 2][0:MID, 0:n], ACT.Relu, scale=0.99)
                nc.scalar.activation(hidT[g % 2][M2:M2 + MID, 0:n], hid_banks[g % 2][M2:M2 + MID, 0:n],
                                     ACT.Copy, scale=0.01).then_inc(hid_copied, 1)

            def l2_edges(b, c, nodes=True):
                take(act, x2_ready)
                nc.scalar.activation(X[:, bass.ts(c, C), :], hb, ACT.Copy).then_inc(x2_copied, 1)
                root(3 * C)
                copy_cat(0)
                copy_cat(1)
                for g in range(4):
                    if g == 3 and nodes:
                        root(NC)
                    copy_hid(g)
                    if g < 2:
                        copy_cat(g + 2)
                    if g == 1:
                        act.sem_inc(cat_used, 1)
                act.sem_inc(turned, -4)
                act.sem_inc(hid_ready, -4)
                if nodes:
                    store_nodes(1 - b, c + 1)

            root(NC)
            store_nodes(0, 0)
            with act.Fori(0, TURNS - 1) as i:
                for b in range(2):
                    l2_edges(b, i * 2 + b)
            l2_edges(0, CHUNKS - 2)
            root(C)
            for b in range(2):
                take(act, node_stored[b], 32)
            act.sem_inc(nodes_done, 1)
            root(C)
            l2_edges(1, CHUNKS - 1, nodes=False)
            with act.Fori(1, TURNS) as i:
                root(C, 2)
            take(act, deg_ready)
            nc.scalar.activation(deg[1][:, :], deg[1][:, :], ACT.Sqrt).then_inc(deg_rooted, 1)
            with act.Fori(0, TURNS) as i:
                root(C, 2)

        @block.tensor
        def _(pe):
            pe.wait_ge(consts_iota, 5)
            pe.wait_ge(consts_dve, 1)

            def turn_ends(ways=1):
                take(pe, ends_ready)
                nc.tensor.transpose(carry_ps[0:F, 0:P], ends[:, 0, :], ident[:, :])
                nc.tensor.transpose(carry_ps[0:F, P:2 * P], ends[:, 1, :], ident[:, :]).then_inc(ends_turned, 1)
                take(pe, carry_ready)
                for q in range(ways):
                    t = nc.tensor.transpose(carry_ps[:, 256 + q * F:256 + (q + 1) * F], (carryT, carryT_back)[q][:, 0:P],
                                            ident[0:F, 0:F])
                t.then_inc(carry_turned, 1)

            def sort(k):
                for n, R in enumerate((LOW, HIGH)):
                    if n == 0:
                        take(pe, hot16_ready)
                        for q in range(0, T, 8):
                            t = nc.tensor.matmul(carry_ps[:, 0:P], fixed_hot[:, q * 16:(q + 8) * 16],
                                                 hot16[1][:, :, q:q + 8],
                                                 start=(q == 0), stop=(q == T - 8))
                        t.then_inc(pairs_ready, 1)
                        if k == 0:
                            take(pe, disorder_ready)
                            nc.tensor.matmul(y_ps[0:1, 0:1], disorder[:, :], onesT[:, 0:1], start=True,
                                             stop=True).then_inc(disorder_sum, 1)
                        take(pe, spread_ready)
                        nc.tensor.matmul(hist_ps[:, 0:R], onesT[:, 0:P], spread16[:, :, :].rearrange("p a b -> p (a b)"),
                                         start=True, stop=True).then_inc(hist_ready, 1)
                    take(pe, base_ready)
                    if n == 0:
                        nc.tensor.matmul(hist_ps[:, 0:HIGH], ones16[:, :], high_hot[1][:, 0:HIGH], start=True,
                                         stop=True).then_inc(high_free, 2)
                    for q in range(2):
                        nc.tensor.matmul(count_ps[q][:, 0:R], first_row[:, :], base[:, 0:R], start=True, stop=True,
                                         skip_group_check=True)
                    with pe.Fori(0, TURNS) as i:
                        for j in range(2 * C):
                            pe.wait_ge(rank_hot, j + 1)
                            nc.tensor.matmul(count_ps[j % 2][:, 0:R], before[:, :], onehot[j % 4][:, 0:R],
                                             start=False, stop=True, skip_group_check=True).then_inc(rank_ready, 1)
                            pe.wait_ge(rank_read, j + 1)
                            nc.tensor.matmul(count_ps[1 - j % 2][:, 0:R], rest[:, :], onehot[(j - 1) % 4][:, 0:R],
                                             start=False, stop=True, skip_group_check=True).then_inc(rank_free, 1)
                            nc.tensor.matmul(count_ps[1 - j % 2][:, 0:R], ones16[:, :], onehot[j % 4][:, 0:R],
                                             start=False, stop=True, skip_group_check=True).then_inc(rank_done, 1)
                            if n == 0:
                                pe.wait_ge(high_hot_ready, j + 1)
                                nc.tensor.matmul(hist_ps[:, 0:HIGH], ones16[:, :], high_hot[j % 2][:, 0:HIGH],
                                                 start=False, stop=True, skip_group_check=True).then_inc(high_free, 1)
                        if n == 0:
                            pe.sem_inc(high_hot_ready, -2 * C)
                        pe.sem_inc(rank_hot, -2 * C)
                        pe.sem_inc(rank_read, -2 * C)

            sort(0)
            with pe.If(dst_unsorted(pe)):
                sort(1)
            pe.wait_ge(consts_load, 16 * 11)
            nc.tensor.transpose(y_ps[0:F, 0:P], w_stack[:, :], ident[:, :]).then_inc(w_in_turn, 1)
            take(pe, w_ready)
            for side in range(2):
                t = nc.tensor.matmul(y_ps[:, (side + 1) * P:(side + 2) * P], fcw_wide[:, side, :], w_turned,
                                     start=True, stop=True, skip_group_check=True)
            t.then_inc(u_ready, 1)
            turn_ends()
            turn_ends()
            turn_ends()
            turn_ends(2)
            turn_ends(2)
            turn_ends(2)
            with pe.Fori(0, TURNS) as i:
                for b in range(2):
                    take(pe, q_ready)

                    def turn(g):
                        j0, j1 = GROUPS[g]
                        for j in range(j0, j1):
                            t = nc.tensor.transpose(turn_ps[g % 2][:, (j - j0) * P:(j - j0 + 1) * P],
                                                    prod[:, j, :, :].rearrange("p h f -> p (h f)"), ident[:, :])
                        t.then_inc(turned, 1)

                    turn(0)
                    take(pe, y_used)
                    for g, (j0, j1) in enumerate(GROUPS):
                        if g < 3:
                            turn(g + 1)
                        pe.wait_ge(copied, g + 1)
                        for j in range(j0, j1):
                            t = nc.tensor.matmul(y_banks[b][:, j * F:(j + 1) * F], qT[g % 2][:, (j - j0) * P:(j - j0 + 1) * P],
                                                 w_stack[:, :], start=True, stop=True, skip_group_check=True)
                        t.then_inc(q_free if g < 3 else y_ready, 1)
                    pe.sem_inc(copied, -4)
            turn_ends()
            with pe.Fori(0, TURNS) as i:
                for b in range(2):
                    take(pe, cat_ready)
                    for g, (j0, j1) in enumerate(GROUPS):
                        for j in range(j0, j1):
                            t = nc.tensor.transpose(turn_banks[g][0:CAT, (j - j0) * P:(j - j0 + 1) * P],
                                                    cat[:, j, :], ident[:, :])
                        t.then_inc(turned, 1)

                    def hidden(g):
                        n = (GROUPS[g][1] - GROUPS[g][0]) * P
                        pe.wait_ge(copied, g + 1)
                        nc.tensor.matmul(hid_banks[g % 2][:, 0:n], W1_sb[:, :], catT[g % 2][:, 0:n], start=True,
                                         stop=True, skip_group_check=True).then_inc(hid_ready, 1)

                    hidden(0)
                    take(pe, y_used)
                    for g, (j0, j1) in enumerate(GROUPS):
                        if g < 3:
                            hidden(g + 1)
                        pe.wait_ge(hid_copied, g + 1)
                        for j in range(j0, j1):
                            t = nc.tensor.matmul(y_ps[:, j * F:(j + 1) * F], hidT[g % 2][:, (j - j0) * P:(j - j0 + 1) * P],
                                                 W2_sb[:, :], start=True, stop=True, skip_group_check=True)
                    t.then_inc(y_ready, 1)
                    pe.sem_inc(copied, -4)
                    pe.sem_inc(hid_copied, -4)
            turn_ends()
            turn_ends()

        @block.vector
        def _(dve):
            v = nc.vector
            chain = [0]

            def link(ins):
                chain[0] += 1
                ins.then_inc(dve_chain, 1)
                dve.wait_ge(dve_chain, chain[0])

            def chain_end():
                if chain[0]:
                    dve.sem_inc(dve_chain, -chain[0])
                chain[0] = 0

            def per_row(a, n, f=F):
                return a.unsqueeze(2).to_broadcast([P, n, f])

            def per_feature(a, n, f=F):
                return a.unsqueeze(1).to_broadcast([P, n, f])

            def center(src_ap, n):
                link(v.tensor_reduce(sums[:, 0:n], src_ap, AX.X, ALU.add))
                link(v.scalar_tensor_tensor(out=cen[:, 0:n, :], in0=per_row(sums[:, 0:n], n), scalar=-1.0 / F,
                                            in1=src_ap, op0=ALU.mult, op1=ALU.add))
                link(v.tensor_tensor(sqr[:, 0:n, :], cen[:, 0:n, :], cen[:, 0:n, :], ALU.mult))
                link(v.tensor_reduce(var[:, 0:n], sqr[:, 0:n, :], AX.X, ALU.add))
                link(v.tensor_scalar(var[:, 0:n], var[:, 0:n], 1.0 / F, 1e-5, ALU.mult, ALU.add))

            def scale(n):
                link(v.tensor_tensor(cen[:, 0:n, :], cen[:, 0:n, :], per_row(std[:, 0:n], n), ALU.mult))

            def layernorm_relu(src_ap, dst_ap, n):
                center(src_ap, n)
                root(n)
                scale(n)
                link(v.tensor_scalar(dst_ap, cen[:, 0:n, :], 0.0, None, ALU.max))

            def root(n):
                dve.sem_inc(var_ready, 1)
                take(dve, std_ready)
                link(v.reciprocal(std[:, 0:n], std[:, 0:n]))

            link(v.memset(dst_prev[:, :], -1))
            link(v.memset(dst_next[:, :], -1))
            dve.sem_inc(staging_set, 1)
            link(v.memset(W1_sb[:, :], 0.0))
            link(v.memset(W2_sb[:, :], 0.0))
            link(v.memset(edge_prev[0][:, :], -1.0))
            link(v.memset(edge_next[0][:, :], -1.0))
            dve.sem_inc(staging_set, 1)
            link(v.memset(onesT[:, :], 1.0))
            link(v.memset(fix[:, :], 0.0))
            link(v.memset(ends[:, :, :], 0.0))
            dve.wait_ge(consts_iota, 5)
            link(v.tensor_scalar(half_i[:, 0:1], half_i[:, 0:1], 4, None, ALU.logical_shift_right))
            link(v.tensor_scalar(half_i[:, 1:2], half_i[:, 1:2], 15, None, ALU.bitwise_and))
            link(v.tensor_copy(half_f[:, :], half_i[:, :]))
            link(v.tensor_scalar(block_mask[:, :], digits_row[:, 0:8], half_f[:, 0:1], None, ALU.is_equal))
            link(v.tensor_scalar(place_mask[:, :], digits_row[:, 0:16], half_f[:, 1:2], None, ALU.is_equal))
            dve.sem_inc(consts_dve, 1)
            dve.wait_ge(edges_in, 96)
            chain_end()

            def carries(op, values, factors, f, back=None):
                neutral = 0.0 if op == ALU.add else -BIG
                link(v.tensor_copy(ends[:, 0, 0:f], values))
                v.tensor_copy(ends[:, 1, 0:f], factors.to_broadcast([P, f])).then_inc(dve_chain, 1)
                chain[0] += 1
                if back:
                    link(v.tensor_copy(ends[:, 0, f:2 * f], back[0]))
                    v.tensor_copy(ends[:, 1, f:2 * f], back[1].to_broadcast([P, f])).then_inc(dve_chain, 1)
                    chain[0] += 1
                dve.wait_ge(dve_chain, chain[0])
                dve.sem_inc(ends_ready, 1)
                v.memset(carryT[:, :], neutral).then_inc(dve_chain, 1)
                v.memset(carryT_back[:, :], neutral).then_inc(dve_chain, 1)
                chain[0] += 2
                take(dve, ends_turned)
                link(v.tensor_copy(endsT[:, :, :], carry_ps[0:F, 0:2 * P].rearrange("f (a p) -> f a p", a=2)))
                if op == ALU.max:
                    link(v.tensor_scalar(endsT[:, 1, :], endsT[:, 1, :], -1.0, BIG, ALU.add, ALU.mult))
                op0 = ALU.mult if op == ALU.add else ALU.add
                ins = v.tensor_tensor_scan(carryT[:, 1:P + 1], endsT[:, 1, :], endsT[:, 0, :], neutral, op0, op)
                if back:
                    ins.then_inc(dve_chain, 1)
                    chain[0] += 1
                    ins = v.tensor_tensor_scan(carryT_back[:, P - 2::-1], endsT[:, 1, P - 1:0:-1],
                                               endsT[:, 0, P - 1:0:-1], neutral, op0, op)
                link(ins)
                dve.sem_inc(carry_ready, 1)
                take(dve, carry_turned)
                if back:
                    v.tensor_copy(carry_back[:, :], carry_ps[:, 256 + F:256 + 2 * F]).then_inc(dve_chain, 1)
                    chain[0] += 1
                link(v.tensor_copy(carry[:, :], carry_ps[:, 256:256 + F]))

            def first_places(R, q_hist):
                link(v.tensor_copy(hist_sb[:, 0:R], q_hist[:, 0:R]))
                link(v.tensor_tensor_scan(base[:, 0:R], onesT[:, 0:R], hist_sb[:, 0:R], 0.0, ALU.mult, ALU.add))
                link(v.tensor_tensor(base[:, 0:R], base[:, 0:R], hist_sb[:, 0:R], ALU.subtract))

            def count_disorder():
                link(v.tensor_copy(keyf[:, :], dst_row[1][:, :]))
                link(v.tensor_copy(edge_prev[1][:, :], dst_prev[:, :]))
                link(v.tensor_copy(edge_next[1][:, :], dst_next[:, :]))
                link(v.tensor_tensor(junk[:, 0:1], keyf[:, 0:1], edge_prev[1][:, :], ALU.is_lt))
                link(v.tensor_tensor(junk[:, 1:T], keyf[:, 1:T], keyf[:, 0:T - 1], ALU.is_lt))
                link(v.tensor_reduce(disorder[:, :], junk[:, :], AX.X, ALU.add))
                dve.sem_inc(disorder_ready, 1)

            def decide_order():
                take(dve, disorder_sum)
                link(v.tensor_scalar(junk[0:1, 0:1], y_ps[0:1, 0:1], 1.0, None, ALU.min))
                link(v.tensor_copy(unsorted[:, :], junk[0:1, 0:1]))
                dve.sem_inc(unsorted_ready, 1)

            def sort(k):
                for n, R in enumerate((LOW, HIGH)):
                    if n == 0:
                        dve.sem_inc(pay_made, 1)
                        whole_i = out_row[k]
                        link(v.tensor_scalar(whole_i[:, :], key_i[:, :], 8, None, ALU.logical_shift_right))
                        link(v.tensor_copy(high[:, :], whole_i[:, :]))
                        link(v.tensor_scalar(key_i[:, :], key_i[:, :], LOW - 1, None, ALU.bitwise_and))
                        link(v.tensor_copy(digit[:, :], key_i[:, :]))
                        link(v.tensor_scalar(whole_i[:, :], key_i[:, :], 4, None, ALU.logical_shift_right))
                        link(v.tensor_scalar(key_i[:, :], key_i[:, :], 15, None, ALU.bitwise_and))
                        for q, half_int in enumerate((whole_i, key_i)):
                            link(v.tensor_copy(onehot[q][:, :], half_int[:, :]))
                            for a in range(16):
                                v.tensor_scalar(hot16[q][:, a, :], onehot[q][:, :], float(a), None, ALU.is_equal)
                        v.drain()
                        dve.sem_inc(hot16_ready, 1)
                        if k == 0:
                            count_disorder()
                        take(dve, pairs_ready)
                        link(v.tensor_tensor(pairs, carry_ps[:, 0:P].rearrange("p (b k) -> p b k", b=16),
                                             per_feature(block_mask[:, :], 16, 8), ALU.mult))
                        link(v.tensor_reduce(pair_sums[:, :], pairs, AX.X, ALU.add))
                        link(v.tensor_tensor(spread16[:, :, :], per_row(place_mask[:, :], 16, 16),
                                             per_feature(pair_sums[:, :], 16, 16), ALU.mult))
                        dve.sem_inc(spread_ready, 1)
                        if k == 0:
                            decide_order()
                        take(dve, hist_ready)
                        first_places(R, hist_ps)
                        link(v.memset(high_hot[1][:, :], 0.0))
                    else:
                        take(dve, high_free, 2)
                        first_places(R, hist_ps)
                        dve.wait_ge(pass_loaded, 16 * (1 + 2 * k))
                        dve.sem_inc(pay_made, 1)
                        link(v.tensor_copy(key_i[:, :], PAY[k][:, :, k]))
                        link(v.tensor_scalar(key_i[:, :], key_i[:, :], 8, None, ALU.logical_shift_right))
                        link(v.tensor_copy(digit[:, :], key_i[:, :]))
                    link(v.memset(onehot[3][:, :], 0.0))
                    dve.sem_inc(base_ready, 1)
                    dve.sem_inc(rank_read, 1)
                    dve.sem_inc(rank_free, 3)
                    chain_end()
                    with dve.Fori(0, TURNS) as i:
                        for b in range(2):
                            link(v.tensor_scalar(digit_c[:, :], digit[:, bass.ts(i * 2 + b, C)], 1.0, None, ALU.mult))
                            if n == 0:
                                link(v.tensor_scalar(high_c[:, :], high[:, bass.ts(i * 2 + b, C)], 1.0, None, ALU.mult))

                            def make_hot(j):
                                g = b * C + j
                                dve.wait_ge(rank_free, g + 1)
                                v.tensor_scalar(onehot[g % 4][:, 0:R], digits_row[:, 0:R], digit_c[:, j:j + 1], None,
                                                ALU.is_equal).then_inc(rank_hot, 1)

                            make_hot(0)
                            for j in range(C):
                                g = b * C + j
                                if j + 1 < C:
                                    make_hot(j + 1)
                                if n == 0:
                                    dve.wait_ge(high_free, g + 1)
                                    v.tensor_scalar(high_hot[g % 2][:, 0:HIGH], digits_row[:, 0:HIGH], high_c[:, j:j + 1],
                                                    None, ALU.is_equal).then_inc(high_hot_ready, 1)
                                dve.wait_ge(rank_ready, g + 1)
                                v.tensor_tensor_reduce((junk, hist_sb)[g % 2][:, 0:R], count_ps[g % 2][:, 0:R],
                                                       onehot[g % 4][:, 0:R],
                                                       1.0, 0.0, ALU.mult, ALU.add, rank_c[:, j:j + 1]).then_inc(rank_read, 1)
                            landed(dve, "dve", sort_scatter[2 * k + n][b], i * (16 * C) + PRIME)
                            v.drain()
                            if n == 0:
                                link(v.tensor_copy(int_c[:, 0, :], rank_c[:, :]))
                                link(v.tensor_scalar(int_c[:, 1, :], int_c[:, 0, :], 7, None, ALU.logical_shift_right))
                                link(v.tensor_scalar(int_c[:, 0, :], int_c[:, 0, :], P - 1, None, ALU.bitwise_and))
                                link(v.tensor_copy(flt_c[:, :, :], int_c[:, :, :]))
                                link(v.scalar_tensor_tensor(out=rank_c[:, :], in0=flt_c[:, 0, :], scalar=float(T),
                                                            in1=flt_c[:, 1, :], op0=ALU.mult, op1=ALU.add))
                            link(v.tensor_copy(row_c[b][:, 2, :], rank_c[:, :]))
                            dve.sem_inc(rows_ready[b], 1)
                        if n == 0:
                            dve.sem_inc(high_free, -2 * C)
                        dve.sem_inc(rank_free, -2 * C)
                        dve.sem_inc(rank_ready, -2 * C)
                        chain_end()
                    take(dve, rank_free, 3)
                    take(dve, rank_done, T)
                    take(dve, rank_read)
                dve.wait_ge(pass_loaded, 16 * (2 + 2 * k))

            def rows_from(row_ap, values):
                link(v.tensor_scalar(junk[:, :], values, float(N - 1), None, ALU.min))
                link(v.tensor_copy(row_ap, junk[:, :]))

            def segments(k):
                link(v.tensor_tensor(same[k][:, 1:T], keyf[:, 1:T], keyf[:, 0:T - 1], ALU.is_equal))
                link(v.tensor_tensor(same[k][:, 0:1], keyf[:, 0:1], edge_prev[k][:, :], ALU.is_equal))
                link(v.tensor_tensor(last[k][:, 0:T - 1], keyf[:, 0:T - 1], keyf[:, 1:T], ALU.not_equal))
                link(v.tensor_tensor(last[k][:, T - 1:T], keyf[:, T - 1:T], edge_next[k][:, :], ALU.not_equal))
                link(v.tensor_tensor_scan(whole[k][:, :], same[k][:, :], onesT[:, :], 1.0, ALU.mult, ALU.mult))
                link(v.tensor_scalar(junk[:, :], last[k][:, :], -SKIP, SKIP, ALU.mult, ALU.add))
                link(v.tensor_tensor(junk[:, :], junk[:, :], keyf[:, :], ALU.add))
                link(v.tensor_copy(out_row[k][:, :], junk[:, :]))
                if k == 0:
                    link(v.tensor_scalar(more[:, :], last[0][:, :], -1.0, 1.0, ALU.mult, ALU.add))
                    link(v.tensor_tensor_scan(tail[:, ::-1], more[:, ::-1], onesT[:, :], 1.0, ALU.mult, ALU.mult))
                link(v.tensor_tensor_scan(deg[k][:, :], same[k][:, :], onesT[:, :], 0.0, ALU.mult, ALU.add))
                carries(ALU.add, deg[k][:, T - 1:T], whole[k][:, T - 1:T], 1)
                link(v.scalar_tensor_tensor(out=deg[k][:, :], in0=whole[k][:, :], scalar=carry[:, 0:1],
                                            in1=deg[k][:, :], op0=ALU.mult, op1=ALU.add))
                chain_end()

            link(v.tensor_copy(PAY[0][:, :, 0], key_i[:, :]))
            link(v.tensor_copy(PAY[0][:, :, 1], dst_row[1][:, :]))
            link(v.tensor_copy(PAY[0][:, :, 2], ew_sb[:, :]))
            sort(0)
            link(v.tensor_copy(keyf[:, :], PAY[0][:, :, 0]))
            rows_from(src_row[0][:, :], PAY[0][:, :, 0])
            rows_from(dst_row[0][:, :], PAY[0][:, :, 1])
            link(v.tensor_copy(ew_sb[:, :], PAY[0][:, :, 2]))
            dve.sem_inc(sorted_used, 1)
            chain_end()
            with dve.If(dst_unsorted(dve)):
                link(v.tensor_copy(PAY[1][:, :, 0], src_row[1][:, :]))
                link(v.tensor_copy(PAY[1][:, :, 1], dst_row[1][:, :]))
                link(v.tensor_copy(key_i[:, :], dst_row[1][:, :]))
                dve.wait_ge(attr_copied, 1)
                sort(1)
                link(v.tensor_copy(src_row[1][:, :], PAY[1][:, :, 0]))
                link(v.tensor_copy(dst_row[1][:, :], PAY[1][:, :, 1]))
                dve.wait_ge(edges_loaded, 64)
                dve.wait_ge(attr_stored, 16)
                chain_end()

            def scan_chunk(c, data, factors, neutral_op, op):
                for f in range(F):
                    ins = v.tensor_tensor_scan(SEG[:, bass.ds(c * C + 1, C), f], factors, data[:, :, f],
                                               SEG[:, bass.ds(c * C, 1), f], neutral_op, op)
                link(ins)

            def give_rows(b, c, sides):
                for way, rows in sides:
                    link(v.tensor_copy(row_c[b][:, way, :], rows[:, c * C:(c + 1) * C] if isinstance(c, int)
                                       else rows[:, bass.ts(c, C)]))
                dve.sem_inc(rows_ready[b], 1)

            def passed(name, b, i, ways):
                landed(dve, "dve", gathers[name][b], (i + 1) * (16 * C * ways))

            def rows_of(b, way=0, ways=1, width=F):
                return got[b][:, way * C * width:(way + ways) * C * width].rearrange("p (c w) -> p c w", w=width)

            def heads_dot(side, h_ap, dst_ap, n=C):
                link(v.tensor_tensor(prod[:, 0:n, :, :],
                                     h_ap.unsqueeze(2).to_broadcast([P, n, H, F]),
                                     u_heads[:, side, :, :].unsqueeze(1).to_broadcast([P, n, H, F]), ALU.mult))
                link(v.tensor_reduce(dst_ap, prod[:, 0:n, :, :].rearrange("p c h f -> p h c f"), AX.X, ALU.add))

            def first_rows(sides):
                for b in range(2):
                    give_rows(b, b, sides)
                chain_end()

            def gather_loop(name, sides, body, after=None):
                chain_end()
                with dve.Fori(0, TURNS - 1) as i:
                    for b in range(2):
                        passed(name, b, i, len(sides))
                        body(b, i)
                        give_rows(b, i * 2 + b + 2, sides)
                        if after:
                            after(b, i)
                    chain_end()
                for b in range(2):
                    passed(name, b, TURNS - 1, len(sides))
                    body(b, TURNS - 1)
                    if after:
                        after(b, TURNS - 1)
                chain_end()

            def find_fixes(k):
                link(v.tensor_tensor(mark[:, :], last[k][:, :], whole[k][:, :], ALU.mult))
                link(v.tensor_copy(junk[:, :], out_row[k][:, :]))
                link(v.tensor_tensor(hist_sb[:, :], junk[:, :], mark[:, :], ALU.mult))
                link(v.tensor_reduce(sums[:, 0:1], hist_sb[:, :], AX.X, ALU.add))
                link(v.tensor_reduce(sums[:, 1:2], mark[:, :], AX.X, ALU.add))
                link(v.tensor_scalar(sums[:, 1:2], sums[:, 1:2], -SKIP, SKIP, ALU.mult, ALU.add))
                link(v.tensor_tensor(sums[:, 0:1], sums[:, 0:1], sums[:, 1:2], ALU.add))
                link(v.tensor_copy(fix_row[:, :], sums[:, 0:1]))
                link(v.scalar_tensor_tensor(out=junk[:, :], in0=whole[k][:, :], scalar=SKIP, in1=junk[:, :],
                                            op0=ALU.mult, op1=ALU.add))
                link(v.tensor_copy(inner_row[:, :], junk[:, :]))

            def keep_marked(kept, rows, c, width=F):
                marked = cen_flat[:, 0:C * width].rearrange("p (c w) -> p c w", w=width)
                link(v.tensor_tensor(marked, rows, per_row(mark[:, bass.ts(c, C)], C, width), ALU.mult))
                link(v.tensor_reduce(fix_c[:, 0:width], marked.rearrange("p c w -> p w c"), AX.X, ALU.add))
                link(v.tensor_tensor(kept[:, 0:width], kept[:, 0:width], fix_c[:, 0:width], ALU.add))

            def put_inner(name, b, i, width, rows_made):
                c = i * 2 + b
                landed(dve, "dve", scatters[name][b], i * (16 * C) + PRIME)
                link(v.tensor_copy(row_c[b][:, 2, :], inner_row[:, bass.ts(c, C)]))
                rows = put[b][:, 0:C * width].rearrange("p (c w) -> p c w", w=width)
                rows_made(c, rows)
                dve.sem_inc(put_ready[b], 1)
                keep_marked(fix, rows, c, width)

            def neutral_column(value):
                link(v.memset(SEG[:, 0, :], value))

            def l0_gathered(b, i):
                c = i * 2 + b
                layernorm_relu(rows_of(b, 0, 2), both[:, :, :], 2 * C)
                link(v.tensor_tensor(X[:, bass.ts(c, C), :], rows_of(b, 1), per_row(onesT[:, 0:C], C), ALU.mult))
                link(v.tensor_tensor(ha, ha, hb, ALU.subtract))
                link(v.tensor_tensor(ha, ha, per_row(ew_sb[:, bass.ts(c, C)], C), ALU.mult))
                scan_chunk(c, ha, same[0][:, bass.ts(c, C)], ALU.mult, ALU.add)

            l0_sides = [(0, dst_row[0]), (1, src_row[0])]
            first_rows(l0_sides)
            dve.wait_ge(consts_load, 16 * 11)
            link(v.tensor_copy(fcw_wide, fcw_sb[:, :].unsqueeze(2).to_broadcast([F, 2, P])))
            take(dve, w_in_turn)
            link(v.tensor_copy(w_turned, y_ps[0:F, 0:P]))
            dve.sem_inc(w_ready, 1)
            take(dve, u_ready)
            link(v.tensor_copy(u_heads[:, :, :, :], y_ps[:, P:3 * P].rearrange("p (s h f) -> p s h f", s=2, h=H)))
            dve.wait_ge(edges_loaded, 32)
            segments(0)
            find_fixes(0)
            neutral_column(0.0)

            def l0_put(b, i):
                c = i * 2 + b

                def rows_made(c, rows):
                    link(v.tensor_tensor(rows, SEG[:, bass.ds(c * C + 1, C), :], X[:, bass.ts(c, C), :], ALU.add))
                    link(v.tensor_scalar(X[:, bass.ts(c, C), :], rows, 1.0, None, ALU.mult))

                put_inner("l0", b, i, F, rows_made)
                layernorm_relu(X[:, bass.ts(c, C), :], hb, C)
                heads_dot(0, hb, a_src[:, :, bass.ts(c, C)])

            dve.wait_ge(tables_ready, 1)
            gather_loop("l0", l0_sides, l0_gathered, l0_put)
            carries(ALU.add, SEG[:, T, :], whole[0][:, T - 1:T], F)
            link(v.tensor_copy(carry_l0[:, :], carry[:, :]))
            link(v.tensor_tensor(fix[:, 0:F], fix[:, 0:F], carry[:, :], ALU.add))
            dve.sem_inc(fix_ready, 1)
            layernorm_relu(fix[:, 0:F].unsqueeze(1), fix_h[:, :, :], 1)
            heads_dot(0, fix_h[:, :, :], fix_score[:, :, :], 1)
            link(v.tensor_copy(keyf[:, :], dst_row[1][:, :]))
            rows_from(dst_row[1][:, :], keyf[:, :])
            link(v.tensor_copy(hist_sb[:, :], src_row[1][:, :]))
            rows_from(src_row[1][:, :], hist_sb[:, :])
            segments(1)

            def per_head(a):
                return a.unsqueeze(1).to_broadcast([P, H, T])

            def over_heads(op):
                for h in range(H):
                    ins = op(h)
                    if h < H - 1:
                        ins.then_inc(dve_chain, 1)
                        chain[0] += 1
                link(ins)

            dve.wait_ge(layer_done, 1)
            first_rows([(0, dst_row[0])])
            link(v.memset(fix[:, :], 0.0))
            link(v.tensor_tensor(hist_sb[:, :], last[0][:, :], mark[:, :], ALU.subtract))
            link(v.tensor_tensor(back, a_src[:, :, :], per_head(hist_sb[:, :]), ALU.mult))
            over_heads(lambda h: v.scalar_tensor_tensor(out=back[:, h, :], in0=mark[:, :], scalar=fix_score[:, h, 0:1],
                                                        in1=back[:, h, :], op0=ALU.mult, op1=ALU.add))
            over_heads(lambda h: v.tensor_tensor_scan(own_score[:, h, ::-1], more[:, ::-1], back[:, h, ::-1], 0.0,
                                                      ALU.mult, ALU.add))
            carries(ALU.add, own_score[:, :, 0], tail[:, 0:1], H, back=(own_score[:, :, 0], tail[:, 0:1]))
            over_heads(lambda h: v.scalar_tensor_tensor(out=own_score[:, h, :], in0=tail[:, :],
                                                        scalar=carry_back[:, H + h:H + h + 1],
                                                        in1=own_score[:, h, :], op0=ALU.mult, op1=ALU.add))
            link(v.tensor_scalar(own_score, own_score, fcb_sb[:, 0:1], None, ALU.add))
            for factor, kept in ((same[0], base), (more, digit), (whole[0], hist_sb), (tail, junk)):
                link(v.tensor_scalar(kept[:, :], factor[:, :], -1.0, BIG, ALU.add, ALU.mult))
            link(v.memset(fore[:, :, 0], -BIG))

            def l1_gathered(b, i):
                c = i * 2 + b
                rows = put[b][:, 0:C * F].rearrange("p (c w) -> p c w", w=F)
                take(dve, h1_stored[b], 16)
                layernorm_relu(rows_of(b), rows, C)
                dve.sem_inc(h1_ready[b], 1)
                e = a_dst[:, :, bass.ts(c, C)]
                heads_dot(1, rows, e)
                link(v.tensor_tensor(e, e, own_score[:, :, bass.ts(c, C)], ALU.add))
                link(v.scalar_tensor_tensor(out=e, in0=e, scalar=0.2, in1=e, op0=ALU.mult, op1=ALU.max))
                over_heads(lambda h: v.tensor_tensor_scan(fore[:, h, bass.ds(c * C + 1, C)], base[:, bass.ts(c, C)],
                                                          a_dst[:, h, bass.ts(c, C)], fore[:, h, bass.ds(c * C, 1)],
                                                          ALU.add, ALU.max))

            for b in range(2):
                dve.sem_inc(h1_stored[b], 16)
            gather_loop("l1", [(0, dst_row[0])], l1_gathered)
            for b in range(2):
                take(dve, h1_stored[b], 16)
                dve.sem_inc(h1_used[b], 1)
                dve.sem_inc(h1_used[b], 1)
            over_heads(lambda h: v.tensor_tensor_scan(back[:, h, ::-1], digit[:, ::-1], a_dst[:, h, ::-1], -BIG,
                                                      ALU.add, ALU.max))
            link(v.tensor_tensor(a_src[:, :, :], fore[:, :, 1:T + 1], back, ALU.max))
            carries(ALU.max, fore[:, :, T], whole[0][:, T - 1:T], H, back=(back[:, :, 0], tail[:, 0:1]))
            over_heads(lambda h: v.scalar_tensor_tensor(out=a_src[:, h, :], in0=hist_sb[:, :], scalar=carry[:, h:h + 1],
                                                        in1=a_src[:, h, :], op0=ALU.add, op1=ALU.max))
            over_heads(lambda h: v.scalar_tensor_tensor(out=a_src[:, h, :], in0=junk[:, :],
                                                        scalar=carry_back[:, H + h:H + h + 1],
                                                        in1=a_src[:, h, :], op0=ALU.add, op1=ALU.max))
            link(v.tensor_tensor(a_dst[:, :, :], a_dst[:, :, :], a_src[:, :, :], ALU.subtract))
            dve.sem_inc(e_ready, 1)
            take(dve, p_ready)
            total = own_score
            over_heads(lambda h: v.tensor_tensor_scan(fore[:, h, 1:T + 1], same[0][:, :], a_dst[:, h, :], 0.0,
                                                      ALU.mult, ALU.add))
            over_heads(lambda h: v.tensor_tensor_scan(back[:, h, ::-1], more[:, ::-1], a_dst[:, h, ::-1], 0.0,
                                                      ALU.mult, ALU.add))
            carries(ALU.add, fore[:, :, T], whole[0][:, T - 1:T], H, back=(back[:, :, 0], tail[:, 0:1]))
            link(v.tensor_tensor(total, fore[:, :, 1:T + 1], back, ALU.add))
            link(v.tensor_tensor(total, total, a_dst[:, :, :], ALU.subtract))
            over_heads(lambda h: v.scalar_tensor_tensor(out=total[:, h, :], in0=whole[0][:, :], scalar=carry[:, h:h + 1],
                                                        in1=total[:, h, :], op0=ALU.mult, op1=ALU.add))
            over_heads(lambda h: v.scalar_tensor_tensor(out=total[:, h, :], in0=tail[:, :],
                                                        scalar=carry_back[:, H + h:H + h + 1],
                                                        in1=total[:, h, :], op0=ALU.mult, op1=ALU.add))

            def weights(columns):
                link(v.reciprocal(total[:, :, columns], total[:, :, columns]))
                link(v.scalar_tensor_tensor(out=a_dst[:, :, columns], in0=total[:, :, columns], scalar=1.0 / H,
                                            in1=a_dst[:, :, columns], op0=ALU.mult, op1=ALU.mult))

            weights(slice(0, 2 * C))
            neutral_column(0.0)

            def weigh(b, c):
                take(dve, h1_loaded[b], 16)
                for h in range(H):
                    ins = v.tensor_tensor(prod[:, :, h, :], rows_of(b),
                                          per_row(a_dst[:, h, bass.ts(c, C)], C), ALU.mult)
                link(ins)
                dve.sem_inc(h1_used[b], 1)
                dve.sem_inc(q_ready, 1)

            def l1_put(b, c, i):
                take(dve, y_ready)
                dve.sem_inc(q_last, 1)
                scan_chunk(c, y_banks[b][:, 0:C * F].rearrange("p (c w) -> p c w", w=F),
                           same[0][:, bass.ts(c, C)], ALU.mult, ALU.add)
                dve.sem_inc(y_used, 1)

                def rows_made(c, rows):
                    link(v.tensor_tensor(rows[:, :, 0:F], SEG[:, bass.ds(c * C + 1, C), :], X[:, bass.ts(c, C), :],
                                         ALU.add))
                    link(v.tensor_scalar(rows[:, :, F], deg[0][:, bass.ts(c, C)], 1.0, None, ALU.mult))

                put_inner("l1", b, i, RW, rows_made)

            dve.sem_inc(y_used, 2)
            weigh(0, 0)
            weights(slice(2 * C, T))
            chain_end()
            with dve.Fori(0, TURNS - 1) as i:
                for b in range(2):
                    take(dve, q_used)
                    weigh(1 - b, i * 2 + b + 1)
                    l1_put(b, i * 2 + b, i)
                chain_end()
            for b in range(2):
                take(dve, q_used)
                if b == 0:
                    weigh(1, CHUNKS - 1)
                l1_put(b, CHUNKS - 2 + b, TURNS - 1)
            take(dve, y_used)
            carries(ALU.add, SEG[:, T, :], whole[0][:, T - 1:T], F)
            link(v.tensor_tensor(fix[:, 0:F], fix[:, 0:F], carry[:, :], ALU.add))
            link(v.tensor_tensor(fix[:, 0:F], fix[:, 0:F], carry_l0[:, :], ALU.add))
            dve.sem_inc(fix_ready, 1)
            chain_end()
            neutral_column(-BIG)
            dve.wait_ge(layer_done, 2)
            l2_sides = [(0, src_row[1]), (1, dst_row[1])]
            first_rows(l2_sides)
            for b in range(2):
                dve.sem_inc(attr_used[b], 1)
                dve.sem_inc(node_stored[b], 32)
                dve.sem_inc(node_used[b], 1)
            link(v.memset(cat, 1.0))
            link(v.tensor_scalar(digit[:, :], same[1][:, :], -1.0, BIG, ALU.add, ALU.mult))
            find_fixes(1)
            link(v.memset(fix_x2[:, :], 0.0))
            link(v.memset(fix_max[:, :], 0.0))
            chain_end()

            def l2_edges(b, c):
                rows = rows_of(b, 0, 2, RW)
                link(v.tensor_tensor(both[:, :, :], rows[:, :, 0:F], per_feature(bias_sb[:, :], 2 * C), ALU.add))
                dve.sem_inc(x2_ready, 1)
                center(both[:, :, :], 2 * C)
                link(v.tensor_scalar(var[:, 2 * C:3 * C], rows[:, 0:C, F], 1.0, None, ALU.max))
                root(3 * C)
                link(v.tensor_scalar(more[:, bass.ts(c, C)], std[:, 2 * C:3 * C], 1.0, None, ALU.mult))
                scale(2 * C)
                take(dve, cat_used)
                for side in range(2):
                    link(v.tensor_scalar(cat[:, :, side * F:(side + 1) * F], cen[:, side * C:(side + 1) * C, :],
                                         0.0, None, ALU.max))
                take(dve, attr_loaded[b], 16)
                link(v.tensor_copy(cat[:, :, 2 * F:2 * F + A], attr_c[b][:, :, :]))
                dve.sem_inc(attr_used[b], 1)
                dve.sem_inc(cat_ready, 1)
                take(dve, x2_copied)

            def l2_maxima(c):
                take(dve, y_ready)
                scan_chunk(c, y_ps[:, 0:C * F].rearrange("p (c w) -> p c w", w=F), digit[:, bass.ts(c, C)],
                           ALU.add, ALU.max)
                dve.sem_inc(y_used, 1)

            def l2_nodes(b):
                take(dve, node_loaded[b], 16)
                take(dve, node_stored[b], 32)
                link(v.tensor_tensor(node_out[b][:, :, :], node_in[b][:, :, 0:F], per_feature(bias_sb[:, :], NC), ALU.add))
                dve.sem_inc(node_used[b], 1)
                center(node_out[b][:, :, :], NC)
                root(NC)
                scale(NC)
                link(v.scalar_tensor_tensor(out=node_out[b][:, :, :], in0=cen[:, 0:NC, :], scalar=0.0,
                                            in1=node_out[b][:, :, :], op0=ALU.max, op1=ALU.add))
                dve.sem_inc(node_ready[b], 1)

            l2_nodes(0)
            passed("l2", 0, 0, 2)
            l2_edges(0, 0)
            give_rows(0, 2, l2_sides)
            chain_end()
            with dve.Fori(0, TURNS - 2) as i:
                for b in (1, 0):
                    c = i * 2 + (1 if b else 2)
                    l2_nodes(b)
                    passed("l2", b, i if b else i + 1, 2)
                    l2_edges(b, c)
                    give_rows(b, c + 2, l2_sides)
                    l2_maxima(c - 1)
                chain_end()
            for c in range(CHUNKS - 3, CHUNKS - 1):
                l2_nodes(c % 2)
                passed("l2", c % 2, c // 2, 2)
                l2_edges(c % 2, c)
                if c + 2 < CHUNKS:
                    give_rows(c % 2, c + 2, l2_sides)
                l2_maxima(c - 1)
                chain_end()

            def l2_put(b, c, i):
                landed(dve, "dve", scatters["l2"][b], i * (16 * C) + PRIME)
                link(v.tensor_copy(row_c[b][:, 2, :], inner_row[:, bass.ts(c, C)]))
                rows = put[b][:, 0:C * F].rearrange("p (c w) -> p c w", w=F)
                x2 = X[:, bass.ts(c, C), :]
                layernorm_relu(x2, hb, C)
                best = SEG[:, bass.ds(c * C + 1, C), :]
                link(v.scalar_tensor_tensor(out=ha, in0=best, scalar=0.01, in1=best, op0=ALU.mult, op1=ALU.max))
                link(v.tensor_tensor(ha, ha, hb, ALU.max))
                link(v.tensor_tensor(rows, ha, x2, ALU.add))
                dve.sem_inc(put_ready[b], 1)
                keep_marked(fix_x2, x2, c)
                keep_marked(fix_max, ha, c)
                link(v.tensor_scalar(x2, rows, 1.0, None, ALU.mult))

            l2_nodes(1)
            for c in range(2):
                l2_put(c, c, 0)
            chain_end()
            passed("l2", 1, TURNS - 1, 2)
            l2_edges(1, CHUNKS - 1)
            l2_maxima(CHUNKS - 2)
            l2_put(0, 2, 1)
            l2_maxima(CHUNKS - 1)
            take(dve, y_used)
            l2_put(1, 3, 1)
            chain_end()
            with dve.Fori(2, TURNS) as i:
                for b in range(2):
                    l2_put(b, i * 2 + b, i)
                chain_end()
            carries(ALU.max, SEG[:, T, :], whole[1][:, T - 1:T], F)
            link(v.scalar_tensor_tensor(out=gain_l2[:, :], in0=carry[:, :], scalar=0.01, in1=carry[:, :],
                                        op0=ALU.mult, op1=ALU.max))
            link(v.tensor_tensor(gain_l2[:, :], gain_l2[:, :], fix_max[:, :], ALU.max))
            link(v.tensor_tensor(fix[:, 0:F], fix_x2[:, :], gain_l2[:, :], ALU.add))
            dve.sem_inc(fix_ready, 1)
            link(v.tensor_tensor(gain_l2[:, :], gain_l2[:, :], fix_max[:, :], ALU.subtract))
            chain_end()

            neutral_column(0.0)
            link(v.tensor_scalar(deg[1][:, :], deg[1][:, :], 1.0, None, ALU.max))
            dve.sem_inc(deg_ready, 1)
            take(dve, deg_rooted)
            link(v.reciprocal(deg[1][:, :], deg[1][:, :]))
            link(v.tensor_tensor(junk[:, :], deg[1][:, :], mark[:, :], ALU.mult))
            link(v.tensor_reduce(fix_std[:, :], junk[:, :], AX.X, ALU.add))
            dve.wait_ge(layer_done, 3)
            first_rows([(0, src_row[1])])
            link(v.tensor_copy(fix[:, 0:F], gain_l2[:, :]))

            def l3_gathered(b, i):
                c = i * 2 + b
                layernorm_relu(rows_of(b), ha, C)
                link(v.tensor_tensor(ha, ha, per_row(more[:, bass.ts(c, C)], C), ALU.mult))
                scan_chunk(c, ha, same[1][:, bass.ts(c, C)], ALU.mult, ALU.add)

            def l3_put(b, i):
                def rows_made(c, rows):
                    link(v.tensor_tensor(ha, SEG[:, bass.ds(c * C + 1, C), :], per_row(deg[1][:, bass.ts(c, C)], C),
                                         ALU.mult))
                    link(v.tensor_tensor(rows, ha, X[:, bass.ts(c, C), :], ALU.add))

                put_inner("l3", b, i, F, rows_made)

            gather_loop("l3", [(0, src_row[1])], l3_gathered, l3_put)
            carries(ALU.add, SEG[:, T, :], whole[1][:, T - 1:T], F)
            link(v.scalar_tensor_tensor(out=fix[:, 0:F], in0=carry[:, :], scalar=fix_std[:, 0:1], in1=fix[:, 0:F],
                                        op0=ALU.mult, op1=ALU.add))
            dve.sem_inc(fix_ready, 1)
            dve.wait_ge(layer_done, 4)


_INS = ["x", "src", "dst", "edge_attr_16", "edge_weight", "L1_gnn_w", "L1_gnn_fc_w", "L1_gnn_fc_b", "L1_gnn_bias",
        "L2_gnn_W1", "L2_gnn_b1", "L2_gnn_W2", "L2_gnn_b2"]


def kernel(**inputs):
    import concourse.bacc as _bacc
    from concourse.bass_utils import run_bass_kernel_spmd as _run

    def padded(a, rows, fill):
        a = np.asarray(a)
        return np.concatenate([a, np.full((rows - a.shape[0],) + a.shape[1:], fill, a.dtype)])

    given = {n: np.ascontiguousarray(inputs[n]) for n in _INS}
    given["x"] = padded(given["x"], NP, 0)
    given["src"] = padded(given["src"], EP, PADKEY)
    given["dst"] = padded(given["dst"], EP, PADKEY)
    given["edge_attr_16"] = padded(given["edge_attr_16"], EP, 0)
    given["edge_weight"] = padded(given["edge_weight"], EP, 0)
    nc = _bacc.Bacc("TRN2", target_bir_lowering=False, num_devices=1)
    arrays, args = {}, []
    for n in _INS:
        a = given[n]
        arrays[f"in_{n}_dram"] = a
        args.append(nc.dram_tensor(f"in_{n}_dram", a.shape, mybir.dt.from_np(a.dtype), kind="ExternalInput").ap())
    out = nc.dram_tensor("out_0_dram", (NP, F), F32, kind="ExternalOutput").ap()
    build_gnn(nc, *args, out)
    r = _run(nc, [arrays], core_ids=[0])
    return r.results[0]["out_0_dram"][0:N]
```
